# Optimizing a Trainium2 kernel written in Bass

```python
import numpy as np
import jax
import jax.numpy as jnp

def _softmax(x, axis=-1):
    return jax.nn.softmax(x, axis=axis)

def _gelu(x):
    return jax.nn.gelu(x, approximate=True)

def _silu(x):
    return jax.nn.silu(x)

def _sigmoid(x):
    return jax.nn.sigmoid(x)

def _layernorm(x, axis=-1, eps=1e-05):
    m = jnp.mean(x, axis=axis, keepdims=True)
    v = jnp.var(x, axis=axis, keepdims=True)
    return (x - m) / jnp.sqrt(v + eps)

def _scatter_add(tgt, idx, src, axis=0):
    return tgt.at[idx].add(src)

def _segment_sum(src, seg, n):
    return jax.ops.segment_sum(src, seg, n)
kernel_name = 'mk_gnn_resnorm_d4_gnn_r8_c9ad4e'

def setup_inputs(seed: int=0):
    np.random.seed(seed)
    _w = jnp.asarray

    def _rec_inputs():
        import jax
        import jax.numpy as jnp
        _gk = jax.random.key(seed)
        x = -0.0003713 + 1 * jax.random.normal(jax.random.fold_in(_gk, 1), (12500, 128), jnp.float32)
        _s = jax.random.randint(jax.random.fold_in(_gk, 2), (100000,), 0, 12500, jnp.int32)
        _d = jax.random.randint(jax.random.fold_in(_gk, 3), (100000,), 0, 12500, jnp.int32)
        _loop = jnp.arange(12500, dtype=jnp.int32)
        src = jnp.concatenate([_s, _d, _loop])
        dst = jnp.concatenate([_d, _s, _loop])
        _o = jnp.argsort(dst, stable=True)
        src = src[_o]
        dst = dst[_o]
        edge_attr_16 = 0.000196303 + 1.00016 * jax.random.normal(jax.random.fold_in(_gk, 12), (212500, 16), jnp.float32)
        edge_attr_3 = jax.random.uniform(jax.random.fold_in(_gk, 13), (212500, 3), jnp.float32, 0.0, 1)
        edge_attr_6 = jax.random.uniform(jax.random.fold_in(_gk, 14), (212500, 6), jnp.float32, 0.0, 1)
        return (x, src, dst, edge_attr_16, edge_attr_3, edge_attr_6)
    x, src, dst, edge_attr_16, edge_attr_3, edge_attr_6 = _rec_inputs()

    def _L0_gnn_setup():
        import jax, jax.numpy as jnp
        import numpy as np
        N_NODES = 12500
        N_EDGES = 200000
        EMB = 128
        EDGE_DIMS = [6, 3]
        BN_EPS = 1e-05
        key = jax.random.key(seed)
        ks = jax.random.split(key, 16)
        inp = {'node_feats': jax.random.normal(ks[0], (N_NODES, EMB), jnp.float32), 'edge_feat_0': jax.random.uniform(ks[1], (N_EDGES, EDGE_DIMS[0]), jnp.float32), 'edge_feat_1': jax.random.uniform(ks[2], (N_EDGES, EDGE_DIMS[1]), jnp.float32), 'src': jax.random.randint(ks[3], (N_EDGES,), 0, N_NODES, jnp.int32), 'dst': jax.random.randint(ks[4], (N_EDGES,), 0, N_NODES, jnp.int32)}
        s0 = 1.0 / np.sqrt(EDGE_DIMS[0])
        s1 = 1.0 / np.sqrt(EDGE_DIMS[1])
        inp['We0'] = jax.random.uniform(ks[5], (EDGE_DIMS[0], EMB), jnp.float32, -s0, s0)
        inp['be0'] = jax.random.uniform(ks[6], (EMB,), jnp.float32, -s0, s0)
        inp['We1'] = jax.random.uniform(ks[7], (EDGE_DIMS[1], EMB), jnp.float32, -s1, s1)
        inp['be1'] = jax.random.uniform(ks[8], (EMB,), jnp.float32, -s1, s1)
        sm = 1.0 / np.sqrt(EMB)
        sh = 1.0 / np.sqrt(2 * EMB)
        inp['W1'] = jax.random.uniform(ks[9], (EMB, 2 * EMB), jnp.float32, -sm, sm)
        inp['b1'] = jax.random.uniform(ks[10], (2 * EMB,), jnp.float32, -sm, sm)
        inp['W2'] = jax.random.uniform(ks[11], (2 * EMB, EMB), jnp.float32, -sh, sh)
        inp['b2'] = jax.random.uniform(ks[12], (EMB,), jnp.float32, -sh, sh)
        inp['gamma'] = jnp.ones((EMB,), jnp.float32)
        inp['beta'] = jnp.zeros((EMB,), jnp.float32)
        return inp
    _L0_gnn_all = _L0_gnn_setup()
    _L0_gnn_in = {k: v for k, v in _L0_gnn_all.items() if k in ('We0', 'be0', 'We1', 'be1', 'W1', 'b1', 'W2', 'b2', 'gamma', 'beta')}
    del _L0_gnn_all

    def _L1_gnn_setup():
        import jax, jax.numpy as jnp
        import numpy as np
        N_NODES = 12500
        N_EDGES = 200000
        IN_CH = 128
        HEADS = 8
        OUT_CH = 16
        OUT_DIM = HEADS * OUT_CH
        NEG_SLOPE = 0.2
        LN_EPS = 1e-05
        key = jax.random.key(seed)
        ks = jax.random.split(key, 8)
        x = jax.random.normal(ks[0], (N_NODES, IN_CH), dtype=jnp.float32)
        edge_index = jax.random.randint(ks[1], (2, N_EDGES), 0, N_NODES, dtype=jnp.int64)
        W = jax.random.normal(ks[2], (IN_CH, OUT_DIM), dtype=jnp.float32) / np.sqrt(IN_CH)
        att_src = jax.random.normal(ks[3], (HEADS, OUT_CH), dtype=jnp.float32) / np.sqrt(OUT_CH)
        att_dst = jax.random.normal(ks[4], (HEADS, OUT_CH), dtype=jnp.float32) / np.sqrt(OUT_CH)
        bias = jnp.zeros((OUT_DIM,), dtype=jnp.float32)
        ln_gamma = jnp.ones((OUT_DIM,), dtype=jnp.float32)
        ln_beta = jnp.zeros((OUT_DIM,), dtype=jnp.float32)
        return {'x': x, 'edge_index': edge_index, 'W': W, 'att_src': att_src, 'att_dst': att_dst, 'bias': bias, 'ln_gamma': ln_gamma, 'ln_beta': ln_beta}
    _L1_gnn_all = _L1_gnn_setup()
    _L1_gnn_in = {k: v for k, v in _L1_gnn_all.items() if k in ('W', 'att_src', 'att_dst', 'bias', 'ln_gamma', 'ln_beta')}
    del _L1_gnn_all

    def _L2_gnn_setup():
        import jax, jax.numpy as jnp
        import numpy as np
        N_NODES = 12500
        N_EDGES = 200000
        IN_F = 128
        OUT_F = 128
        EDGE_F = 16
        key = jax.random.key(seed)
        ks = jax.random.split(key, 8)
        H = jax.random.normal(ks[0], (N_NODES, IN_F), dtype=jnp.float32)
        edge_index = jax.random.randint(ks[1], (2, N_EDGES), 0, (N_ODES_ := N_NODES), dtype=jnp.int64) if False else jax.random.randint(ks[1], (2, N_EDGES), 0, N_NODES, dtype=jnp.int32).astype(jnp.int64)
        edge_attr = jax.random.normal(ks[2], (N_EDGES, EDGE_F), dtype=jnp.float32)
        We = jax.random.normal(ks[3], (EDGE_F, IN_F), dtype=jnp.float32) * (1.0 / np.sqrt(EDGE_F))
        be = jnp.zeros((IN_F,), dtype=jnp.float32)
        W1 = jax.random.normal(ks[4], (IN_F, OUT_F), dtype=jnp.float32) * (1.0 / np.sqrt(IN_F))
        b1 = jnp.zeros((OUT_F,), dtype=jnp.float32)
        W2 = jax.random.normal(ks[5], (OUT_F, OUT_F), dtype=jnp.float32) * (1.0 / np.sqrt(OUT_F))
        b2 = jnp.zeros((OUT_F,), dtype=jnp.float32)
        return {'H': H, 'edge_index': edge_index, 'edge_attr': edge_attr, 'We': We, 'be': be, 'W1': W1, 'b1': b1, 'W2': W2, 'b2': b2}
    _L2_gnn_all = _L2_gnn_setup()
    _L2_gnn_in = {k: v for k, v in _L2_gnn_all.items() if k in ('We', 'be', 'W1', 'b1', 'W2', 'b2')}
    del _L2_gnn_all

    def _L3_gnn_setup():
        import jax, jax.numpy as jnp
        import numpy as np
        N_NODES = 6250
        N_EDGES = 100000
        IN_CH = 128
        OUT_CH = 128
        key = jax.random.key(seed)
        k1, k2, k3, k4 = jax.random.split(key, 4)
        x = jax.random.normal(k1, (N_NODES, IN_CH), dtype=jnp.float32)
        edge_index = jax.random.randint(k2, (2, N_EDGES), 0, N_NODES, dtype=jnp.int64)
        W = jax.random.normal(k3, (OUT_CH, IN_CH), dtype=jnp.float32) / np.sqrt(IN_CH)
        b = jax.random.normal(k4, (OUT_CH,), dtype=jnp.float32) * 0.01
        agg_weight = jnp.ones((1,), dtype=jnp.float32)
        return {'x': x, 'edge_index': edge_index, 'W': W, 'b': b, 'agg_weight': agg_weight}
    _L3_gnn_all = _L3_gnn_setup()
    _L3_gnn_in = {k: v for k, v in _L3_gnn_all.items() if k in ('W', 'b', 'agg_weight')}
    del _L3_gnn_all
    return {'x': x, 'src': src, 'dst': dst, 'edge_attr_16': edge_attr_16, 'edge_attr_3': edge_attr_3, 'edge_attr_6': edge_attr_6, 'L0_gnn_We0': _L0_gnn_in['We0'], 'L0_gnn_be0': _L0_gnn_in['be0'], 'L0_gnn_We1': _L0_gnn_in['We1'], 'L0_gnn_be1': _L0_gnn_in['be1'], 'L0_gnn_W1': _L0_gnn_in['W1'], 'L0_gnn_b1': _L0_gnn_in['b1'], 'L0_gnn_W2': _L0_gnn_in['W2'], 'L0_gnn_b2': _L0_gnn_in['b2'], 'L0_gnn_gamma': _L0_gnn_in['gamma'], 'L0_gnn_beta': _L0_gnn_in['beta'], 'L1_gnn_W': _L1_gnn_in['W'], 'L1_gnn_att_src': _L1_gnn_in['att_src'], 'L1_gnn_att_dst': _L1_gnn_in['att_dst'], 'L1_gnn_bias': _L1_gnn_in['bias'], 'L1_gnn_ln_gamma': _L1_gnn_in['ln_gamma'], 'L1_gnn_ln_beta': _L1_gnn_in['ln_beta'], 'L2_gnn_We': _L2_gnn_in['We'], 'L2_gnn_be': _L2_gnn_in['be'], 'L2_gnn_W1': _L2_gnn_in['W1'], 'L2_gnn_b1': _L2_gnn_in['b1'], 'L2_gnn_W2': _L2_gnn_in['W2'], 'L2_gnn_b2': _L2_gnn_in['b2'], 'L3_gnn_W': _L3_gnn_in['W'], 'L3_gnn_b': _L3_gnn_in['b'], 'L3_gnn_agg_weight': _L3_gnn_in['agg_weight']}

def reference(x, src, dst, edge_attr_16, edge_attr_3, edge_attr_6, L0_gnn_We0, L0_gnn_be0, L0_gnn_We1, L0_gnn_be1, L0_gnn_W1, L0_gnn_b1, L0_gnn_W2, L0_gnn_b2, L0_gnn_gamma, L0_gnn_beta, L1_gnn_W, L1_gnn_att_src, L1_gnn_att_dst, L1_gnn_bias, L1_gnn_ln_gamma, L1_gnn_ln_beta, L2_gnn_We, L2_gnn_be, L2_gnn_W1, L2_gnn_b1, L2_gnn_W2, L2_gnn_b2, L3_gnn_W, L3_gnn_b, L3_gnn_agg_weight):
    import jax
    import jax.numpy as jnp

    def _L0_gnn_ref(node_feats, edge_feat_0, edge_feat_1, src, dst, We0, be0, We1, be1, W1, b1, W2, b2, gamma, beta):
        import jax, jax.numpy as jnp
        import numpy as np
        N_NODES = 12500
        N_EDGES = 200000
        EMB = 128
        EDGE_DIMS = [6, 3]
        BN_EPS = 1e-05
        n_nodes = node_feats.shape[0]
        edge_embs = edge_feat_0 @ We0 + be0 + (edge_feat_1 @ We1 + be1)
        msgs = node_feats[src] + edge_embs
        agg = jax.ops.segment_sum(msgs, dst, num_segments=n_nodes)
        h = jax.nn.relu(agg @ W1 + b1) @ W2 + b2
        mean = jnp.mean(h, axis=0)
        var = jnp.var(h, axis=0)
        h = (h - mean) * jax.lax.rsqrt(var + BN_EPS) * gamma + beta
        return h

    def _L1_gnn_ref(x, edge_index, W, att_src, att_dst, bias, ln_gamma, ln_beta):
        import jax, jax.numpy as jnp
        import numpy as np
        N_NODES = 12500
        N_EDGES = 200000
        IN_CH = 128
        HEADS = 8
        OUT_CH = 16
        OUT_DIM = HEADS * OUT_CH
        NEG_SLOPE = 0.2
        LN_EPS = 1e-05
        N = x.shape[0]
        loops = jnp.arange(N, dtype=edge_index.dtype)
        src = jnp.concatenate([edge_index[0], loops])
        dst = jnp.concatenate([edge_index[1], loops])
        h = (x @ W).reshape(N, HEADS, OUT_CH)
        a_s = jnp.sum(h * att_src[None], axis=-1)
        a_d = jnp.sum(h * att_dst[None], axis=-1)
        e = jax.nn.leaky_relu(a_s[src] + a_d[dst], NEG_SLOPE)
        e_max = jax.ops.segment_max(e, dst, num_segments=N)
        ex = jnp.exp(e - e_max[dst])
        denom = jax.ops.segment_sum(ex, dst, num_segments=N)
        alpha = ex / denom[dst]
        msg = alpha[:, :, None] * h[src]
        agg = jax.ops.segment_sum(msg, dst, num_segments=N)
        out = agg.reshape(N, OUT_DIM) + bias
        mu = jnp.mean(out, axis=-1, keepdims=True)
        var = jnp.mean(jnp.square(out - mu), axis=-1, keepdims=True)
        out = (out - mu) * jax.lax.rsqrt(var + LN_EPS) * ln_gamma + ln_beta
        return jax.nn.elu(out)

    def _L2_gnn_ref(H, edge_index, edge_attr, We, be, W1, b1, W2, b2):
        import jax, jax.numpy as jnp
        import numpy as np
        N_NODES = 12500
        N_EDGES = 200000
        IN_F = 128
        OUT_F = 128
        EDGE_F = 16
        edge_messages = edge_attr @ We + be
        messages = H[edge_index[0]] + edge_messages
        aggregated = jax.ops.segment_sum(messages, edge_index[1], num_segments=H.shape[0])
        h = jax.nn.relu(aggregated @ W1 + b1)
        out = h @ W2 + b2
        return out

    def _L3_gnn_ref(x, edge_index, W, b, agg_weight):
        import jax, jax.numpy as jnp
        import numpy as np
        N_NODES = 6250
        N_EDGES = 100000
        IN_CH = 128
        OUT_CH = 128
        row, col = (edge_index[0], edge_index[1])
        messages = jnp.einsum('ei,oi->eo', x[col], W) + b
        out = jax.ops.segment_sum(messages * agg_weight, row, num_segments=x.shape[0])
        return out
    edge_index = jnp.stack([src, dst])
    x = _layernorm(x + _L0_gnn_ref(x, edge_attr_6, edge_attr_3, src, dst, L0_gnn_We0, L0_gnn_be0, L0_gnn_We1, L0_gnn_be1, L0_gnn_W1, L0_gnn_b1, L0_gnn_W2, L0_gnn_b2, L0_gnn_gamma, L0_gnn_beta), axis=-1)
    x = _layernorm(x + _L1_gnn_ref(x, edge_index, L1_gnn_W, L1_gnn_att_src, L1_gnn_att_dst, L1_gnn_bias, L1_gnn_ln_gamma, L1_gnn_ln_beta), axis=-1)
    x = _layernorm(x + _L2_gnn_ref(x, edge_index, edge_attr_16, L2_gnn_We, L2_gnn_be, L2_gnn_W1, L2_gnn_b1, L2_gnn_W2, L2_gnn_b2), axis=-1)
    x = _layernorm(x + _L3_gnn_ref(x, edge_index, L3_gnn_W, L3_gnn_b, L3_gnn_agg_weight), axis=-1)
    return x

_drawn_inputs = setup_inputs


def setup_inputs(seed=0):
    import zlib

    import numpy as np

    out = dict(_drawn_inputs(seed))
    spreads = {'L0_gnn_gamma': (1.0, 0.2),
     'L0_gnn_beta': (0.0, 0.1),
     'L1_gnn_bias': (0.0, 0.1),
     'L1_gnn_ln_gamma': (1.0, 0.2),
     'L1_gnn_ln_beta': (0.0, 0.1),
     'L2_gnn_be': (0.0, 0.1),
     'L2_gnn_b1': (0.0, 0.746),
     'L2_gnn_b2': (0.0, 0.48)}
    factors = {'L0_gnn_b1': 28.179, 'L0_gnn_b2': 64.0, 'L3_gnn_b': 4.401}
    for name, (base, spread) in spreads.items():
        noise = np.random.default_rng([zlib.crc32(name.encode()), seed]).standard_normal(out[name].shape)
        drawn = base * np.exp(spread * noise) if base else spread * noise
        out[name] = jnp.asarray(drawn.astype(out[name].dtype))
    for name, factor in factors.items():
        out[name] = (out[name] * factor).astype(out[name].dtype)
    return out
```

```python
from contextlib import ExitStack

import concourse.bass as bass
from concourse import mybir

P = 128
F = 128
HEADS = 8
HEAD_CH = F // HEADS
HALF = 16
BODY = 2 * HALF
GROUP = 4
GROUP_W = GROUP * P
REC = 28
COL_LOCAL, COL_INDEX, COL_ATTR = 0, 1, 2
EXTRA = REC - COL_ATTR
REC_S = 4
SUM_W = EXTRA + F + HEADS
FEAT = EXTRA
DEN = EXTRA + F
ROW = F + HEADS
ONEHOTS = 8
SUM_BANKS = 4
BIG = float(2.0 ** 100)
NORM_EPS = 1e-5
SLOPE = 0.2


def _sizes(n_nodes, n_edges):
    s = {}
    s["tiles"] = -(-n_nodes // P)
    s["groups"] = -(-s["tiles"] // GROUP)
    s["padded_tiles"] = s["groups"] * GROUP
    most = (n_edges + s["tiles"] * (P - 1)) // P
    s["slots"] = -(-most // BODY) * BODY
    s["cols"] = n_edges // P
    s["tail"] = n_edges - s["cols"] * P
    s["sort_half"] = max(k for k in range(1, 13) if s["cols"] % (2 * k) == 0)
    return s


def gnn_kernel(nc, t, out):
    f32, bf16, i32 = mybir.dt.float32, mybir.dt.bfloat16, mybir.dt.int32
    ALU, ACT, AX = mybir.AluOpType, mybir.ActivationFunctionType, mybir.AxisListType
    N, E = t["x"].shape[0], t["src"].shape[0]
    z = _sizes(N, E)
    TILES, GROUPS, PT, NT = z["tiles"], z["groups"], z["padded_tiles"], z["slots"]
    COLS, TAIL, CS = z["cols"], z["tail"], z["sort_half"]
    SORT_ITERS, ITERS = COLS // (2 * CS), NT // BODY
    MAIN = COLS * P
    ds = bass.ds

    ctx = ExitStack()
    with ctx:
        def sb(name, shape, dt=f32, where=ctx):
            return where.enter_context(nc.sbuf_tensor(name, shape, dt))

        def sem(name):
            return ctx.enter_context(nc.semaphore(name))

        def dram(name, shape, dt=f32):
            return nc.dram_tensor(name, shape, dt, kind="Internal").ap()

        rec_d = dram("rec_by_dst", (P * NT, REC))
        rec_s = dram("rec_by_src", (P * NT, REC_S))
        xs = [dram(f"x_layer{k}", (PT * P, F)) for k in range(4)]
        hrow = dram("attention_rows", (PT * P, ROW))
        asrc = dram("attention_src", (PT * P, HEADS))

        psum = ctx.enter_context(nc.psum_tensor("psum", [P, 8, 512], f32))

        iota_row = sb("iota_row", [P, P])
        iota_part = sb("iota_part", [P, 1])
        ident = sb("ident", [P, P])
        ident_b = sb("ident_b", [P, P], bf16)
        eps = sb("eps", [P, 1])
        w1_0 = sb("w1_0", [P, 2 * F])
        w2_0 = sb("w2_0", [P, 2, F])
        we_0 = sb("we_0", [EXTRA, F])
        be1_0 = sb("be1_0", [EXTRA, F])
        w_gat = sb("w_gat", [P, F + 2 * HEADS])
        att = sb("att", [P, 2, F])
        att_w = sb("att_w", [P, 2, F])
        w1_2 = sb("w1_2", [P, F])
        w2_2 = sb("w2_2", [P, 1, F])
        we_2 = sb("we_2", [EXTRA, F])
        w_3 = sb("w_3", [P, F])
        w_3t = sb("w_3t", [P, F])
        b_3 = sb("b_3", [EXTRA, F])
        b1_0 = sb("b1_0", [P, 2])
        cols = sb("cols", [P, 8])
        b2_0, gamma_0, beta_0, b1_2, b2_2, agg_w = (cols[:, k:k + 1] for k in range(6))
        rows = sb("rows", [P, 3, F])
        bias_1, gamma_1, beta_1 = (rows[:, k, :] for k in range(3))
        affine = sb("affine", [P, 4])
        bn_scale, bn_shift, one_col, zero_col = (affine[:, k:k + 1] for k in range(4))
        tile_of_d = sb("tile_of_d", [1, NT], i32)
        tile_of_s = sb("tile_of_s", [1, NT], i32)
        sums = sb("sums", [P, PT, SUM_W])
        dst_max = sb("dst_max", [P, PT, 2 * HEADS])
        rec = sb("rec", [P, 2, HALF, REC])
        recs = sb("recs", [P, 2, HALF, REC_S])
        gathered = sb("gathered", [P, BODY, ROW])

        loaded = sem("loaded")
        made = sem("made")
        dve_steps = sem("dve_steps")
        hist_done = sem("hist_done")
        prefix_done = sem("prefix_done")
        owner_done = sem("owner_done")
        owner_copied = sem("owner_copied")
        filled = sem("filled")
        small_psum = sem("small_psum")

        sort = ctx.enter_context(ExitStack())
        with sort:
            W = COLS + 1
            key = [sb(f"key{k}", [P, W], i32, sort) for k in range(2)]
            tmp = sb("key_tmp", [P, W], i32, sort)
            bin_ = [sb(f"bin{k}", [P, W], f32, sort) for k in range(2)]
            local = [sb(f"local{k}", [P, W], f32, sort) for k in range(2)]
            junk = sb("junk", [P, W], bf16, sort)
            hist = sb("hist", [P, 2, TILES], f32, sort)
            tiles_f = sb("tiles_f", [P, 2, TILES], f32, sort)
            tiles_i = sb("tiles_i", [P, 2, TILES], i32, sort)
            ends = sb("ends", [P, 2, TILES], f32, sort)
            zeros = sb("zeros", [P, TILES], f32, sort)
            place = sb("place", [P, 2, TILES], f32, sort)
            end_col = sb("end_col", [P, 2], f32, sort)
            before = sb("before", [P, P], f32, sort)
            ones = sb("ones", [P, P], f32, sort)
            iota_t = sb("iota_t", [P, NT], f32, sort)
            ended = sb("ended", [P, NT], f32, sort)
            blank = sb("blank", [P, HALF, REC], f32, sort)
            FILL = blank[:, :, :]
            picked = sb("picked", [P, 2, 2, TILES], f32, sort)
            pos = sb("pos", [P, 2, 2, CS], f32, sort)
            pos_i = sb("pos_i", [P, 2, 2, CS], i32, sort)
            pos_t = sb("pos_t", [P, 2, 2, CS], i32, sort)
            addr = sb("addr", [P, 2, 2, CS], i32, sort)
            ea = [sb(f"ea{w}", [P, 2, CS, w], f32, sort) for w in (6, 3, 16)]
            out_d = sb("out_d", [P, 2, CS, REC], f32, sort)
            spare_row = sb("spare_row", [1, F], f32, sort)
            out_s = sb("out_s", [P, 2, CS, REC_S], f32, sort)

            keys_in = [t["dst"], t["src"]]
            attrs_in = [t["edge_attr_6"], t["edge_attr_3"], t["edge_attr_16"]]

            with nc.Block() as block:

                @block.sync
                def _(sp):
                    sp.wait_ge(made, 2)
                    for k in range(2):
                        sp.dma_start(key[k][:, 0:COLS], keys_in[k][0:MAIN].rearrange("(p c) -> p c", p=P)).then_inc(loaded, 16)
                        if TAIL:
                            sp.dma_start(key[k][0:TAIL, COLS:W], keys_in[k][MAIN:E].rearrange("(p c) -> p c", c=1)).then_inc(loaded, 16)
                    sp.wait_ge(loaded, 16 * (4 if TAIL else 2))
                    col = lambda a, c=1: a.rearrange("(p c) -> p c", c=c)
                    row = lambda a: a.rearrange("(a n) -> a n", a=1)
                    sp.wait_ge(made, 3)
                    small = [
                        (w1_0[:], t["L0_gnn_W1"]), (w2_0[:], t["L0_gnn_W2"].rearrange("(j p) n -> p j n", j=2)),
                        (we_0[0:6, :], t["L0_gnn_We0"]), (we_0[6:9, :], t["L0_gnn_We1"]),
                        (we_0[25:26, :], row(t["L0_gnn_be0"])), (be1_0[25:26, :], row(t["L0_gnn_be1"])),
                        (w_gat[:, 0:F], t["L1_gnn_W"]),
                        (att[:, 0, :], row(t["L1_gnn_att_src"].rearrange("h c -> (h c)")).to_broadcast([P, F])),
                        (att[:, 1, :], row(t["L1_gnn_att_dst"].rearrange("h c -> (h c)")).to_broadcast([P, F])),
                        (w1_2[:], t["L2_gnn_W1"]), (w2_2[:, 0, :], t["L2_gnn_W2"]),
                        (we_2[9:25, :], t["L2_gnn_We"]), (we_2[25:26, :], row(t["L2_gnn_be"])),
                        (w_3[:], t["L3_gnn_W"]), (b_3[25:26, :], row(t["L3_gnn_b"])),
                        (b2_0, col(t["L0_gnn_b2"])), (gamma_0, col(t["L0_gnn_gamma"])), (beta_0, col(t["L0_gnn_beta"])),
                        (b1_2, col(t["L2_gnn_b1"])), (b2_2, col(t["L2_gnn_b2"])),
                        (agg_w, row(t["L3_gnn_agg_weight"]).to_broadcast([P, 1])),
                        (bias_1, row(t["L1_gnn_bias"]).to_broadcast([P, F])),
                        (gamma_1, row(t["L1_gnn_ln_gamma"]).to_broadcast([P, F])),
                        (beta_1, row(t["L1_gnn_ln_beta"]).to_broadcast([P, F])),
                        (b1_0[:, 0:1], col(t["L0_gnn_b1"][0:P])), (b1_0[:, 1:2], col(t["L0_gnn_b1"][P:2 * P])),
                    ]
                    for to, of in small:
                        sp.dma_start(to, of).then_inc(loaded, 16)
                    sp.wait_ge(loaded, 16 * ((4 if TAIL else 2) + len(small)))

                @block.scalar
                def _(act):
                    act.wait_ge(made, 4)
                    rd = rec_d.rearrange("(p t) w -> p t w", t=NT)
                    with act.Fori(0, NT // HALF) as i:
                        act.dma_start(rd[:, ds(i * HALF, HALF), :], FILL).then_inc(filled, 16)
                    rs = rec_s.rearrange("(p t) w -> p t w", t=NT)
                    few = blank[:, :, 0:REC_S]
                    with act.Fori(0, NT // HALF) as i:
                        act.dma_start(rs[:, ds(i * HALF, HALF), :], few).then_inc(filled, 16)
                    act.dma_start(xs[0][0:N, :], t["x"]).then_inc(filled, 16)
                    total = 2 * (NT // HALF) + 1
                    spare = PT * P - N
                    for r in range(0, spare, P):
                        k = min(P, spare - r)
                        act.dma_start(xs[0][N + r:N + r + k, :], ones[0:k, :]).then_inc(filled, 16)
                        total += 1
                    act.wait_ge(filled, 16 * total)

                @block.gpsimd
                def _(pool):
                    for k in range(2):
                        pool.memset(key[k][:, COLS:W], -P).then_inc(made, 1)
                    for m in (we_0, be1_0, we_2, b_3):
                        pool.memset(m[:], 0.0)
                    pool.memset(dst_max[:], 0.0)
                    pool.memset(zeros[:], 0.0)
                    pool.memset(one_col, 1.0)
                    pool.memset(zero_col, 0.0)
                    pool.memset(eps[:], NORM_EPS).then_inc(made, 1)
                    pool.memset(ones[:], 1.0)
                    pool.memset(blank[:], 0.0).then_inc(small_psum, 1)
                    pool.wait_ge(small_psum, 1)
                    pool.memset(blank[:, :, 0:1], -1.0).then_inc(made, 1)
                    pool.iota(iota_row[:], pattern=[[1, P]], base=0, channel_multiplier=0, allow_small_or_imprecise_dtypes=True)
                    pool.iota(iota_part[:], pattern=[[0, 1]], base=0, channel_multiplier=1, allow_small_or_imprecise_dtypes=True)
                    pool.iota(iota_t[:], pattern=[[1, NT]], base=0, channel_multiplier=0, allow_small_or_imprecise_dtypes=True).then_inc(made, 1)

                @block.vector
                def _(v):
                    n = [0]

                    def link(ins):
                        n[0] += 1
                        ins.then_inc(dve_steps, 1)
                        v.wait_ge(dve_steps, n[0])

                    v.memset(sums[:, :, :], 0.0)
                    v.wait_ge(made, 5)
                    link(v.tensor_scalar(ident[:], iota_row[:], iota_part[:], None, ALU.is_equal))
                    v.tensor_copy(ident_b[:], ident[:])
                    v.tensor_scalar(before[:], iota_row[:], iota_part[:], None, ALU.is_gt)
                    v.wait_ge(loaded, 16 * (4 if TAIL else 2))
                    for k in range(2):
                        link(v.tensor_single_scalar(tmp[:], key[k][:], 7, ALU.arith_shift_right))
                        link(v.tensor_copy(bin_[k][:], tmp[:]))
                        link(v.tensor_single_scalar(tmp[:], key[k][:], P - 1, ALU.bitwise_and))
                        link(v.tensor_copy(local[k][:], tmp[:]))
                    for k in range(2):
                        for b in range(TILES):
                            link(v.tensor_scalar(junk[:], bin_[k][:], float(b), 0.0, ALU.is_equal, ALU.add,
                                                 accum_out=hist[:, k, b:b + 1]))
                    v.sem_inc(hist_done, 1)
                    v.wait_ge(prefix_done, 1)
                    total_p = psum[:, 1, 0:2 * TILES].rearrange("p (k b) -> p k b", k=2)
                    prefix_p = psum[:, 0, 0:2 * TILES].rearrange("p (k b) -> p k b", k=2)
                    link(v.tensor_single_scalar(tiles_f[:], total_p, float(P - 1), ALU.add))
                    link(v.tensor_copy(tiles_i[:], tiles_f[:]))
                    link(v.tensor_single_scalar(tiles_i[:], tiles_i[:], 7, ALU.arith_shift_right))
                    link(v.tensor_copy(tiles_f[:], tiles_i[:]))
                    for k in range(2):
                        link(v.tensor_tensor_scan(ends[:, k, :], tiles_f[:, k, :], zeros[:], 0.0, ALU.add, ALU.add))
                    link(v.tensor_sub(place[:], ends[:], tiles_f[:]))
                    link(v.scalar_tensor_tensor(place[:], place[:], float(P), prefix_p, ALU.mult, ALU.add))
                    for k in range(2):
                        link(v.tensor_tensor(picked[0:TILES, 0, k, :], ends[0:TILES, k, :], ident[0:TILES, 0:TILES], ALU.mult))
                        link(v.tensor_reduce(end_col[0:TILES, k:k + 1], picked[0:TILES, 0, k, :], AX.X, ALU.add))
                    for k, table in enumerate((tile_of_d, tile_of_s)):
                        if k:
                            v.wait_ge(owner_done, 1)
                        link(v.tensor_scalar(ended[0:TILES, :], iota_t[0:TILES, :], end_col[0:TILES, k:k + 1], None, ALU.is_ge))
                        v.sem_inc(owner_copied, 1)
                        v.wait_ge(owner_done, k + 1)
                        for c in range(0, NT, 512):
                            w = min(512, NT - c)
                            link(v.tensor_single_scalar(table[0:1, c:c + w], psum[0:1, 4 + c // 512, 0:w], float(TILES - 1), ALU.min))
                    v.sem_inc(owner_copied, 1)
                    v.wait_ge(loaded, 16 * ((4 if TAIL else 2) + 26))
                    link(v.tensor_tensor(att_w[:], att[:], w_gat[:, 0:F].unsqueeze(1).to_broadcast([P, 2, F]), ALU.mult))
                    link(v.tensor_reduce(w_gat[:, F:F + 2 * HEADS], att_w[:].rearrange("p a (h c) -> p (a h) c", h=HEADS), AX.X, ALU.add))
                    link(v.tensor_add(we_0[:], we_0[:], be1_0[:]))
                    v.wait_ge(owner_done, 3)
                    link(v.tensor_copy(w_3t[:], psum[:, 2, 0:P]))

                @block.tensor
                def _(pe):
                    pe.wait_ge(hist_done, 1)
                    h2 = hist[:].rearrange("p k b -> p (k b)")
                    pe.matmul(psum[:, 0, 0:2 * TILES], before[:], h2, start=True, stop=True)
                    pe.matmul(psum[:, 1, 0:2 * TILES], ones[:], h2, start=True, stop=True).then_inc(prefix_done, 1)
                    for k in range(2):
                        pe.wait_ge(owner_copied, k + 1)
                        for c in range(0, NT, 512):
                            w = min(512, NT - c)
                            last = pe.matmul(psum[:, 4 + c // 512, 0:w], ones[0:TILES, :], ended[0:TILES, c:c + w], start=True, stop=True)
                        last.then_inc(owner_done, 1)
                    pe.wait_ge(loaded, 16 * ((4 if TAIL else 2) + 26))
                    pe.transpose(psum[:, 2, 0:P], w_3[:], ident[:]).then_inc(owner_done, 1)

            attrs_loaded = [sem(f"attrs_loaded{h}") for h in range(2)]
            attrs_copied = sem("attrs_copied")
            keys_copied = sem("keys_copied")
            addr_ready = sem("addr_ready")
            scattered = [sem(f"scattered{h}") for h in range(2)]
            half_free = [sem(f"half_free{h}") for h in range(2)]
            half_taken = sem("half_taken")
            rank_step = sem("rank_step")
            addr_step = sem("addr_step")
            HALF_SC = 2 * CS * 16

            def attr_src(k, start, h):
                return attrs_in[k][0:MAIN, :].rearrange("(p c) w -> p c w", c=COLS)[:, ds(start, CS), :]

            with nc.Block() as block:

                @block.sync
                def _(sp):
                    with sp.Fori(0, SORT_ITERS) as i:
                        for h in range(2):
                            sp.wait_ge(attrs_copied, i * 2 + h + 1)
                            for k in range(3):
                                sp.dma_start(ea[k][:, h, :, :], attr_src(k, i * (2 * CS) + h * CS, h)).then_inc(attrs_loaded[h], 16)
                    if TAIL:
                        sp.wait_ge(attrs_copied, 2 * SORT_ITERS + 1)
                        for k in range(3):
                            sp.dma_start(ea[k][0:TAIL, 0, 0, :], attrs_in[k][MAIN:E, :]).then_inc(attrs_loaded[0], 16)

                @block.scalar
                def _(act):
                    def copy_attrs(h, rows, c):
                        at = COL_ATTR
                        for k in range(3):
                            w = ea[k].shape[3]
                            act.copy(out_d[0:rows, h, 0:c, at:at + w], ea[k][0:rows, h, 0:c, :])
                            at += w
                        act.copy(out_d[0:rows, h, 0:c, REC - 1:REC], one_col[0:rows].unsqueeze(1).to_broadcast([rows, c, 1]))
                        act.copy(out_s[0:rows, h, 0:c, 2:3], one_col[0:rows].unsqueeze(1).to_broadcast([rows, c, 1]))
                        return act.copy(out_s[0:rows, h, 0:c, 3:4], zero_col[0:rows].unsqueeze(1).to_broadcast([rows, c, 1]))

                    act.sem_inc(attrs_copied, 2)
                    act.sem_inc(half_free[0], 1)
                    with act.Fori(0, SORT_ITERS) as i:
                        for h in range(2):
                            act.wait_ge(half_free[h], i + 1)
                            act.wait_ge(attrs_loaded[h], i * 48 + 48)
                            copy_attrs(h, P, CS).then_inc(attrs_copied, 1)
                    if TAIL:
                        act.wait_ge(half_free[0], SORT_ITERS + 1)
                        act.wait_ge(attrs_loaded[0], SORT_ITERS * 48 + 48)
                        copy_attrs(0, TAIL, 1).then_inc(attrs_copied, 1)

                @block.vector
                def _(v):
                    def rank(col, h, j, step):
                        for k in range(2):
                            v.wait_ge(rank_step, step + k)
                            v.scalar_tensor_tensor(picked[:, h, k, :], iota_row[:, 0:TILES], bin_[k][:, col], place[:, k, :],
                                                   ALU.is_equal, ALU.mult, accum_out=pos[:, h, k, j:j + 1])
                        for k in range(2):
                            v.scalar_tensor_tensor(place[:, k, :], iota_row[:, 0:TILES], bin_[k][:, col], place[:, k, :],
                                                   ALU.is_equal, ALU.add).then_inc(rank_step, 1)

                    def address(h, c, col0, n_rank, n_addr, rows):
                        sl = lambda m: m[0:rows, h, :, 0:c]
                        v.wait_ge(rank_step, n_rank)
                        v.tensor_copy(sl(pos_i), sl(pos)).then_inc(addr_step, 1)
                        v.wait_ge(addr_step, n_addr + 1)
                        v.tensor_single_scalar(sl(pos_t), sl(pos_i), 7, ALU.arith_shift_right).then_inc(addr_step, 1)
                        v.wait_ge(addr_step, n_addr + 2)
                        v.tensor_single_scalar(sl(pos_i), sl(pos_i), P - 1, ALU.bitwise_and).then_inc(addr_step, 1)
                        v.wait_ge(addr_step, n_addr + 3)
                        v.tensor_copy(out_d[0:rows, h, 0:c, COL_LOCAL], local[0][0:rows, col0])
                        v.tensor_copy(out_d[0:rows, h, 0:c, COL_INDEX].bitcast(i32), key[1][0:rows, col0])
                        v.tensor_copy(out_s[0:rows, h, 0:c, COL_LOCAL], local[1][0:rows, col0])
                        v.tensor_copy(out_s[0:rows, h, 0:c, COL_INDEX].bitcast(i32), key[0][0:rows, col0])
                        v.scalar_tensor_tensor(sl(addr), sl(pos_i), float(NT), sl(pos_t), ALU.mult, ALU.add).then_inc(addr_ready, 1)

                    v.sem_inc(rank_step, 2)
                    with v.Fori(0, SORT_ITERS) as i:
                        for h in range(2):
                            for j in range(CS):
                                rank(ds(i * (2 * CS) + h * CS + j, 1), h, j, i * (4 * CS) + 2 * (h * CS + j) + 1)
                            v.wait_ge(half_free[h], i + 1)
                            address(h, CS, ds(i * (2 * CS) + h * CS, CS), i * (4 * CS) + 2 * (h + 1) * CS + 2,
                                    i * 6 + h * 3, P)
                    if TAIL:
                        rank(ds(COLS, 1), 0, 0, 2 * COLS + 1)
                        v.wait_ge(half_free[0], SORT_ITERS + 1)
                        address(0, 1, ds(COLS, 1), 2 * COLS + 4, SORT_ITERS * 6, TAIL)

                @block.gpsimd
                def _(pool):
                    def scatter(h, c, rows, other_done=None):
                        for j in range(c):
                            if other_done is not None and j == min(2, c - 1):
                                pool.wait_ge(scattered[1 - h], other_done)
                                pool.sem_inc(half_free[1 - h], 1)
                            for k, (table, of) in enumerate(((rec_d, out_d), (rec_s, out_s))):
                                pool.indirect_dma_start(
                                    table, bass.IndirectOffsetOnAxis(ap=addr[0:rows, h, k, j:j + 1], axis=0),
                                    of[0:rows, h, j, :], None).then_inc(scattered[h], 16)

                    pool.dma_start(spare_row[:], t["x"][0:1, :]).then_inc(scattered[1], 16)
                    with pool.Fori(0, SORT_ITERS) as i:
                        for h in range(2):
                            pool.wait_ge(attrs_copied, i * 2 + h + 3)
                            pool.wait_ge(addr_ready, i * 2 + h + 1)
                            pool.sem_inc(half_taken, 1)
                            scatter(h, CS, P, i * HALF_SC + (HALF_SC if h else 16))
                    if TAIL:
                        pool.wait_ge(attrs_copied, 2 * SORT_ITERS + 3)
                        pool.wait_ge(addr_ready, 2 * SORT_ITERS + 1)
                        scatter(0, 1, TAIL)
                    pool.wait_ge(scattered[0], SORT_ITERS * HALF_SC + (32 if TAIL else 0))
                    pool.wait_ge(scattered[1], SORT_ITERS * HALF_SC + 16)

        onehot_ready = sem("onehot_ready")
        tile_summed = sem("tile_summed")
        tile_added = sem("tile_added")
        rec_loaded = [sem(f"rec_loaded{h}") for h in range(2)]
        row_here = [sem(f"row_here{s}") for s in range(BODY)]
        cleared = sem("cleared")
        spare = sb("spare", [1, 2, F])
        half_started = sem("half_started")
        stats_made = sem("stats_made")
        work = ctx.enter_context(ExitStack())
        onehot = sb("onehot", [P, ONEHOTS, P])
        loop = [0]

        def free_rings(pe, v):
            if pe is not None and loop[0] == 0:
                pe.sem_inc(tile_summed, BODY)
            if v is not None and loop[0] == 0:
                v.sem_inc(tile_added, SUM_BANKS)

        def load_records(sp, table, width, ring):
            view = table.rearrange("(p t) w -> p t w", t=NT)
            base = loop[0] * NT
            with sp.Fori(0, ITERS) as i:
                for h in range(2):
                    sp.wait_ge(tile_summed, i * BODY + (base + h * HALF + HALF))
                    sp.dma_start(ring[:, h, :, :], view[:, ds(i * BODY + h * HALF, HALF), :]).then_inc(rec_loaded[h], 16)

        def gather_rows(pool, table, width, ring):
            base, turns = loop[0] * NT, loop[0] * ITERS
            with pool.Fori(0, ITERS) as i:
                for h in range(2):
                    pool.wait_ge(rec_loaded[h], i * 16 + (turns + 1) * 16)
                    pool.wait_ge(tile_summed, i * BODY + (base + h * HALF + HALF))
                    pool.sem_inc(half_started, 1)
                    for u in range(HALF):
                        slot = h * HALF + u
                        pool.indirect_dma_start(
                            gathered[:, slot, 0:width], None, table,
                            bass.IndirectOffsetOnAxis(ap=ring[:, h, u, COL_INDEX:COL_INDEX + 1].bitcast(i32), axis=0),
                        ).then_inc(row_here[slot], 16)

        def tile_numbers(eng, regs, table, at):
            eng.load(regs, table[0:1, ds(at, HALF)])
            return [eng.snap(r, min_val=0, max_val=TILES - 1) for r in regs]

        def sum_layer(rec_table, rec_w, ring, tile_of, x_table, extra):
            base, turns = loop[0] * NT, loop[0] * ITERS
            at = EXTRA - (extra[1] - extra[0]) if extra else FEAT
            end = FEAT + F
            width = end - at

            with nc.Block() as block:

                @block.sync
                def _(sp):
                    load_records(sp, rec_table, rec_w, ring)

                @block.gpsimd
                def _(pool):
                    gather_rows(pool, x_table, F, ring)

                @block.vector
                def _(v):
                    free_rings(None, v)
                    regs = [v.alloc_register(f"v{loop[0]}_{u}") for u in range(HALF)]
                    with v.Fori(0, ITERS) as i:
                        for h in range(2):
                            nodes = tile_numbers(v, regs, tile_of, i * BODY + h * HALF)
                            v.wait_ge(rec_loaded[h], i * 16 + (turns + 1) * 16)

                            def make_onehot(u):
                                s = h * HALF + u
                                v.wait_ge(tile_summed, i * BODY + (base + s + 1 + BODY - ONEHOTS))
                                v.tensor_scalar(onehot[:, s % ONEHOTS, :], iota_row[:], ring[:, h, u, COL_LOCAL:COL_LOCAL + 1],
                                                None, ALU.is_equal).then_inc(onehot_ready, 1)

                            def add(u):
                                s = h * HALF + u
                                v.wait_ge(tile_summed, i * BODY + (base + s + 1 + BODY))
                                v.wait_ge(tile_added, i * BODY + (base + s + SUM_BANKS))
                                to = sums[:, ds(nodes[u], 1), at:end].rearrange("p a w -> p (a w)")
                                v.tensor_tensor(to, psum[:, s % SUM_BANKS, 0:width], to, ALU.add).then_inc(tile_added, 1)

                            for u in range(3):
                                make_onehot(u)
                            for u in range(HALF):
                                if u + 3 < HALF:
                                    make_onehot(u + 3)
                                add(u)
                    for r in regs:
                        v.free_register(r)

                @block.tensor
                def _(pe):
                    free_rings(pe, None)
                    with pe.Fori(0, ITERS) as i:
                        for s in range(BODY):
                            h, u, bank = s // HALF, s % HALF, s % SUM_BANKS
                            pe.wait_ge(onehot_ready, i * BODY + (base + s + 1))
                            pe.wait_ge(tile_added, i * BODY + (base + s + 1))
                            if extra:
                                pe.matmul(psum[:, bank, 0:width - F], onehot[:, s % ONEHOTS, :], ring[:, h, u, extra[0]:extra[1]],
                                          start=True, stop=True)
                            pe.wait_ge(row_here[s], i * 16 + (turns + 1) * 16)
                            pe.matmul(psum[:, bank, width - F:width], onehot[:, s % ONEHOTS, :], gathered[:, s, 0:F],
                                      start=True, stop=True).then_inc(tile_summed, 1)
            loop[0] += 1

        def clear_sums(name, lo, hi):
            with nc.Block() as block:
                @block.vector
                def _(v):
                    v.memset(sums[:, :, lo:hi], 0.0).then_inc(cleared, 1)

        phase = [0]

        def mlp_phase(we, w1, b1, w2, b2, hidden, feat_t, extra_out=None, scale=None):
            k = phase[0]
            phase[0] += 1
            s_stage, s_ext, s_extc, s_agg, s_aggc, s_h, s_hc, s_o, s_oc = (sem(f"m{k}_{n}") for n in (
                "staged", "extras_turned", "extras_copied", "sums_turned", "sums_copied", "hidden", "hidden_copied", "outs", "outs_copied"))
            with ExitStack() as scope:
                stage = sb(f"m{k}_stage", [P, GROUP, SUM_W], f32, scope)
                ext = sb(f"m{k}_ext", [EXTRA, GROUP_W], f32, scope)
                agg = sb(f"m{k}_agg", [P, GROUP_W], f32, scope)
                hid = sb(f"m{k}_hid", [P, max(hidden, 1), GROUP_W], f32, scope)
                with nc.Block() as block:

                    @block.vector
                    def _(v):
                        v.sem_inc(s_agg, 1)
                        with v.Fori(0, GROUPS) as g:
                            v.wait_ge(s_agg, g + 1)
                            v.tensor_copy(stage[:], sums[:, ds(g * GROUP, GROUP), :]).then_inc(s_stage, 1)
                            v.wait_ge(s_ext, g + 1)
                            v.tensor_copy(ext[:], psum[0:EXTRA, 0, :]).then_inc(s_extc, 1)
                            v.wait_ge(s_agg, g + 2)
                            v.tensor_copy(agg[:], psum[:, 1, :]).then_inc(s_aggc, 1)

                    @block.scalar
                    def _(act):
                        with act.Fori(0, GROUPS) as g:
                            for j in range(hidden):
                                act.wait_ge(s_h, g * hidden + (j + 1))
                                act.activation(hid[:, j, :], psum[:, 2 + j, :], ACT.Relu, bias=b1[:, j:j + 1]).then_inc(s_hc, 1)
                            act.wait_ge(s_o, g + 1)
                            if hidden:
                                act.activation(feat_t[:, ds(g * GROUP_W, GROUP_W)], psum[:, 4, :], ACT.Identity, bias=b2).then_inc(s_oc, 1)
                            else:
                                act.activation(feat_t[:, ds(g * GROUP_W, GROUP_W)], psum[:, 4, :], ACT.Copy, scale=scale).then_inc(s_oc, 1)

                    @block.tensor
                    def _(pe):
                        pe.sem_inc(s_oc, 1)
                        with pe.Fori(0, GROUPS) as g:
                            pe.wait_ge(s_stage, g + 1)
                            for j in range(GROUP):
                                last = pe.transpose(psum[0:EXTRA, 0, j * P:(j + 1) * P], stage[:, j, 0:EXTRA], ident[:])
                            last.then_inc(s_ext, 1)
                            pe.wait_ge(s_extc, g + 1)
                            for j in range(GROUP):
                                last = pe.matmul(psum[:, 1, j * P:(j + 1) * P], stage[:, j, FEAT:FEAT + F], ident[:],
                                                 start=j == 0, stop=not hidden and j == GROUP - 1)
                            if hidden:
                                last = pe.matmul(psum[:, 1, :], we[:], ext[:], start=False, stop=True)
                            last.then_inc(s_agg, 1)
                            pe.wait_ge(s_aggc, g + 1)
                            for j in range(hidden):
                                pe.matmul(psum[:, 2 + j, :], w1[:, j * F:(j + 1) * F], agg[:], start=True, stop=True).then_inc(s_h, 1)
                            pe.wait_ge(s_oc, g + 1)
                            if hidden:
                                for j in range(hidden):
                                    pe.wait_ge(s_hc, g * hidden + (j + 1))
                                    last = pe.matmul(psum[:, 4, :], w2[:, j, :], hid[:, j, :], start=j == 0, stop=j == hidden - 1)
                            else:
                                pe.matmul(psum[:, 4, :], w2[:], agg[:], start=True, stop=False)
                                last = pe.matmul(psum[:, 4, :], extra_out[:], ext[:], start=False, stop=True)
                            last.then_inc(s_o, 1)

        def bn_phase(feat_t):
            CH = 512
            chunks = [(c, min(CH, N - c)) for c in range(0, N, CH)]
            steps, rooted = sem("bn_steps"), sem("bn_rooted")
            with ExitStack() as scope:
                stats = sb("bn_stats", [P, len(chunks), 6], f32, scope)
                mv = sb("bn_mv", [P, 4], f32, scope)
                with nc.Block() as block:

                    @block.vector
                    def _(v):
                        for n, (c, w) in enumerate(chunks):
                            v.bn_stats(stats[:, n, :], feat_t[:, c:c + w]).then_inc(steps, 1)
                        n = [len(chunks)]
                        v.wait_ge(steps, n[0])

                        def link(ins):
                            n[0] += 1
                            ins.then_inc(steps, 1)
                            v.wait_ge(steps, n[0])

                        link(v.bn_aggr(mv[:, 0:2], stats[:].rearrange("p a b -> p (a b)")))
                        v.wait_ge(rooted, 1)
                        link(v.reciprocal(mv[:, 3:4], mv[:, 2:3]))
                        link(v.tensor_mul(bn_scale, mv[:, 3:4], gamma_0))
                        link(v.tensor_mul(mv[:, 0:1], mv[:, 0:1], bn_scale))
                        link(v.tensor_sub(bn_shift, beta_0, mv[:, 0:1]))

                    @block.scalar
                    def _(act):
                        act.wait_ge(steps, len(chunks) + 1)
                        act.activation(mv[:, 2:3], mv[:, 1:2], ACT.Sqrt, bias=eps[:]).then_inc(rooted, 1)

        def norm_rows(v, link, src, dst, stats, mv, root_in, root_out, n_in, n_out):
            for j in range(GROUP):
                last = v.bn_stats(stats[:, j, :], src[:, j, :])
            link(last)
            v.sem_inc(stats_made, 1)
            for j in range(GROUP):
                last = v.bn_aggr(mv[:, j, 0:2], stats[:, j, :])
            last.then_inc(root_in, 1)
            v.wait_ge(root_out, n_out)
            link(v.reciprocal(mv[:, :, 3:4], mv[:, :, 2:3]))
            for j in range(GROUP):
                last = v.tensor_scalar(dst[:, j, :], src[:, j, :], mv[:, j, 0:1], mv[:, j, 3:4], ALU.subtract, ALU.mult)
            return last

        def store_group(sp, table, g, tile, done):
            whole = table[0:table.shape[0] // GROUP_W * GROUP_W, :]
            sp.dma_start(whole.rearrange("(t p) f -> p t f", p=P)[:, ds(g * GROUP, GROUP), :], tile).then_inc(done, 16)

        def prime(eng, done, n):
            for j in range(n):
                eng.dma_start(spare[0:1, j, :], t["x"][0:1, :]).then_inc(done, 16)

        def finish_phase(feat_t, scale, shift, x_old, x_new, last_layer=False):
            k = phase[0]
            phase[0] += 1
            s_y, s_turned, s_x, s_chain, s_var, s_root, s_new, s_st = (sem(f"f{k}_{n}") for n in (
                "affine", "turned", "x_loaded", "steps", "variances", "roots", "normed", "stored"))
            with ExitStack() as scope:
                yt = sb(f"f{k}_yt", [P, GROUP_W], f32, scope)
                xo = sb(f"f{k}_x", [P, GROUP, F], f32, scope)
                zz = sb(f"f{k}_z", [P, GROUP, F], f32, scope)
                xn = sb(f"f{k}_new", [P, GROUP, F], f32, scope)
                stats = sb(f"f{k}_stats", [P, GROUP, 6], f32, scope)
                mv = sb(f"f{k}_mv", [P, GROUP, 4], f32, scope)
                with nc.Block() as block:

                    @block.sync
                    def _(sp):
                        view = x_old.rearrange("(t p) f -> p t f", p=P)
                        sp.sem_inc(s_new, 1)
                        with sp.Fori(0, GROUPS) as g:
                            sp.wait_ge(s_new, g + 1)
                            sp.dma_start(xo[:], view[:, ds(g * GROUP, GROUP), :]).then_inc(s_x, 16)

                    @block.scalar
                    def _(act):
                        act.sem_inc(s_turned, 1)
                        prime(act, s_st, 1)
                        with act.Fori(0, GROUPS if not last_layer else GROUPS - 1) as g:
                            act.wait_ge(s_turned, g + 1)
                            act.activation(yt[:], feat_t[:, ds(g * GROUP_W, GROUP_W)], ACT.Identity, bias=shift, scale=scale).then_inc(s_y, 1)
                            act.wait_ge(s_var, g + 1)
                            act.activation(mv[:, :, 2:3], mv[:, :, 1:2], ACT.Sqrt, bias=eps[:]).then_inc(s_root, 1)
                            act.wait_ge(s_new, g + 2)
                            store_group(act, x_new, g, xn[:], s_st)
                        if last_layer:
                            g = GROUPS - 1
                            act.wait_ge(s_turned, g + 1)
                            act.activation(yt[:], feat_t[:, g * GROUP_W:(g + 1) * GROUP_W], ACT.Identity, bias=shift, scale=scale).then_inc(s_y, 1)
                            act.wait_ge(s_var, g + 1)
                            act.activation(mv[:, :, 2:3], mv[:, :, 1:2], ACT.Sqrt, bias=eps[:]).then_inc(s_root, 1)
                            act.wait_ge(s_new, g + 2)
                            n = 0
                            for j in range(GROUP):
                                r0 = g * GROUP_W + j * P
                                rows_here = min(P, N - r0)
                                if rows_here > 0:
                                    act.dma_start(x_new[r0:r0 + rows_here, :], xn[0:rows_here, j, :]).then_inc(s_st, 16)
                                    n += 1
                            act.wait_ge(s_st, 16 * (GROUPS + n))
                        else:
                            act.wait_ge(s_st, 16 * (GROUPS + 1))

                    @block.tensor
                    def _(pe):
                        pe.sem_inc(s_chain, 1)
                        with pe.Fori(0, GROUPS) as g:
                            pe.wait_ge(s_y, g + 1)
                            pe.wait_ge(s_chain, g * 3 + 1)
                            for j in range(GROUP):
                                last = pe.transpose(psum[:, 0, j * P:(j + 1) * P], yt[:, j * P:(j + 1) * P], ident[:])
                            last.then_inc(s_turned, 1)

                    @block.vector
                    def _(v):
                        with v.Fori(0, GROUPS) as g:
                            n = [0]

                            def link(ins):
                                n[0] += 1
                                ins.then_inc(s_chain, 1)
                                v.wait_ge(s_chain, g * 3 + (n[0] + 1))

                            v.wait_ge(s_turned, g + 2)
                            v.wait_ge(s_x, g * 16 + 16)
                            link(v.tensor_tensor(zz[:], psum[:, 0, :].rearrange("p (j f) -> p j f", j=GROUP), xo[:], ALU.add))
                            v.wait_ge(s_st, g * 16 + 16)
                            norm_rows(v, link, zz, xn, stats, mv, s_var, s_root, g + 1, g + 1).then_inc(s_new, 1)
                            assert n[0] == 3

        def project_phase(x_table):
            k = phase[0]
            phase[0] += 1
            s_x, s_t, s_tc, s_h, s_hc, s_st, s_ad = (sem(f"p{k}_{n}") for n in (
                "x_loaded", "turned", "turned_copied", "rows", "rows_copied", "stored", "dst_copied"))
            with ExitStack() as scope:
                xo = sb(f"p{k}_x", [P, GROUP, F], f32, scope)
                xt = sb(f"p{k}_xt", [P, GROUP, P], f32, scope)
                hr = sb(f"p{k}_rows", [P, GROUP, ROW], f32, scope)
                WP = 256
                with nc.Block() as block:

                    @block.sync
                    def _(sp):
                        sp.sem_inc(s_t, 1)
                        view = x_table.rearrange("(t p) f -> p t f", p=P)
                        with sp.Fori(0, GROUPS) as g:
                            sp.wait_ge(s_t, g + 1)
                            sp.dma_start(xo[:], view[:, ds(g * GROUP, GROUP), :]).then_inc(s_x, 16)

                    @block.tensor
                    def _(pe):
                        pe.sem_inc(s_hc, 1)
                        pe.sem_inc(s_ad, 1)
                        with pe.Fori(0, GROUPS) as g:
                            pe.wait_ge(s_x, g * 16 + 16)
                            for j in range(GROUP):
                                last = pe.transpose(psum[:, 0, j * P:(j + 1) * P], xo[:, j, :], ident[:])
                            last.then_inc(s_t, 1)
                            pe.wait_ge(s_tc, g + 1)
                            pe.wait_ge(s_hc, g + 1)
                            pe.wait_ge(s_ad, g + 1)
                            for j in range(GROUP):
                                last = pe.matmul(psum[:, 2 + j // 2, (j % 2) * WP:(j % 2) * WP + ROW + HEADS], xt[:, j, :], w_gat[:], start=True, stop=True)
                            last.then_inc(s_h, 1)

                    @block.scalar
                    def _(act):
                        prime(act, s_st, 2)
                        hv = psum[:, 2:4, :].rearrange("p a (b w) -> p (a b) w", b=2)
                        hd = hrow.rearrange("(t p) f -> p t f", p=P)
                        ad = asrc.rearrange("(t p) f -> p t f", p=P)
                        with act.Fori(0, GROUPS) as g:
                            act.wait_ge(s_t, g + 2)
                            act.copy(xt[:].rearrange("p j f -> p (j f)"), psum[:, 0, :]).then_inc(s_tc, 1)
                            act.wait_ge(s_h, g + 1)
                            act.wait_ge(s_st, g * 32 + 32)
                            act.copy(hr[:], hv[:, :, 0:ROW]).then_inc(s_hc, 1)
                            act.wait_ge(s_hc, g + 2)
                            act.dma_start(hd[:, ds(g * GROUP, GROUP), :], hr[:]).then_inc(s_st, 16)
                            act.dma_start(ad[:, ds(g * GROUP, GROUP), :], hr[:, :, F:ROW]).then_inc(s_st, 16)
                        act.wait_ge(s_st, GROUPS * 32 + 32)

                    @block.vector
                    def _(v):
                        hv = psum[:, 2:4, :].rearrange("p a (b w) -> p (a b) w", b=2)
                        v.memset(sums[:, :, FEAT:], 0.0).then_inc(cleared, 1)
                        with v.Fori(0, GROUPS) as g:
                            v.wait_ge(s_hc, g + 2)
                            v.tensor_copy(dst_max[:, ds(g * GROUP, GROUP), 0:HEADS], hv[:, :, ROW:ROW + HEADS])
                            v.tensor_copy(dst_max[:, ds(g * GROUP, GROUP), HEADS:], hv[:, :, F:ROW]).then_inc(s_ad, 1)

        def max_phase():
            base, turns = loop[0] * NT, loop[0] * ITERS
            QUADS = HALF // 4
            s_split, s_turn, s_turnc, s_red, s_steps = (sem(f"x_{n}") for n in ("split", "turned", "turned_copied", "reduced", "steps"))
            with ExitStack() as scope:
                mask = sb("x_mask", [P, ONEHOTS, P], bf16, scope)
                parts = sb("x_parts", [P, 2, HALF, 32], bf16, scope)
                rest = sb("x_rest", [P, 2, HALF, HEADS], f32, scope)
                turned = sb("x_turned", [P, 4, P], bf16, scope)
                select = sb("x_select", [P, HEADS, P], bf16, scope)
                sel_i = sb("x_sel_i", [P, 1], i32, scope)
                sel_j = sb("x_sel_j", [P, 1], i32, scope)
                sel_f = sb("x_sel_f", [P, 1], f32, scope)
                sel_c = sb("x_sel_c", [P, HEADS], f32, scope)
                big = sb("x_big", [P, 4, HEADS], f32, scope)
                psum_b = psum[:].bitcast(bf16)
                with nc.Block() as block:
                    @block.vector
                    def _(v):
                        n = [0]

                        def link(ins):
                            n[0] += 1
                            ins.then_inc(s_steps, 1)
                            v.wait_ge(s_steps, n[0])

                        link(v.memset(parts[:], 0.0))
                        link(v.tensor_copy(sel_i[:], iota_part[:]))
                        link(v.tensor_single_scalar(sel_j[:], sel_i[:], HEADS - 1, ALU.bitwise_and))
                        link(v.tensor_copy(sel_f[:], sel_j[:]))
                        link(v.tensor_scalar(sel_c[:], iota_row[:, 0:HEADS], sel_f[:], None, ALU.is_equal))
                        link(v.tensor_copy(select[:], sel_c[:].unsqueeze(2).to_broadcast([P, HEADS, P])))

                PREP = 6
                with nc.Block() as block:

                    @block.sync
                    def _(sp):
                        load_records(sp, rec_d, REC, rec)

                    @block.gpsimd
                    def _(pool):
                        gather_rows(pool, asrc, HEADS, rec)

                    @block.scalar
                    def _(act):
                        with act.Fori(0, ITERS) as i:
                            for q in range(2 * QUADS):
                                act.wait_ge(s_turn, i * (2 * QUADS) + (q + 1))
                                act.wait_ge(tile_summed, i * BODY + (base + q * 4 + 4 + BODY - 16))
                                act.copy(turned[:, q % 4, :], psum_b[:, 6 + q % 2, 0:P]).then_inc(s_turnc, 1)

                    @block.tensor
                    def _(pe):
                        pe.sem_inc(s_turnc, 2)
                        with pe.Fori(0, ITERS) as i:
                            for h in range(2):
                                pe.wait_ge(s_split, i * 2 + (h + 1))

                                def turn(q):
                                    qq = h * QUADS + q
                                    pe.wait_ge(s_turnc, i * (2 * QUADS) + (qq + 1))
                                    pe.transpose(psum_b[:, 6 + qq % 2, 0:P],
                                                 parts[:, h, 4 * q:4 * q + 4, :].rearrange("p a b -> p (a b)"), ident_b[:]).then_inc(s_turn, 1)

                                turn(0)
                                for q in range(QUADS):
                                    qq = h * QUADS + q
                                    if q + 1 < QUADS:
                                        turn(q + 1)
                                    pe.wait_ge(s_turnc, i * (2 * QUADS) + (qq + 3))
                                    for j in range(4):
                                        s = h * HALF + 4 * q + j
                                        b = (s % 2) * 2
                                        pe.wait_ge(onehot_ready, i * BODY + (base + s + 1))
                                        pe.wait_ge(tile_added, i * BODY + (base + s + 3))
                                        for hd in range(HEADS):
                                            pe.matmul(psum[:, b + hd // 4, (hd % 4) * P:(hd % 4) * P + P],
                                                      select[32 * j:32 * j + 32, hd, :], turned[32 * j:32 * j + 32, qq % 4, :],
                                                      start=hd % 4 == 0, stop=False, tile_position=(32 * j, 0))
                                        for c in range(2):
                                            last = pe.matmul(psum[:, b + c, :].rearrange("p (h e) -> p h e", h=4), mask[:, s % ONEHOTS, :],
                                                             ident_b[:].unsqueeze(1).to_broadcast([P, 4, P]), start=False, stop=True)
                                        last.then_inc(tile_summed, 1)

                    @block.vector
                    def _(v):
                        regs = [v.alloc_register(f"x{u}") for u in range(HALF)]
                        with v.Fori(0, ITERS) as i:
                            for h in range(2):
                                nodes = tile_numbers(v, regs, tile_of_d, i * BODY + h * HALF)
                                v.wait_ge(rec_loaded[h], i * 16 + (turns + 1) * 16)

                                def make_mask(u):
                                    s = h * HALF + u
                                    v.wait_ge(tile_summed, i * BODY + (base + s + 1 + BODY - ONEHOTS))
                                    v.tensor_scalar(mask[:, s % ONEHOTS, :], iota_row[:], rec[:, h, u, COL_LOCAL:COL_LOCAL + 1],
                                                    -BIG, ALU.not_equal, ALU.mult).then_inc(onehot_ready, 1)

                                def take_max(u):
                                    s = h * HALF + u
                                    v.wait_ge(tile_summed, i * BODY + (base + s + 1 + BODY))
                                    b = (s % 2) * 2
                                    v.tensor_reduce(big[:, u % 4, :], psum[:, b:b + 2, :].rearrange("p a (h e) -> p (a h) e", h=4), AX.X, ALU.max).then_inc(s_red, 1)
                                    v.wait_ge(s_red, i * BODY + (s + 1))
                                    v.wait_ge(tile_added, i * BODY + (base + s + SUM_BANKS))
                                    to = dst_max[:, ds(nodes[u], 1), HEADS:].rearrange("p a w -> p (a w)")
                                    v.tensor_tensor(to, big[:, u % 4, :], to, ALU.max).then_inc(tile_added, 1)

                                n = [0]

                                def link(ins):
                                    n[0] += 1
                                    ins.then_inc(s_steps, 1)
                                    v.wait_ge(s_steps, i * 8 + (PREP + h * 4 + n[0]))

                                for u in range(2):
                                    make_mask(u)
                                for u in range(HALF):
                                    v.wait_ge(row_here[h * HALF + u], i * 16 + (turns + 1) * 16)
                                src = gathered[:, h * HALF:(h + 1) * HALF, 0:HEADS]
                                r = rest[:, h, :, :]
                                part = lambda m: parts[:, h, :, m * HEADS:(m + 1) * HEADS]
                                link(v.tensor_copy(part(0), src))
                                link(v.tensor_sub(r, src, part(0)))
                                link(v.tensor_copy(part(1), r))
                                link(v.tensor_sub(r, r, part(1)))
                                v.tensor_copy(part(2), r).then_inc(s_split, 1)
                                for u in range(HALF):
                                    if u + 2 < HALF:
                                        make_mask(u + 2)
                                    take_max(u)
                        for r in regs:
                            v.free_register(r)
                        v.wait_ge(tile_added, base + NT + SUM_BANKS)
                        c = [ITERS * 8 + PREP]

                        def link(ins):
                            c[0] += 1
                            ins.then_inc(s_steps, 1)
                            v.wait_ge(s_steps, c[0])

                        m = dst_max[:, :, HEADS:]
                        link(v.tensor_add(m, m, dst_max[:, :, 0:HEADS]))
                        link(v.scalar_tensor_tensor(m, m, SLOPE, m, ALU.mult, ALU.max))
            loop[0] += 1

        def attention_phase():
            base, turns = loop[0] * NT, loop[0] * ITERS
            QUADS = HALF // 4
            s_turn, s_turnc, s_ad, s_e, s_exp, s_msg, s_steps = (sem(f"a_{n}") for n in (
                "turned", "turned_copied", "dst_rows", "scores", "exps", "messages", "steps"))
            with ExitStack() as scope:
                turned = sb("a_turned", [P, 2, 4, P], f32, scope)
                score = sb("a_score", [P, 2, 4, HEADS], f32, scope)
                expd = sb("a_exp", [P, 2, 4, HEADS], f32, scope)
                msg = sb("a_msg", [P, 8, ROW], f32, scope)
                with nc.Block() as block:

                    @block.sync
                    def _(sp):
                        load_records(sp, rec_d, REC, rec)

                    @block.gpsimd
                    def _(pool):
                        gather_rows(pool, hrow, ROW, rec)

                    @block.scalar
                    def _(act):
                        with act.Fori(0, ITERS) as i:
                            for qq in range(2 * QUADS):
                                act.wait_ge(s_turn, i * (2 * QUADS) + (qq + 1))
                                act.wait_ge(s_ad, i * (2 * QUADS) + (qq + 1))
                                act.copy(turned[:, qq % 2, :, :].rearrange("p a b -> p (a b)"), psum[:, 4 + qq % 2, :]).then_inc(s_turnc, 1)
                                act.wait_ge(s_e, i * (2 * QUADS) + (qq + 1))
                                act.wait_ge(s_msg, i * (2 * QUADS) + (qq + 1))
                                act.activation(expd[:, qq % 2, :, :], score[:, qq % 2, :, :], ACT.Exp).then_inc(s_exp, 1)

                    @block.tensor
                    def _(pe):
                        pe.sem_inc(s_turnc, 2)
                        pe.sem_inc(s_ad, 2)
                        regs = [pe.alloc_register(f"pe{u}") for u in range(HALF)]
                        with pe.Fori(0, ITERS) as i:
                            for h in range(2):
                                nodes = tile_numbers(pe, regs, tile_of_d, i * BODY + h * HALF)

                                def turn(q):
                                    qq = h * QUADS + q
                                    pe.wait_ge(s_turnc, i * (2 * QUADS) + (qq + 1))
                                    for j in range(4):
                                        s = qq * 4 + j
                                        pe.wait_ge(onehot_ready, i * BODY + (base + s + 1))
                                        last = pe.transpose(psum[:, 4 + qq % 2, j * P:(j + 1) * P], onehot[:, s % ONEHOTS, :], ident[:])
                                    last.then_inc(s_turn, 1)

                                def dst_rows(q):
                                    qq = h * QUADS + q
                                    pe.wait_ge(s_turnc, i * (2 * QUADS) + (qq + 3))
                                    pe.wait_ge(s_steps, i * (2 * QUADS) * 3 + qq * 3 + 6)
                                    for j in range(4):
                                        s = qq * 4 + j
                                        last = pe.matmul(psum[:, 6 + qq % 2, j * 16:(j + 1) * 16], turned[:, qq % 2, j, :],
                                                         dst_max[:, ds(nodes[4 * q + j], 1), :].rearrange("p a w -> p (a w)"), start=True, stop=True)
                                    last.then_inc(s_ad, 1)

                                def sum_quad(q):
                                    qq = h * QUADS + q
                                    pe.wait_ge(s_msg, i * (2 * QUADS) + (qq + 3))
                                    for j in range(4):
                                        s = qq * 4 + j
                                        pe.wait_ge(tile_added, i * BODY + (base + s + 1))
                                        pe.matmul(psum[:, s % SUM_BANKS, 0:ROW], onehot[:, s % ONEHOTS, :], msg[:, s % 8, :],
                                                  start=True, stop=True).then_inc(tile_summed, 1)

                                turn(0)
                                for q in range(QUADS):
                                    dst_rows(q)
                                    if q + 1 < QUADS:
                                        turn(q + 1)
                                    sum_quad(q)
                        for r in regs:
                            pe.free_register(r)

                    @block.vector
                    def _(v):
                        v.sem_inc(s_steps, 6)
                        v.sem_inc(s_msg, 2)
                        regs = [v.alloc_register(f"a{u}") for u in range(HALF)]
                        with v.Fori(0, ITERS) as i:
                            for h in range(2):
                                nodes = tile_numbers(v, regs, tile_of_d, i * BODY + h * HALF)
                                v.wait_ge(rec_loaded[h], i * 16 + (turns + 1) * 16)

                                def make_onehots(q):
                                    for u in range(4 * q, 4 * q + 4):
                                        s = h * HALF + u
                                        v.wait_ge(tile_summed, i * BODY + (base + s + 1 + BODY - ONEHOTS))
                                        v.tensor_scalar(onehot[:, s % ONEHOTS, :], iota_row[:], rec[:, h, u, COL_LOCAL:COL_LOCAL + 1],
                                                        None, ALU.is_equal).then_inc(onehot_ready, 1)

                                def scores(q):
                                    qq = h * QUADS + q
                                    sl = slice(4 * qq, 4 * qq + 4)
                                    sc = score[:, qq % 2, :, :]
                                    ad = psum[:, 6 + qq % 2, 0:64].rearrange("p (a w) -> p a w", a=4)
                                    n = [0]

                                    def link(ins):
                                        n[0] += 1
                                        ins.then_inc(s_steps, 1)
                                        v.wait_ge(s_steps, i * (2 * QUADS) * 3 + qq * 3 + (6 + n[0]))

                                    for u in range(4 * qq, 4 * qq + 4):
                                        v.wait_ge(row_here[u], i * 16 + (turns + 1) * 16)
                                    v.wait_ge(s_ad, i * (2 * QUADS) + (qq + 3))
                                    link(v.tensor_tensor(sc, ad[:, :, 0:HEADS], gathered[:, sl, F:ROW], ALU.add))
                                    link(v.scalar_tensor_tensor(sc, sc, SLOPE, sc, ALU.mult, ALU.max))
                                    link(v.tensor_tensor(sc, sc, ad[:, :, HEADS:], ALU.subtract))
                                    v.tensor_single_scalar(sc, sc, 0.0, ALU.min).then_inc(s_e, 1)

                                def messages(q):
                                    qq = h * QUADS + q
                                    sl = slice(4 * qq, 4 * qq + 4)
                                    m = msg[:, 4 * (qq % 2):4 * (qq % 2) + 4, :]
                                    v.wait_ge(s_exp, i * (2 * QUADS) + (qq + 1))
                                    v.wait_ge(tile_summed, i * BODY + (base + qq * 4 + 4 + BODY - 8))
                                    v.tensor_copy(m[:, :, F:ROW], expd[:, qq % 2, :, :])
                                    for j in range(4):
                                        last = v.tensor_tensor(
                                            m[:, j, 0:F].rearrange("p (h c) -> p h c", h=HEADS),
                                            gathered[:, 4 * qq + j, 0:F].rearrange("p (h c) -> p h c", h=HEADS),
                                            expd[:, qq % 2, j, :].unsqueeze(2).to_broadcast([P, HEADS, HEAD_CH]), ALU.mult)
                                    last.then_inc(s_msg, 1)

                                def add(q):
                                    for u in range(4 * q, 4 * q + 4):
                                        s = h * HALF + u
                                        v.wait_ge(tile_summed, i * BODY + (base + s + 1 + BODY))
                                        v.wait_ge(tile_added, i * BODY + (base + s + SUM_BANKS))
                                        to = sums[:, ds(nodes[u], 1), FEAT:].rearrange("p a w -> p (a w)")
                                        v.tensor_tensor(to, psum[:, s % SUM_BANKS, 0:ROW], to, ALU.add).then_inc(tile_added, 1)

                                make_onehots(0)
                                for q in range(QUADS):
                                    scores(q)
                                    if q + 1 < QUADS:
                                        make_onehots(q + 1)
                                    messages(q)
                                    add(q)
                        for r in regs:
                            v.free_register(r)
            loop[0] += 1

        def attention_finish(x_old, x_new):
            s_x, s_rows, s_chain, s_score, s_self, s_var, s_root, s_min, s_exp, s_new, s_st = (sem(f"g_{n}") for n in (
                "x_loaded", "rows_loaded", "steps", "scores", "self_exps", "variances", "roots", "minima", "exps", "normed", "stored"))
            with ExitStack() as scope:
                xo = sb("g_x", [P, GROUP, F], f32, scope)
                zz = sb("g_z", [P, GROUP, F], f32, scope)
                ee = sb("g_e", [P, GROUP, F], f32, scope)
                xn = sb("g_new", [P, GROUP, F], f32, scope)
                hr = sb("g_rows", [P, GROUP, ROW], f32, scope)
                score = sb("g_score", [P, GROUP, HEADS], f32, scope)
                den = sb("g_den", [P, GROUP, HEADS], f32, scope)
                stats = sb("g_stats", [P, GROUP, 6], f32, scope)
                mv = sb("g_mv", [P, GROUP, 4], f32, scope)
                STEPS = 18
                with nc.Block() as block:

                    @block.sync
                    def _(sp):
                        view = x_old.rearrange("(t p) f -> p t f", p=P)
                        rows_view = hrow.rearrange("(t p) f -> p t f", p=P)
                        sp.sem_inc(s_new, 1)
                        with sp.Fori(0, GROUPS) as g:
                            sp.wait_ge(s_new, g + 1)
                            sp.dma_start(xo[:], view[:, ds(g * GROUP, GROUP), :]).then_inc(s_x, 16)
                            sp.dma_start(hr[:], rows_view[:, ds(g * GROUP, GROUP), :]).then_inc(s_rows, 16)

                    @block.scalar
                    def _(act):
                        prime(act, s_st, 1)
                        with act.Fori(0, GROUPS) as g:
                            act.wait_ge(s_score, g + 1)
                            act.activation(score[:], score[:], ACT.Exp).then_inc(s_self, 1)
                            for r in range(2):
                                act.wait_ge(s_var, g * 2 + (r + 1))
                                act.activation(mv[:, :, 2:3], mv[:, :, 1:2], ACT.Sqrt, bias=eps[:]).then_inc(s_root, 1)
                                if r == 0:
                                    act.wait_ge(s_min, g + 1)
                                    act.activation(ee[:], ee[:], ACT.Exp).then_inc(s_exp, 1)
                            act.wait_ge(s_new, g + 2)
                            store_group(act, x_new, g, xn[:], s_st)
                        act.wait_ge(s_st, 16 * (GROUPS + 1))

                    @block.vector
                    def _(v):
                        wide = lambda a: a.unsqueeze(1).to_broadcast([P, GROUP, F])
                        with v.Fori(0, GROUPS) as g:
                            n = [0]

                            def link(ins):
                                n[0] += 1
                                ins.then_inc(s_chain, 1)
                                v.wait_ge(s_chain, g * STEPS + n[0])

                            here = lambda m: m[:, ds(g * GROUP, GROUP), :]
                            v.wait_ge(s_rows, g * 16 + 16)
                            link(v.tensor_tensor(score[:], hr[:, :, F:ROW], here(dst_max)[:, :, 0:HEADS], ALU.add))
                            link(v.scalar_tensor_tensor(score[:], score[:], SLOPE, score[:], ALU.mult, ALU.max))
                            v.tensor_tensor(score[:], score[:], here(dst_max)[:, :, HEADS:], ALU.subtract).then_inc(s_score, 1)
                            v.wait_ge(s_self, g + 1)
                            link(v.tensor_tensor(den[:], here(sums)[:, :, DEN:], score[:], ALU.add))
                            link(v.reciprocal(den[:], den[:]))
                            blocks = lambda m, j: m[:, j, 0:F].rearrange("p (h c) -> p h c", h=HEADS)
                            each = lambda m, j: m[:, j, :].unsqueeze(2).to_broadcast([P, HEADS, HEAD_CH])
                            for j in range(GROUP):
                                last = v.tensor_tensor(blocks(zz, j), blocks(hr, j), each(score, j), ALU.mult)
                            link(last)
                            link(v.tensor_tensor(zz[:], zz[:], here(sums)[:, :, FEAT:FEAT + F], ALU.add))
                            for j in range(GROUP):
                                last = v.tensor_tensor(blocks(zz, j), blocks(zz, j), each(den, j), ALU.mult)
                            link(last)
                            link(v.tensor_tensor(zz[:], zz[:], wide(bias_1), ALU.add))
                            link(norm_rows(v, link, zz, zz, stats, mv, s_var, s_root, 0, g * 2 + 1))
                            link(v.tensor_tensor(zz[:], zz[:], wide(gamma_1), ALU.mult))
                            link(v.tensor_tensor(zz[:], zz[:], wide(beta_1), ALU.add))
                            v.tensor_single_scalar(ee[:], zz[:], 0.0, ALU.min).then_inc(s_min, 1)
                            v.wait_ge(s_min, g + 1)
                            link(v.tensor_single_scalar(zz[:], zz[:], 0.0, ALU.max))
                            v.wait_ge(s_exp, g + 1)
                            link(v.scalar_tensor_tensor(zz[:], ee[:], -1.0, zz[:], ALU.add, ALU.add))
                            v.wait_ge(s_x, g * 16 + 16)
                            link(v.tensor_tensor(zz[:], zz[:], xo[:], ALU.add))
                            v.wait_ge(s_st, g * 16 + 16)
                            norm_rows(v, link, zz, xn, stats, mv, s_var, s_root, 0, g * 2 + 2).then_inc(s_new, 1)
                            assert n[0] == STEPS, n

        attrs = (COL_ATTR, REC)
        sum_layer(rec_d, REC, rec, tile_of_d, xs[0], attrs)
        with ExitStack() as scope:
            feat_t = sb("feat_t0", [P, GROUPS * GROUP_W], f32, scope)
            mlp_phase(we_0, w1_0, b1_0, w2_0, b2_0, 2, feat_t)
            bn_phase(feat_t)
            finish_phase(feat_t, bn_scale, bn_shift, xs[0], xs[1])
        project_phase(xs[1])
        max_phase()
        attention_phase()
        attention_finish(xs[1], xs[2])
        clear_sums("c2", FEAT, DEN)
        sum_layer(rec_d, REC, rec, tile_of_d, xs[2], None)
        with ExitStack() as scope:
            feat_t = sb("feat_t2", [P, GROUPS * GROUP_W], f32, scope)
            mlp_phase(we_2, w1_2, b1_2, w2_2, b2_2, 1, feat_t)
            finish_phase(feat_t, one_col, zero_col, xs[2], xs[3])
        clear_sums("c3", 0, DEN)
        sum_layer(rec_s, REC_S, recs, tile_of_s, xs[3], (2, 3))
        with ExitStack() as scope:
            feat_t = sb("feat_t3", [P, GROUPS * GROUP_W], f32, scope)
            mlp_phase(None, None, None, w_3t, None, 0, feat_t, extra_out=b_3, scale=agg_w)
            finish_phase(feat_t, one_col, zero_col, xs[3], out, last_layer=True)


_INS = ["x", "src", "dst", "edge_attr_16", "edge_attr_3", "edge_attr_6",
        "L0_gnn_We0", "L0_gnn_be0", "L0_gnn_We1", "L0_gnn_be1", "L0_gnn_W1", "L0_gnn_b1", "L0_gnn_W2", "L0_gnn_b2",
        "L0_gnn_gamma", "L0_gnn_beta", "L1_gnn_W", "L1_gnn_att_src", "L1_gnn_att_dst", "L1_gnn_bias",
        "L1_gnn_ln_gamma", "L1_gnn_ln_beta", "L2_gnn_We", "L2_gnn_be", "L2_gnn_W1", "L2_gnn_b1", "L2_gnn_W2",
        "L2_gnn_b2", "L3_gnn_W", "L3_gnn_b", "L3_gnn_agg_weight"]


def kernel(**inputs):
    import numpy as _np
    import concourse.bacc as _bacc
    from concourse import mybir as _mybir
    from concourse.bass_utils import run_bass_kernel_spmd as _run

    nc = _bacc.Bacc("TRN2", target_bir_lowering=False, num_devices=1)
    arrays, t = {}, {}
    for name in _INS:
        a = _np.ascontiguousarray(inputs[name])
        arrays[f"in_{name}"] = a
        t[name] = nc.dram_tensor(f"in_{name}", a.shape, _mybir.dt.from_np(a.dtype), kind="ExternalInput").ap()
    n, f = inputs["x"].shape
    out = nc.dram_tensor("out_0", (n, f), _mybir.dt.float32, kind="ExternalOutput").ap()
    gnn_kernel(nc, t, out)
    r = _run(nc, [arrays], core_ids=[0])
    return r.results[0]["out_0"]
```

```python
from contextlib import ExitStack

import concourse.bass as bass
from concourse import mybir

P = 128
F = 128
HEADS = 8
HEAD_CH = F // HEADS
HALF = 16
BODY = 2 * HALF
GROUP = 4
GROUP_W = GROUP * P
REC = 28
COL_LOCAL, COL_INDEX, COL_ATTR = 0, 1, 2
EXTRA = REC - COL_ATTR
REC_S = 4
SUM_W = EXTRA + F + HEADS
FEAT = EXTRA
DEN = EXTRA + F
ROW = F + HEADS
ONEHOTS = 8
SUM_BANKS = 4
BIG = float(2.0 ** 100)
NORM_EPS = 1e-5
SLOPE = 0.2


def _sizes(n_nodes, n_edges):
    s = {}
    s["tiles"] = -(-n_nodes // P)
    s["groups"] = -(-s["tiles"] // GROUP)
    s["padded_tiles"] = s["groups"] * GROUP
    most = (n_edges + s["tiles"] * (P - 1)) // P
    s["slots"] = -(-most // BODY) * BODY
    s["cols"] = n_edges // P
    s["tail"] = n_edges - s["cols"] * P
    s["sort_half"] = max(k for k in range(1, 13) if s["cols"] % (2 * k) == 0)
    return s


def gnn_kernel(nc, t, out):
    f32, bf16, i32 = mybir.dt.float32, mybir.dt.bfloat16, mybir.dt.int32
    ALU, ACT, AX = mybir.AluOpType, mybir.ActivationFunctionType, mybir.AxisListType
    N, E = t["x"].shape[0], t["src"].shape[0]
    z = _sizes(N, E)
    TILES, GROUPS, PT, NT = z["tiles"], z["groups"], z["padded_tiles"], z["slots"]
    COLS, TAIL, CS = z["cols"], z["tail"], z["sort_half"]
    SORT_ITERS, ITERS = COLS // (2 * CS), NT // BODY
    MAIN = COLS * P
    ds = bass.ds

    ctx = ExitStack()
    with ctx:
        def sb(name, shape, dt=f32, where=ctx):
            return where.enter_context(nc.sbuf_tensor(name, shape, dt))

        def sem(name):
            return ctx.enter_context(nc.semaphore(name))

        def dram(name, shape, dt=f32):
            return nc.dram_tensor(name, shape, dt, kind="Internal").ap()

        rec_d = dram("rec_by_dst", (P * NT, REC))
        rec_s = dram("rec_by_src", (P * NT, REC_S))
        xs = [dram(f"x_layer{k}", (PT * P, F)) for k in range(4)]
        hrow = dram("attention_rows", (PT * P, ROW))
        gathered_rows = dram("gathered_rows", (P, NT, ROW))

        psum = ctx.enter_context(nc.psum_tensor("psum", [P, 8, 512], f32))

        iota_row = sb("iota_row", [P, P])
        iota_part = sb("iota_part", [P, 1])
        ident = sb("ident", [P, P])
        ident_b = sb("ident_b", [P, P], bf16)
        eps = sb("eps", [P, 1])
        w1_0 = sb("w1_0", [P, 2 * F])
        w2_0 = sb("w2_0", [P, 2, F])
        we_0 = sb("we_0", [EXTRA, F])
        be1_0 = sb("be1_0", [EXTRA, F])
        w_gat = sb("w_gat", [P, F + 2 * HEADS])
        att = sb("att", [P, 2, F])
        att_w = sb("att_w", [P, 2, F])
        w1_2 = sb("w1_2", [P, F])
        w2_2 = sb("w2_2", [P, 1, F])
        we_2 = sb("we_2", [EXTRA, F])
        w_3 = sb("w_3", [P, F])
        w_3t = sb("w_3t", [P, F])
        b_3 = sb("b_3", [EXTRA, F])
        b1_0 = sb("b1_0", [P, 2])
        cols = sb("cols", [P, 8])
        b2_0, gamma_0, beta_0, b1_2, b2_2, agg_w = (cols[:, k:k + 1] for k in range(6))
        rows = sb("rows", [P, 3, F])
        bias_1, gamma_1, beta_1 = (rows[:, k, :] for k in range(3))
        affine = sb("affine", [P, 4])
        bn_scale, bn_shift, one_col, zero_col = (affine[:, k:k + 1] for k in range(4))
        tile_of_d = sb("tile_of_d", [1, NT], i32)
        tile_of_s = sb("tile_of_s", [1, NT], i32)
        sums = sb("sums", [P, PT, SUM_W])
        dst_max = sb("dst_max", [P, PT, 2 * HEADS])
        rec_src = sb("rec_src", [P, COLS + 1, REC_S])
        addr_src = sb("addr_src", [P, COLS + 1], i32)

        loaded = sem("loaded")
        made = sem("made")
        dve_steps = sem("dve_steps")
        hist_done = sem("hist_done")
        prefix_done = sem("prefix_done")
        owner_done = sem("owner_done")
        owner_copied = sem("owner_copied")
        filled = sem("filled")
        small_psum = sem("small_psum")

        sort = ctx.enter_context(ExitStack())
        with sort:
            W = COLS + 1
            key = [sb(f"key{k}", [P, W], i32, sort) for k in range(2)]
            tmp = sb("key_tmp", [P, W], i32, sort)
            bin_ = [sb(f"bin{k}", [P, W], f32, sort) for k in range(2)]
            local = [sb(f"local{k}", [P, W], f32, sort) for k in range(2)]
            junk = sb("junk", [P, W], bf16, sort)
            hist = sb("hist", [P, 2, TILES], f32, sort)
            tiles_f = sb("tiles_f", [P, 2, TILES], f32, sort)
            tiles_i = sb("tiles_i", [P, 2, TILES], i32, sort)
            ends = sb("ends", [P, 2, TILES], f32, sort)
            zeros = sb("zeros", [P, TILES], f32, sort)
            place = sb("place", [P, 2, TILES], f32, sort)
            end_col = sb("end_col", [P, 2], f32, sort)
            before = sb("before", [P, P], f32, sort)
            ones = sb("ones", [P, P], f32, sort)
            iota_t = sb("iota_t", [P, NT], f32, sort)
            ended = sb("ended", [P, NT], f32, sort)
            blank = sb("blank", [P, HALF, REC], f32, sort)
            FILL = blank[:, :, :]
            picked = sb("picked", [P, 2, 2, TILES], f32, sort)
            pos = sb("pos", [P, 2, 2, CS], f32, sort)
            pos_i = sb("pos_i", [P, 2, 2, CS], i32, sort)
            pos_t = sb("pos_t", [P, 2, 2, CS], i32, sort)
            addr = sb("addr", [P, 2, CS], i32, sort)
            ea = [sb(f"ea{w}", [P, 2, CS, w], f32, sort) for w in (6, 3, 16)]
            out_d = sb("out_d", [P, 2, CS, REC], f32, sort)
            spare_row = sb("spare_row", [1, F], f32, sort)

            keys_in = [t["dst"], t["src"]]
            attrs_in = [t["edge_attr_6"], t["edge_attr_3"], t["edge_attr_16"]]

            with nc.Block() as block:

                @block.sync
                def _(sp):
                    sp.wait_ge(made, 2)
                    for k in range(2):
                        sp.dma_start(key[k][:, 0:COLS], keys_in[k][0:MAIN].rearrange("(p c) -> p c", p=P)).then_inc(loaded, 16)
                        if TAIL:
                            sp.dma_start(key[k][0:TAIL, COLS:W], keys_in[k][MAIN:E].rearrange("(p c) -> p c", c=1)).then_inc(loaded, 16)
                    sp.wait_ge(loaded, 16 * (4 if TAIL else 2))
                    col = lambda a, c=1: a.rearrange("(p c) -> p c", c=c)
                    row = lambda a: a.rearrange("(a n) -> a n", a=1)
                    sp.wait_ge(made, 3)
                    small = [
                        (w1_0[:], t["L0_gnn_W1"]), (w2_0[:], t["L0_gnn_W2"].rearrange("(j p) n -> p j n", j=2)),
                        (we_0[0:6, :], t["L0_gnn_We0"]), (we_0[6:9, :], t["L0_gnn_We1"]),
                        (we_0[25:26, :], row(t["L0_gnn_be0"])), (be1_0[25:26, :], row(t["L0_gnn_be1"])),
                        (w_gat[:, 0:F], t["L1_gnn_W"]),
                        (att[:, 0, :], row(t["L1_gnn_att_src"].rearrange("h c -> (h c)")).to_broadcast([P, F])),
                        (att[:, 1, :], row(t["L1_gnn_att_dst"].rearrange("h c -> (h c)")).to_broadcast([P, F])),
                        (w1_2[:], t["L2_gnn_W1"]), (w2_2[:, 0, :], t["L2_gnn_W2"]),
                        (we_2[9:25, :], t["L2_gnn_We"]), (we_2[25:26, :], row(t["L2_gnn_be"])),
                        (w_3[:], t["L3_gnn_W"]), (b_3[25:26, :], row(t["L3_gnn_b"])),
                        (b2_0, col(t["L0_gnn_b2"])), (gamma_0, col(t["L0_gnn_gamma"])), (beta_0, col(t["L0_gnn_beta"])),
                        (b1_2, col(t["L2_gnn_b1"])), (b2_2, col(t["L2_gnn_b2"])),
                        (agg_w, row(t["L3_gnn_agg_weight"]).to_broadcast([P, 1])),
                        (bias_1, row(t["L1_gnn_bias"]).to_broadcast([P, F])),
                        (gamma_1, row(t["L1_gnn_ln_gamma"]).to_broadcast([P, F])),
                        (beta_1, row(t["L1_gnn_ln_beta"]).to_broadcast([P, F])),
                        (b1_0[:, 0:1], col(t["L0_gnn_b1"][0:P])), (b1_0[:, 1:2], col(t["L0_gnn_b1"][P:2 * P])),
                    ]
                    for to, of in small:
                        sp.dma_start(to, of).then_inc(loaded, 16)
                    sp.wait_ge(loaded, 16 * ((4 if TAIL else 2) + len(small)))

                @block.scalar
                def _(act):
                    act.wait_ge(made, 4)
                    rd = rec_d.rearrange("(p t) w -> p t w", t=NT)
                    with act.Fori(0, NT // HALF) as i:
                        act.dma_start(rd[:, ds(i * HALF, HALF), :], FILL).then_inc(filled, 16)
                    rs = rec_s.rearrange("(p t) w -> p t w", t=NT)
                    few = blank[:, :, 0:REC_S]
                    with act.Fori(0, NT // HALF) as i:
                        act.dma_start(rs[:, ds(i * HALF, HALF), :], few).then_inc(filled, 16)
                    act.dma_start(xs[0][0:N, :], t["x"]).then_inc(filled, 16)
                    total = 2 * (NT // HALF) + 1
                    spare = PT * P - N
                    for r in range(0, spare, P):
                        k = min(P, spare - r)
                        act.dma_start(xs[0][N + r:N + r + k, :], ones[0:k, :]).then_inc(filled, 16)
                        total += 1
                    act.wait_ge(filled, 16 * total)

                @block.gpsimd
                def _(pool):
                    for k in range(2):
                        pool.memset(key[k][:, COLS:W], -P).then_inc(made, 1)
                    for m in (we_0, be1_0, we_2, b_3):
                        pool.memset(m[:], 0.0)
                    pool.memset(dst_max[:], 0.0)
                    pool.memset(zeros[:], 0.0)
                    pool.memset(rec_src[:], 0.0)
                    pool.memset(one_col, 1.0)
                    pool.memset(zero_col, 0.0)
                    pool.memset(eps[:], NORM_EPS).then_inc(made, 1)
                    pool.memset(ones[:], 1.0)
                    pool.memset(blank[:], 0.0).then_inc(small_psum, 1)
                    pool.wait_ge(small_psum, 1)
                    pool.memset(blank[:, :, 0:1], -1.0).then_inc(made, 1)
                    pool.iota(iota_row[:], pattern=[[1, P]], base=0, channel_multiplier=0, allow_small_or_imprecise_dtypes=True)
                    pool.iota(iota_part[:], pattern=[[0, 1]], base=0, channel_multiplier=1, allow_small_or_imprecise_dtypes=True)
                    pool.iota(iota_t[:], pattern=[[1, NT]], base=0, channel_multiplier=0, allow_small_or_imprecise_dtypes=True).then_inc(made, 1)

                @block.vector
                def _(v):
                    n = [0]

                    def link(ins):
                        n[0] += 1
                        ins.then_inc(dve_steps, 1)
                        v.wait_ge(dve_steps, n[0])

                    v.memset(sums[:, :, :], 0.0)
                    v.wait_ge(made, 5)
                    link(v.tensor_scalar(ident[:], iota_row[:], iota_part[:], None, ALU.is_equal))
                    v.tensor_copy(ident_b[:], ident[:])
                    v.tensor_scalar(before[:], iota_row[:], iota_part[:], None, ALU.is_gt)
                    v.wait_ge(loaded, 16 * (4 if TAIL else 2))
                    for k in range(2):
                        link(v.tensor_single_scalar(tmp[:], key[k][:], 7, ALU.arith_shift_right))
                        link(v.tensor_copy(bin_[k][:], tmp[:]))
                        link(v.tensor_single_scalar(tmp[:], key[k][:], P - 1, ALU.bitwise_and))
                        link(v.tensor_copy(local[k][:], tmp[:]))
                    v.tensor_copy(rec_src[:, :, COL_LOCAL:COL_LOCAL + 1], local[1][:].unsqueeze(2))
                    v.tensor_copy(rec_src[:, :, COL_INDEX:COL_INDEX + 1].bitcast(i32), key[0][:].unsqueeze(2))
                    v.memset(rec_src[:, :, 2:3], 1.0)
                    for k in range(2):
                        for b in range(TILES):
                            link(v.tensor_scalar(junk[:], bin_[k][:], float(b), 0.0, ALU.is_equal, ALU.add,
                                                 accum_out=hist[:, k, b:b + 1]))
                    v.sem_inc(hist_done, 1)
                    v.wait_ge(prefix_done, 1)
                    total_p = psum[:, 1, 0:2 * TILES].rearrange("p (k b) -> p k b", k=2)
                    prefix_p = psum[:, 0, 0:2 * TILES].rearrange("p (k b) -> p k b", k=2)
                    link(v.tensor_single_scalar(tiles_f[:], total_p, float(P - 1), ALU.add))
                    link(v.tensor_copy(tiles_i[:], tiles_f[:]))
                    link(v.tensor_single_scalar(tiles_i[:], tiles_i[:], 7, ALU.arith_shift_right))
                    link(v.tensor_copy(tiles_f[:], tiles_i[:]))
                    for k in range(2):
                        link(v.tensor_tensor_scan(ends[:, k, :], tiles_f[:, k, :], zeros[:], 0.0, ALU.add, ALU.add))
                    link(v.tensor_sub(place[:], ends[:], tiles_f[:]))
                    link(v.scalar_tensor_tensor(place[:], place[:], float(P), prefix_p, ALU.mult, ALU.add))
                    for k in range(2):
                        link(v.tensor_tensor(picked[0:TILES, 0, k, :], ends[0:TILES, k, :], ident[0:TILES, 0:TILES], ALU.mult))
                        link(v.tensor_reduce(end_col[0:TILES, k:k + 1], picked[0:TILES, 0, k, :], AX.X, ALU.add))
                    for k, table in enumerate((tile_of_d, tile_of_s)):
                        if k:
                            v.wait_ge(owner_done, 1)
                        link(v.tensor_scalar(ended[0:TILES, :], iota_t[0:TILES, :], end_col[0:TILES, k:k + 1], None, ALU.is_ge))
                        v.sem_inc(owner_copied, 1)
                        v.wait_ge(owner_done, k + 1)
                        for c in range(0, NT, 512):
                            w = min(512, NT - c)
                            link(v.tensor_single_scalar(table[0:1, c:c + w], psum[0:1, 4 + c // 512, 0:w], float(TILES - 1), ALU.min))
                    v.sem_inc(owner_copied, 1)
                    v.wait_ge(loaded, 16 * ((4 if TAIL else 2) + 26))
                    link(v.tensor_tensor(att_w[:], att[:], w_gat[:, 0:F].unsqueeze(1).to_broadcast([P, 2, F]), ALU.mult))
                    link(v.tensor_reduce(w_gat[:, F:F + 2 * HEADS], att_w[:].rearrange("p a (h c) -> p (a h) c", h=HEADS), AX.X, ALU.add))
                    link(v.tensor_add(we_0[:], we_0[:], be1_0[:]))
                    v.wait_ge(owner_done, 3)
                    link(v.tensor_copy(w_3t[:], psum[:, 2, 0:P]))

                @block.tensor
                def _(pe):
                    pe.wait_ge(hist_done, 1)
                    h2 = hist[:].rearrange("p k b -> p (k b)")
                    pe.matmul(psum[:, 0, 0:2 * TILES], before[:], h2, start=True, stop=True)
                    pe.matmul(psum[:, 1, 0:2 * TILES], ones[:], h2, start=True, stop=True).then_inc(prefix_done, 1)
                    for k in range(2):
                        pe.wait_ge(owner_copied, k + 1)
                        for c in range(0, NT, 512):
                            w = min(512, NT - c)
                            last = pe.matmul(psum[:, 4 + c // 512, 0:w], ones[0:TILES, :], ended[0:TILES, c:c + w], start=True, stop=True)
                        last.then_inc(owner_done, 1)
                    pe.wait_ge(loaded, 16 * ((4 if TAIL else 2) + 26))
                    pe.transpose(psum[:, 2, 0:P], w_3[:], ident[:]).then_inc(owner_done, 1)

            attrs_loaded = [sem(f"attrs_loaded{h}") for h in range(2)]
            attrs_copied = sem("attrs_copied")
            keys_copied = sem("keys_copied")
            addr_ready = sem("addr_ready")
            scattered = [sem(f"scattered{h}") for h in range(2)]
            half_free = [sem(f"half_free{h}") for h in range(2)]
            half_taken = sem("half_taken")
            rank_step = sem("rank_step")
            addr_step = sem("addr_step")
            HALF_SC = CS * 16

            def attr_src(k, start, h):
                return attrs_in[k][0:MAIN, :].rearrange("(p c) w -> p c w", c=COLS)[:, ds(start, CS), :]

            with nc.Block() as block:

                @block.sync
                def _(sp):
                    with sp.Fori(0, SORT_ITERS) as i:
                        for h in range(2):
                            sp.wait_ge(attrs_copied, i * 2 + h + 1)
                            for k in range(3):
                                sp.dma_start(ea[k][:, h, :, :], attr_src(k, i * (2 * CS) + h * CS, h)).then_inc(attrs_loaded[h], 16)
                    if TAIL:
                        sp.wait_ge(attrs_copied, 2 * SORT_ITERS + 1)
                        for k in range(3):
                            sp.dma_start(ea[k][0:TAIL, 0, 0, :], attrs_in[k][MAIN:E, :]).then_inc(attrs_loaded[0], 16)

                @block.scalar
                def _(act):
                    def copy_attrs(h, rows, c):
                        at = COL_ATTR
                        for k in range(3):
                            w = ea[k].shape[3]
                            act.copy(out_d[0:rows, h, 0:c, at:at + w], ea[k][0:rows, h, 0:c, :])
                            at += w
                        return act.copy(out_d[0:rows, h, 0:c, REC - 1:REC], one_col[0:rows].unsqueeze(1).to_broadcast([rows, c, 1]))

                    act.sem_inc(attrs_copied, 2)
                    act.sem_inc(half_free[0], 1)
                    with act.Fori(0, SORT_ITERS) as i:
                        for h in range(2):
                            act.wait_ge(half_free[h], i + 1)
                            act.wait_ge(attrs_loaded[h], i * 48 + 48)
                            copy_attrs(h, P, CS).then_inc(attrs_copied, 1)
                    if TAIL:
                        act.wait_ge(half_free[0], SORT_ITERS + 1)
                        act.wait_ge(attrs_loaded[0], SORT_ITERS * 48 + 48)
                        copy_attrs(0, TAIL, 1).then_inc(attrs_copied, 1)

                @block.vector
                def _(v):
                    def rank(col, h, j, step):
                        for k in range(2):
                            v.wait_ge(rank_step, step + k)
                            v.scalar_tensor_tensor(picked[:, h, k, :], iota_row[:, 0:TILES], bin_[k][:, col], place[:, k, :],
                                                   ALU.is_equal, ALU.mult, accum_out=pos[:, h, k, j:j + 1])
                        for k in range(2):
                            v.scalar_tensor_tensor(place[:, k, :], iota_row[:, 0:TILES], bin_[k][:, col], place[:, k, :],
                                                   ALU.is_equal, ALU.add).then_inc(rank_step, 1)

                    def address(h, c, col0, n_rank, n_addr, rows):
                        sl = lambda m: m[0:rows, h, :, 0:c]
                        v.wait_ge(rank_step, n_rank)
                        v.tensor_copy(sl(pos_i), sl(pos)).then_inc(addr_step, 1)
                        v.wait_ge(addr_step, n_addr + 1)
                        v.tensor_single_scalar(sl(pos_t), sl(pos_i), 7, ALU.arith_shift_right).then_inc(addr_step, 1)
                        v.wait_ge(addr_step, n_addr + 2)
                        v.tensor_single_scalar(sl(pos_i), sl(pos_i), P - 1, ALU.bitwise_and).then_inc(addr_step, 1)
                        v.wait_ge(addr_step, n_addr + 3)
                        v.tensor_copy(out_d[0:rows, h, 0:c, COL_LOCAL], local[0][0:rows, col0])
                        v.tensor_copy(out_d[0:rows, h, 0:c, COL_INDEX].bitcast(i32), key[1][0:rows, col0])
                        v.scalar_tensor_tensor(addr_src[0:rows, col0], pos_i[0:rows, h, 1, 0:c], float(NT), pos_t[0:rows, h, 1, 0:c], ALU.mult, ALU.add)
                        v.scalar_tensor_tensor(addr[0:rows, h, 0:c], pos_i[0:rows, h, 0, 0:c], float(NT), pos_t[0:rows, h, 0, 0:c], ALU.mult, ALU.add).then_inc(addr_ready, 1)

                    v.sem_inc(rank_step, 2)
                    with v.Fori(0, SORT_ITERS) as i:
                        for h in range(2):
                            for j in range(CS):
                                rank(ds(i * (2 * CS) + h * CS + j, 1), h, j, i * (4 * CS) + 2 * (h * CS + j) + 1)
                            v.wait_ge(half_free[h], i + 1)
                            address(h, CS, ds(i * (2 * CS) + h * CS, CS), i * (4 * CS) + 2 * (h + 1) * CS + 2,
                                    i * 6 + h * 3, P)
                    if TAIL:
                        rank(ds(COLS, 1), 0, 0, 2 * COLS + 1)
                        v.wait_ge(half_free[0], SORT_ITERS + 1)
                        address(0, 1, ds(COLS, 1), 2 * COLS + 4, SORT_ITERS * 6, TAIL)

                @block.gpsimd
                def _(pool):
                    def scatter(h, c, rows, other_done=None):
                        for j in range(c):
                            if other_done is not None and j == min(2, c - 1):
                                pool.wait_ge(scattered[1 - h], other_done)
                                pool.sem_inc(half_free[1 - h], 1)
                            pool.indirect_dma_start(
                                rec_d, bass.IndirectOffsetOnAxis(ap=addr[0:rows, h, j:j + 1], axis=0),
                                out_d[0:rows, h, j, :], None).then_inc(scattered[h], 16)

                    pool.dma_start(spare_row[:], t["x"][0:1, :]).then_inc(scattered[1], 16)
                    with pool.Fori(0, SORT_ITERS) as i:
                        for h in range(2):
                            pool.wait_ge(attrs_copied, i * 2 + h + 3)
                            pool.wait_ge(addr_ready, i * 2 + h + 1)
                            pool.sem_inc(half_taken, 1)
                            scatter(h, CS, P, i * HALF_SC + (HALF_SC if h else 16))
                    if TAIL:
                        pool.wait_ge(attrs_copied, 2 * SORT_ITERS + 3)
                        pool.wait_ge(addr_ready, 2 * SORT_ITERS + 1)
                        scatter(0, 1, TAIL)
                    pool.wait_ge(scattered[0], SORT_ITERS * HALF_SC + (16 if TAIL else 0))
                    pool.wait_ge(scattered[1], SORT_ITERS * HALF_SC + 16)

        onehot_ready = sem("onehot_ready")
        tile_summed = sem("tile_summed")
        tile_added = sem("tile_added")
        rec_loaded = [sem(f"rec_loaded{h}") for h in range(2)]
        row_here = [sem(f"row_here{s}") for s in range(BODY)]
        cleared = sem("cleared")
        spare = sb("spare", [1, 2, F])
        half_started = sem("half_started")
        stats_made = sem("stats_made")
        work = ctx.enter_context(ExitStack())
        rec = sb("rec", [P, 2, HALF, REC])
        recs = sb("recs", [P, 2, HALF, REC_S])
        gathered = sb("gathered", [P, BODY, ROW])
        onehot = sb("onehot", [P, BODY, P])
        loop = [0]

        def free_rings(pe, v):
            if pe is not None and loop[0] == 0:
                pe.sem_inc(tile_summed, BODY)
            if v is not None and loop[0] == 0:
                v.sem_inc(tile_added, SUM_BANKS)

        NH = NT // HALF
        turns_rec, turns_row = [0], [0]

        class Half:

            def __init__(self, i, n):
                self.i, self.n, self.parity = i, n, n % 2

            def __add__(self, k):
                return Half(self.i, self.n + k)

            def times(self, k, c=0):
                return self.n * k + c if self.i is None else self.i * (2 * k) + (self.n * k + c)

            def turns(self, before=0):
                return self.times(8, 16 * (before + 1) - 8 * self.parity)

        def halves(eng, start, stop, body):
            pairs = (stop - start) // 2
            with eng.Fori(0, pairs) as i:
                for k in range(2):
                    body(Half(i, start + k))
            if (stop - start) % 2:
                body(Half(None, stop - 1))

        def load_records(sp, table, width, ring):
            view = table.rearrange("(p t) w -> p t w", t=NT)
            base = loop[0] * NT
            with sp.Fori(0, ITERS) as i:
                for h in range(2):
                    sp.wait_ge(tile_summed, i * BODY + (base + h * HALF + HALF))
                    sp.dma_start(ring[:, h, :, :], view[:, ds(i * BODY + h * HALF, HALF), :]).then_inc(rec_loaded[h], 16)

        def gather_rows(pool, table, width, ring):
            base = loop[0] * NT
            with pool.Fori(0, ITERS) as i:
                for h in range(2):
                    pool.wait_ge(rec_loaded[h], i * 16 + (turns_rec[0] + 1) * 16)
                    pool.wait_ge(tile_summed, i * BODY + (base + h * HALF + HALF))
                    pool.sem_inc(half_started, 1)
                    for u in range(HALF):
                        slot = h * HALF + u
                        pool.indirect_dma_start(
                            gathered[:, slot, 0:width], None, table,
                            bass.IndirectOffsetOnAxis(ap=ring[:, h, u, COL_INDEX:COL_INDEX + 1].bitcast(i32), axis=0),
                        ).then_inc(row_here[slot], 16)

        def tile_numbers(eng, regs, table, at):
            eng.load(regs, table[0:1, ds(at, HALF)])
            return [eng.snap(r, min_val=0, max_val=TILES - 1) for r in regs]

        def sum_layer(rec_table, rec_w, ring, tile_of, x_table, extra):
            base = loop[0] * NT
            at = EXTRA - (extra[1] - extra[0]) if extra else FEAT
            end = FEAT + F
            width = end - at

            with nc.Block() as block:

                @block.sync
                def _(sp):
                    load_records(sp, rec_table, rec_w, ring)

                @block.gpsimd
                def _(pool):
                    gather_rows(pool, x_table, F, ring)

                @block.vector
                def _(v):
                    free_rings(None, v)
                    regs = [v.alloc_register(f"v{loop[0]}_{u}") for u in range(HALF)]
                    with v.Fori(0, ITERS) as i:
                        for h in range(2):
                            nodes = tile_numbers(v, regs, tile_of, i * BODY + h * HALF)
                            v.wait_ge(rec_loaded[h], i * 16 + (turns_rec[0] + 1) * 16)

                            def make_onehot(u):
                                s = h * HALF + u
                                v.wait_ge(tile_summed, i * BODY + (base + s + 1 + BODY - ONEHOTS))
                                v.tensor_scalar(onehot[:, s % ONEHOTS, :], iota_row[:], ring[:, h, u, COL_LOCAL:COL_LOCAL + 1],
                                                None, ALU.is_equal).then_inc(onehot_ready, 1)

                            def add(u):
                                s = h * HALF + u
                                v.wait_ge(tile_summed, i * BODY + (base + s + 1 + BODY))
                                v.wait_ge(tile_added, i * BODY + (base + s + SUM_BANKS))
                                to = sums[:, ds(nodes[u], 1), at:end].rearrange("p a w -> p (a w)")
                                v.tensor_tensor(to, psum[:, s % SUM_BANKS, 0:width], to, ALU.add).then_inc(tile_added, 1)

                            for u in range(3):
                                make_onehot(u)
                            for u in range(HALF):
                                if u + 3 < HALF:
                                    make_onehot(u + 3)
                                add(u)
                    for r in regs:
                        v.free_register(r)

                @block.tensor
                def _(pe):
                    free_rings(pe, None)
                    with pe.Fori(0, ITERS) as i:
                        for s in range(BODY):
                            h, u, bank = s // HALF, s % HALF, s % SUM_BANKS
                            pe.wait_ge(onehot_ready, i * BODY + (base + s + 1))
                            pe.wait_ge(tile_added, i * BODY + (base + s + 1))
                            if extra:
                                pe.matmul(psum[:, bank, 0:width - F], onehot[:, s % ONEHOTS, :], ring[:, h, u, extra[0]:extra[1]],
                                          start=True, stop=True)
                            pe.wait_ge(row_here[s], i * 16 + (turns_row[0] + 1) * 16)
                            pe.matmul(psum[:, bank, width - F:width], onehot[:, s % ONEHOTS, :], gathered[:, s, 0:F],
                                      start=True, stop=True).then_inc(tile_summed, 1)
            loop[0] += 1
            turns_rec[0] += ITERS
            turns_row[0] += ITERS

        def clear_sums(lo, hi):
            with nc.Block() as block:
                @block.vector
                def _(v):
                    v.memset(sums[:, :, lo:hi], 0.0).then_inc(cleared, 1)

        phase = [0]

        def feats(g):
            return sums[:, ds(g * GROUP, GROUP), FEAT:FEAT + F]

        def mlp_phase(we, w1, b1, w2, b2, hidden, extra_out=None, scale=None):
            k = phase[0]
            phase[0] += 1
            s_stage, s_ext, s_extc, s_agg, s_aggc, s_h, s_hc, s_o, s_oc = (sem(f"m{k}_{n}") for n in (
                "staged", "extras_turned", "extras_copied", "sums_turned", "sums_copied", "hidden", "hidden_copied", "outs", "outs_copied"))
            with ExitStack() as scope:
                stage = sb(f"m{k}_stage", [P, GROUP, SUM_W], f32, scope)
                ext = sb(f"m{k}_ext", [EXTRA, GROUP_W], f32, scope)
                agg = sb(f"m{k}_agg", [P, GROUP_W], f32, scope)
                hid = sb(f"m{k}_hid", [P, max(hidden, 1), GROUP_W], f32, scope)
                with nc.Block() as block:

                    @block.vector
                    def _(v):
                        v.sem_inc(s_agg, 1)
                        with v.Fori(0, GROUPS) as g:
                            v.wait_ge(s_agg, g + 1)
                            v.tensor_copy(stage[:], sums[:, ds(g * GROUP, GROUP), :]).then_inc(s_stage, 1)
                            v.wait_ge(s_ext, g + 1)
                            v.tensor_copy(ext[:], psum[0:EXTRA, 0, :]).then_inc(s_extc, 1)
                            v.wait_ge(s_agg, g + 2)
                            v.tensor_copy(agg[:], psum[:, 1, :]).then_inc(s_aggc, 1)

                    @block.scalar
                    def _(act):
                        wide_psum = psum[:, 4, :].rearrange("p (j f) -> p j f", j=GROUP)
                        with act.Fori(0, GROUPS) as g:
                            for j in range(hidden):
                                act.wait_ge(s_h, g * hidden + (j + 1))
                                act.activation(hid[:, j, :], psum[:, 2 + j, :], ACT.Relu, bias=b1[:, j:j + 1]).then_inc(s_hc, 1)
                            act.wait_ge(s_o, g + 1)
                            if hidden:
                                act.activation(feats(g), wide_psum, ACT.Identity, bias=b2).then_inc(s_oc, 1)
                            else:
                                act.activation(feats(g), wide_psum, ACT.Copy, scale=scale).then_inc(s_oc, 1)

                    @block.tensor
                    def _(pe):
                        pe.sem_inc(s_oc, 1)
                        with pe.Fori(0, GROUPS) as g:
                            pe.wait_ge(s_stage, g + 1)
                            for j in range(GROUP):
                                last = pe.transpose(psum[0:EXTRA, 0, j * P:(j + 1) * P], stage[:, j, 0:EXTRA], ident[:])
                            last.then_inc(s_ext, 1)
                            pe.wait_ge(s_extc, g + 1)
                            for j in range(GROUP):
                                last = pe.matmul(psum[:, 1, j * P:(j + 1) * P], stage[:, j, FEAT:FEAT + F], ident[:],
                                                 start=j == 0, stop=not hidden and j == GROUP - 1)
                            if hidden:
                                last = pe.matmul(psum[:, 1, :], we[:], ext[:], start=False, stop=True)
                            last.then_inc(s_agg, 1)
                            pe.wait_ge(s_aggc, g + 1)
                            for j in range(hidden):
                                pe.matmul(psum[:, 2 + j, :], w1[:, j * F:(j + 1) * F], agg[:], start=True, stop=True).then_inc(s_h, 1)
                            pe.wait_ge(s_oc, g + 1)
                            if hidden:
                                for j in range(hidden):
                                    pe.wait_ge(s_hc, g * hidden + (j + 1))
                                    last = pe.matmul(psum[:, 4, :], w2[:, j, :], hid[:, j, :], start=j == 0, stop=j == hidden - 1)
                            else:
                                pe.matmul(psum[:, 4, :], w2[:], agg[:], start=True, stop=False)
                                last = pe.matmul(psum[:, 4, :], extra_out[:], ext[:], start=False, stop=True)
                            last.then_inc(s_o, 1)

        def bn_phase():
            whole, rest_n = N // P, N % P
            chunks = [(c, min(GROUP, whole - c), P) for c in range(0, whole, GROUP)] + [(whole, 1, rest_n)] * (rest_n > 0)
            steps, rooted = sem("bn_steps"), sem("bn_rooted")
            with ExitStack() as scope:
                stats = sb("bn_stats", [P, len(chunks), 6], f32, scope)
                mv = sb("bn_mv", [P, 4], f32, scope)
                with nc.Block() as block:

                    @block.vector
                    def _(v):
                        for n, (c, k, w) in enumerate(chunks):
                            v.bn_stats(stats[:, n, :], sums[:, c:c + k, FEAT:FEAT + w]).then_inc(steps, 1)
                        n = [len(chunks)]
                        v.wait_ge(steps, n[0])

                        def link(ins):
                            n[0] += 1
                            ins.then_inc(steps, 1)
                            v.wait_ge(steps, n[0])

                        link(v.bn_aggr(mv[:, 0:2], stats[:].rearrange("p a b -> p (a b)")))
                        v.wait_ge(rooted, 1)
                        link(v.reciprocal(mv[:, 3:4], mv[:, 2:3]))
                        link(v.tensor_mul(bn_scale, mv[:, 3:4], gamma_0))
                        link(v.tensor_mul(mv[:, 0:1], mv[:, 0:1], bn_scale))
                        link(v.tensor_sub(bn_shift, beta_0, mv[:, 0:1]))

                    @block.scalar
                    def _(act):
                        act.wait_ge(steps, len(chunks) + 1)
                        act.activation(mv[:, 2:3], mv[:, 1:2], ACT.Sqrt, bias=eps[:]).then_inc(rooted, 1)

        def norm_rows(v, link, src, dst, stats, mv, root_in, root_out, n_in, n_out):
            for j in range(GROUP):
                last = v.bn_stats(stats[:, j, :], src[:, j, :])
            link(last)
            v.sem_inc(stats_made, 1)
            for j in range(GROUP):
                last = v.bn_aggr(mv[:, j, 0:2], stats[:, j, :])
            last.then_inc(root_in, 1)
            v.wait_ge(root_out, n_out)
            link(v.reciprocal(mv[:, :, 3:4], mv[:, :, 2:3]))
            for j in range(GROUP):
                last = v.tensor_scalar(dst[:, j, :], src[:, j, :], mv[:, j, 0:1], mv[:, j, 3:4], ALU.subtract, ALU.mult)
            return last

        def store_group(sp, table, g, tile, done):
            whole = table[0:table.shape[0] // GROUP_W * GROUP_W, :]
            sp.dma_start(whole.rearrange("(t p) f -> p t f", p=P)[:, ds(g * GROUP, GROUP), :], tile).then_inc(done, 16)

        def prime(eng, done, n=1):
            for j in range(n):
                eng.dma_start(spare[0:1, j, :], t["x"][0:1, :]).then_inc(done, 16)

        def finish_phase(scale, shift, x_old, x_new, last_layer=False):
            k = phase[0]
            phase[0] += 1
            s_y, s_turned, s_x, s_chain, s_var, s_root, s_new, s_st = (sem(f"f{k}_{n}") for n in (
                "affine", "turned", "x_loaded", "steps", "variances", "roots", "normed", "stored"))
            with ExitStack() as scope:
                yt = sb(f"f{k}_yt", [P, GROUP, P], f32, scope)
                xo = sb(f"f{k}_x", [P, GROUP, F], f32, scope)
                zz = sb(f"f{k}_z", [P, GROUP, F], f32, scope)
                xn = sb(f"f{k}_new", [P, GROUP, F], f32, scope)
                stats = sb(f"f{k}_stats", [P, GROUP, 6], f32, scope)
                mv = sb(f"f{k}_mv", [P, GROUP, 4], f32, scope)
                with nc.Block() as block:

                    @block.sync
                    def _(sp):
                        view = x_old.rearrange("(t p) f -> p t f", p=P)
                        sp.sem_inc(s_new, 1)
                        with sp.Fori(0, GROUPS) as g:
                            sp.wait_ge(s_new, g + 1)
                            sp.dma_start(xo[:], view[:, ds(g * GROUP, GROUP), :]).then_inc(s_x, 16)

                    @block.scalar
                    def _(act):
                        act.sem_inc(s_turned, 1)
                        prime(act, s_st, 1)
                        with act.Fori(0, GROUPS if not last_layer else GROUPS - 1) as g:
                            act.wait_ge(s_turned, g + 1)
                            act.activation(yt[:], feats(g), ACT.Identity, bias=shift, scale=scale).then_inc(s_y, 1)
                            act.wait_ge(s_var, g + 1)
                            act.activation(mv[:, :, 2:3], mv[:, :, 1:2], ACT.Sqrt, bias=eps[:]).then_inc(s_root, 1)
                            act.wait_ge(s_new, g + 2)
                            store_group(act, x_new, g, xn[:], s_st)
                        if last_layer:
                            g = GROUPS - 1
                            act.wait_ge(s_turned, g + 1)
                            act.activation(yt[:], feats(g), ACT.Identity, bias=shift, scale=scale).then_inc(s_y, 1)
                            act.wait_ge(s_var, g + 1)
                            act.activation(mv[:, :, 2:3], mv[:, :, 1:2], ACT.Sqrt, bias=eps[:]).then_inc(s_root, 1)
                            act.wait_ge(s_new, g + 2)
                            n = 0
                            for j in range(GROUP):
                                r0 = g * GROUP_W + j * P
                                rows_here = min(P, N - r0)
                                if rows_here > 0:
                                    act.dma_start(x_new[r0:r0 + rows_here, :], xn[0:rows_here, j, :]).then_inc(s_st, 16)
                                    n += 1
                            act.wait_ge(s_st, 16 * (GROUPS + n))
                        else:
                            act.wait_ge(s_st, 16 * (GROUPS + 1))

                    @block.tensor
                    def _(pe):
                        pe.sem_inc(s_chain, 1)
                        with pe.Fori(0, GROUPS) as g:
                            pe.wait_ge(s_y, g + 1)
                            pe.wait_ge(s_chain, g * 3 + 1)
                            for j in range(GROUP):
                                last = pe.transpose(psum[:, 0, j * P:(j + 1) * P], yt[:, j, :], ident[:])
                            last.then_inc(s_turned, 1)

                    @block.vector
                    def _(v):
                        with v.Fori(0, GROUPS) as g:
                            n = [0]

                            def link(ins):
                                n[0] += 1
                                ins.then_inc(s_chain, 1)
                                v.wait_ge(s_chain, g * 3 + (n[0] + 1))

                            v.wait_ge(s_turned, g + 2)
                            v.wait_ge(s_x, g * 16 + 16)
                            link(v.tensor_tensor(zz[:], psum[:, 0, :].rearrange("p (j f) -> p j f", j=GROUP), xo[:], ALU.add))
                            v.wait_ge(s_st, g * 16 + 16)
                            norm_rows(v, link, zz, xn, stats, mv, s_var, s_root, g + 1, g + 1).then_inc(s_new, 1)
                            assert n[0] == 3

        def project_phase(x_table):
            k = phase[0]
            phase[0] += 1
            s_x, s_t, s_tc, s_h, s_hc, s_st, s_ad = (sem(f"p{k}_{n}") for n in (
                "x_loaded", "turned", "turned_copied", "rows", "rows_copied", "stored", "dst_copied"))
            with ExitStack() as scope:
                xo = sb(f"p{k}_x", [P, GROUP, F], f32, scope)
                xt = sb(f"p{k}_xt", [P, GROUP, P], f32, scope)
                hr = sb(f"p{k}_rows", [P, GROUP, ROW], f32, scope)
                WP = 256
                with nc.Block() as block:

                    @block.sync
                    def _(sp):
                        sp.sem_inc(s_t, 1)
                        view = x_table.rearrange("(t p) f -> p t f", p=P)
                        with sp.Fori(0, GROUPS) as g:
                            sp.wait_ge(s_t, g + 1)
                            sp.dma_start(xo[:], view[:, ds(g * GROUP, GROUP), :]).then_inc(s_x, 16)

                    @block.tensor
                    def _(pe):
                        pe.sem_inc(s_hc, 1)
                        pe.sem_inc(s_ad, 1)
                        with pe.Fori(0, GROUPS) as g:
                            pe.wait_ge(s_x, g * 16 + 16)
                            for j in range(GROUP):
                                last = pe.transpose(psum[:, 0, j * P:(j + 1) * P], xo[:, j, :], ident[:])
                            last.then_inc(s_t, 1)
                            pe.wait_ge(s_tc, g + 1)
                            pe.wait_ge(s_hc, g + 1)
                            pe.wait_ge(s_ad, g + 1)
                            for j in range(GROUP):
                                last = pe.matmul(psum[:, 2 + j // 2, (j % 2) * WP:(j % 2) * WP + ROW + HEADS], xt[:, j, :], w_gat[:], start=True, stop=True)
                            last.then_inc(s_h, 1)

                    @block.scalar
                    def _(act):
                        prime(act, s_st, 1)
                        hv = psum[:, 2:4, :].rearrange("p a (b w) -> p (a b) w", b=2)
                        hd = hrow.rearrange("(t p) f -> p t f", p=P)
                        with act.Fori(0, GROUPS) as g:
                            act.wait_ge(s_t, g + 2)
                            act.copy(xt[:].rearrange("p j f -> p (j f)"), psum[:, 0, :]).then_inc(s_tc, 1)
                            act.wait_ge(s_h, g + 1)
                            act.wait_ge(s_st, g * 16 + 16)
                            act.copy(hr[:], hv[:, :, 0:ROW]).then_inc(s_hc, 1)
                            act.wait_ge(s_hc, g + 2)
                            act.dma_start(hd[:, ds(g * GROUP, GROUP), :], hr[:]).then_inc(s_st, 16)
                        act.wait_ge(s_st, GROUPS * 16 + 16)

                    @block.vector
                    def _(v):
                        hv = psum[:, 2:4, :].rearrange("p a (b w) -> p (a b) w", b=2)
                        v.memset(sums[:, :, FEAT:], 0.0).then_inc(cleared, 1)
                        with v.Fori(0, GROUPS) as g:
                            v.wait_ge(s_hc, g + 2)
                            v.tensor_copy(dst_max[:, ds(g * GROUP, GROUP), 0:HEADS], hv[:, :, ROW:ROW + HEADS])
                            v.tensor_copy(dst_max[:, ds(g * GROUP, GROUP), HEADS:], hv[:, :, F:ROW]).then_inc(s_ad, 1)

        def max_phase():
            QUADS = HALF // 4
            UNITS = HEADS // 2
            PARTS = P
            PREP = 16
            LOC = 3 * HEADS
            s_split, s_turn, s_turnc, s_prod, s_red, s_max, s_steps = (sem(f"x_{n}") for n in (
                "rows_split", "turned", "turned_copied", "products", "reduced", "maxima", "steps"))
            s_apart = sem("x_apart_turned")
            s_spill = [sem(f"x_rows_kept{k}") for k in range(2)]
            rec0, row0 = turns_rec[0], turns_row[0]
            with ExitStack() as scope:
                parts = sb("x_parts", [P, 2, HALF, PARTS], bf16, scope)
                rest = sb("x_rest", [P, HALF, HEADS], f32, scope)
                square = sb("x_square", [P, HALF, 1], f32, scope)
                turned = sb("x_turned", [PARTS, 2 * QUADS, GROUP_W], bf16, scope)
                select = sb("x_select", [PARTS, HEADS, P], bf16, scope)
                apart_n = sb("x_apart_n", [P, PARTS], bf16, scope)
                apart = sb("x_apart", [PARTS, P], bf16, scope)
                node_sq = sb("x_node_sq", [P, 4], f32, scope)
                sel_i = sb("x_sel_i", [P, 2], i32, scope)
                sel_f = sb("x_sel_f", [P, 1], f32, scope)
                sel_c = sb("x_sel_c", [P, HEADS], f32, scope)
                real = sb("x_real", [P, 1], f32, scope)
                big = sb("x_big", [P, 2, QUADS, HEADS, 4], f32, scope)
                psum_b = psum[:].bitcast(bf16)
                with nc.Block() as block:
                    @block.vector
                    def _(v):
                        n = [0]

                        def link(ins):
                            n[0] += 1
                            ins.then_inc(s_steps, 1)
                            v.wait_ge(s_steps, n[0])

                        link(v.memset(parts[:], 0.0))
                        link(v.memset(parts[:, :, :, LOC + 3:LOC + 5], 1.0))
                        link(v.tensor_copy(sel_i[:, 0:1], iota_part[:]))
                        link(v.tensor_single_scalar(sel_i[:, 1:2], sel_i[:, 0:1], HEADS - 1, ALU.bitwise_and))
                        link(v.tensor_copy(sel_f[:], sel_i[:, 1:2]))
                        link(v.tensor_single_scalar(real[:], iota_part[:], float(LOC), ALU.is_lt))
                        link(v.tensor_scalar(sel_c[:], iota_row[:, 0:HEADS], sel_f[:], real[:], ALU.is_equal, ALU.mult))
                        link(v.tensor_copy(select[:], sel_c[0:PARTS, :].unsqueeze(2).to_broadcast([PARTS, HEADS, P])))
                        link(v.memset(apart_n[:], 0.0))
                        link(v.tensor_mul(node_sq[:, 0:1], iota_part[:], iota_part[:]))
                        link(v.tensor_single_scalar(node_sq[:, 0:1], node_sq[:, 0:1], -BIG, ALU.mult))
                        link(v.tensor_single_scalar(apart_n[:, LOC:LOC + 1], iota_part[:], 2.0 * BIG, ALU.mult))
                        link(v.memset(apart_n[:, LOC + 1:LOC + 3], -BIG))
                        link(v.tensor_copy(apart_n[:, LOC + 3:LOC + 4], node_sq[:, 0:1]))
                        link(v.tensor_sub(apart_n[:, LOC + 4:LOC + 5], node_sq[:, 0:1], apart_n[:, LOC + 3:LOC + 4]))
                        v.sem_inc(s_split, 2)
                        v.wait_ge(s_apart, 1)
                        link(v.tensor_copy(apart[:], psum_b[0:PARTS, 6, 0:P]))
                        assert n[0] == PREP
                        v.sem_inc(s_red, 2)

                    @block.tensor
                    def _(pe):
                        pe.wait_ge(s_split, 2)
                        pe.wait_ge(s_steps, PREP - 1)
                        pe.transpose(psum_b[0:PARTS, 6, 0:P], apart_n[:], ident_b[:]).then_inc(s_apart, 1)
                        pe.sem_inc(s_turn, 2 * QUADS)
                        pe.sem_inc(s_prod, 2 * QUADS * UNITS)

                    @block.scalar
                    def _(act):
                        act.sem_inc(s_turnc, 2)

                with nc.Block() as block:

                    @block.sync
                    def _(sp):
                        records = rec_d.rearrange("(p t) w -> p t w", t=NT)

                        def load(H):
                            sp.wait_ge(s_split, H.times(1, 1))
                            sp.dma_start(rec[:, H.parity, :, :], records[:, ds(H.times(HALF), HALF), :]).then_inc(rec_loaded[H.parity], 16)

                        def keep(H):
                            at = H.parity * HALF
                            for u in range(HALF):
                                sp.wait_ge(row_here[at + u], H.turns(row0))
                            sp.dma_start(gathered_rows[:, ds(H.times(HALF), HALF), :], gathered[:, at:at + HALF, :]).then_inc(s_spill[H.parity], 16)

                        load(Half(None, 0))
                        load(Half(None, 1))

                        def both(H):
                            keep(H)
                            load(H + 2)

                        halves(sp, 0, NH - 2, both)
                        keep(Half(None, NH - 2))
                        keep(Half(None, NH - 1))
                        for k in range(2):
                            sp.wait_ge(s_spill[k], NH // 2 * 16)

                    @block.gpsimd
                    def _(pool):
                        def gather(H, first=False):
                            pool.wait_ge(rec_loaded[H.parity], H.turns(rec0))
                            pool.wait_ge(s_split, H.times(1, 1))
                            if not first:
                                pool.wait_ge(s_spill[H.parity], H.turns(-1))
                            pool.sem_inc(half_started, 1)
                            for u in range(HALF):
                                pool.indirect_dma_start(
                                    gathered[:, H.parity * HALF + u, :], None, hrow,
                                    bass.IndirectOffsetOnAxis(ap=rec[:, H.parity, u, COL_INDEX:COL_INDEX + 1].bitcast(i32), axis=0),
                                ).then_inc(row_here[H.parity * HALF + u], 16)

                        gather(Half(None, 0), True)
                        gather(Half(None, 1), True)
                        halves(pool, 2, NH, gather)

                    @block.scalar
                    def _(act):
                        def copy_turned(H):
                            for q in range(QUADS):
                                act.wait_ge(s_turn, H.times(QUADS, q + 1 + 2 * QUADS))
                                act.wait_ge(s_prod, H.times(QUADS * UNITS, (q + 1) * UNITS))
                                act.copy(turned[:, H.parity * QUADS + q, :], psum_b[0:PARTS, 6 + q % 2, 0:GROUP_W]).then_inc(s_turnc, 1)

                        halves(act, 0, NH, copy_turned)

                    @block.tensor
                    def _(pe):
                        def turn(H):
                            pe.wait_ge(s_split, H.times(1, 3))
                            for q in range(QUADS):
                                pe.wait_ge(s_turnc, H.times(QUADS, q + 1))
                                for j in range(4):
                                    last = pe.transpose(psum_b[0:PARTS, 6 + q % 2, j * P:(j + 1) * P], parts[:, H.parity, 4 * q + j, :], ident_b[:])
                                last.then_inc(s_turn, 1)

                        def products(H, q):
                            pe.wait_ge(s_turnc, H.times(QUADS, q + 3))
                            rows_q = turned[:, H.parity * QUADS + q, :]
                            for u in range(UNITS):
                                pe.wait_ge(s_red, H.times(QUADS * UNITS, q * UNITS + u + 1))
                                b = 2 * (u % 2)
                                for c in range(2):
                                    pe.matmul(psum[:, b + c, :], apart[:], rows_q, start=True, stop=False)
                                    last = pe.matmul(psum[:, b + c, :], select[:, 2 * u + c, :], rows_q, start=False, stop=True)
                                last.then_inc(s_prod, 1)

                        turn(Half(None, 0))

                        def body(H):
                            products(H, 0)
                            products(H, 1)
                            turn(H + 1)
                            products(H, 2)
                            products(H, 3)

                        halves(pe, 0, NH - 1, body)
                        for q in range(QUADS):
                            products(Half(None, NH - 1), q)

                    @block.vector
                    def _(v):
                        regs = [v.alloc_register(f"x{u}") for u in range(HALF)]
                        SPLIT = 9

                        def split(H):
                            n = [0]

                            def link(ins):
                                n[0] += 1
                                ins.then_inc(s_steps, 1)
                                v.wait_ge(s_steps, H.times(SPLIT, PREP + n[0]))

                            v.wait_ge(rec_loaded[H.parity], H.turns(rec0))
                            for u in range(HALF):
                                v.wait_ge(row_here[H.parity * HALF + u], H.turns(row0))
                            v.wait_ge(s_turn, H.times(QUADS, QUADS))
                            of = gathered[:, H.parity * HALF:(H.parity + 1) * HALF, F:ROW]
                            loc = rec[:, H.parity, :, COL_LOCAL:COL_LOCAL + 1]
                            part = lambda m: parts[:, H.parity, :, m * HEADS:(m + 1) * HEADS]
                            col = lambda m: parts[:, H.parity, :, LOC + m:LOC + m + 1]
                            link(v.tensor_copy(part(0), of))
                            link(v.tensor_sub(rest[:], of, part(0)))
                            link(v.tensor_copy(part(1), rest[:]))
                            link(v.tensor_sub(rest[:], rest[:], part(1)))
                            link(v.tensor_copy(part(2), rest[:]))
                            link(v.tensor_copy(col(0), loc))
                            link(v.tensor_mul(square[:], loc, loc))
                            link(v.tensor_copy(col(1), square[:]))
                            link(v.tensor_sub(col(2), square[:], col(1)))
                            v.sem_inc(s_split, 1)
                            assert n[0] == SPLIT

                        def take(H, nodes, q, t):
                            v.wait_ge(s_max, H.times(HALF, 4 * q + t + 1))
                            to = dst_max[:, ds(nodes[4 * q + t], 1), HEADS:].rearrange("p a w -> p (a w)")
                            v.tensor_tensor(to, big[:, H.parity, q, :, t], to, ALU.max).then_inc(s_max, 1)

                        def reduce(H):
                            nodes = tile_numbers(v, regs, tile_of_d, H.times(HALF))
                            for q in range(QUADS):
                                for u in range(UNITS):
                                    v.wait_ge(s_prod, H.times(QUADS * UNITS, q * UNITS + u + 1 + 2 * QUADS * UNITS))
                                    b = 2 * (u % 2)
                                    v.tensor_reduce(big[:, H.parity, q, 2 * u:2 * u + 2, :], psum[:, b:b + 2, :].rearrange("p a (t e) -> p a t e", t=4),
                                                    AX.X, ALU.max).then_inc(s_red, 1)
                                    if q and u:
                                        take(H, nodes, q - 1, u - 1)
                                        if u == 3:
                                            take(H, nodes, q - 1, 3)
                                    if u == 3:
                                        v.wait_ge(s_red, H.times(QUADS * UNITS, (q + 1) * UNITS + 2))
                            for t in range(4):
                                take(H, nodes, QUADS - 1, t)

                        v.sem_inc(s_max, 1)
                        split(Half(None, 0))

                        def body(H):
                            split(H + 1)
                            reduce(H)

                        halves(v, 0, NH - 1, body)
                        reduce(Half(None, NH - 1))
                        for r in regs:
                            v.free_register(r)
                        v.wait_ge(s_max, NT + 1)
                        c = [NH * SPLIT + PREP]

                        def link(ins):
                            c[0] += 1
                            ins.then_inc(s_steps, 1)
                            v.wait_ge(s_steps, c[0])

                        m = dst_max[:, :, HEADS:]
                        link(v.tensor_add(m, m, dst_max[:, :, 0:HEADS]))
                        link(v.scalar_tensor_tensor(m, m, SLOPE, m, ALU.mult, ALU.max))
            turns_rec[0] += NH // 2
            turns_row[0] += NH // 2

        def attention_phase():
            QUADS = HALF // 4
            s_one, s_turn, s_turnc, s_ad, s_e, s_exp, s_msg, s_sum, s_add, s_steps = (sem(f"a_{n}") for n in (
                "onehots", "turned", "turned_copied", "dst_rows", "scores", "exps", "messages", "summed", "added", "steps"))
            s_rows = [sem(f"a_rows_loaded{k}") for k in range(2)]
            s_scat = [sem(f"a_scattered{k}") for k in range(2)]
            s_taken = sem("a_taken")
            rec0 = turns_rec[0]
            with ExitStack() as scope:
                turned = sb("a_turned", [P, QUADS, 4, P], f32, scope)
                score = sb("a_score", [P, 2, HALF, HEADS], f32, scope)
                msg = sb("a_msg", [P, BODY, ROW], f32, scope)
                to_rec = sb("a_to_rec", [P, 2, CS, REC_S], f32, scope)
                to_addr = sb("a_to_addr", [P, 2, CS], i32, scope)
                spare_a = sb("a_spare", [1, 2, F], f32, scope)
                with nc.Block() as block:

                    @block.sync
                    def _(sp):
                        records = rec_d.rearrange("(p t) w -> p t w", t=NT)

                        def load(H):
                            at = H.parity * HALF
                            sp.wait_ge(s_msg, H.times(QUADS, QUADS))
                            sp.dma_start(rec[:, H.parity, :, :], records[:, ds(H.times(HALF), HALF), :]).then_inc(rec_loaded[H.parity], 16)
                            sp.dma_start(gathered[:, at:at + HALF, :], gathered_rows[:, ds(H.times(HALF), HALF), :]).then_inc(s_rows[H.parity], 16)

                        halves(sp, 0, NH, load)

                    @block.gpsimd
                    def _(pool):
                        for h in range(2):
                            pool.dma_start(spare_a[0:1, h, :], t["x"][0:1, :]).then_inc(s_scat[h], 16)

                        def scatter(h, rows, c, col, before, n_taken):
                            pool.wait_ge(s_scat[h], before)
                            pool.tensor_copy(to_addr[0:rows, h, 0:c], addr_src[0:rows, ds(col, c)]).then_inc(s_taken, 1)
                            pool.tensor_copy(to_rec[0:rows, h, 0:c, :], rec_src[0:rows, ds(col, c), :]).then_inc(s_taken, 1)
                            pool.wait_ge(s_taken, n_taken)
                            pool.sem_inc(half_started, 1)
                            for j in range(c):
                                pool.indirect_dma_start(
                                    rec_s, bass.IndirectOffsetOnAxis(ap=to_addr[0:rows, h, j:j + 1], axis=0),
                                    to_rec[0:rows, h, j, :], None).then_inc(s_scat[h], 16)

                        with pool.Fori(0, SORT_ITERS) as i:
                            for h in range(2):
                                scatter(h, P, CS, i * (2 * CS) + h * CS, i * (CS * 16) + 16, i * 4 + (2 * h + 2))
                        if TAIL:
                            scatter(0, TAIL, 1, COLS, SORT_ITERS * CS * 16 + 16, SORT_ITERS * 4 + 2)
                        pool.wait_ge(s_scat[0], SORT_ITERS * CS * 16 + 16 + (16 if TAIL else 0))
                        pool.wait_ge(s_scat[1], SORT_ITERS * CS * 16 + 16)

                    @block.scalar
                    def _(act):
                        def copy_turned(H):
                            for q in range(QUADS):
                                act.wait_ge(s_turn, H.times(QUADS, q + 1))
                                act.wait_ge(s_ad, H.times(QUADS, q + 1))
                                act.copy(turned[:, q, :, :].rearrange("p a b -> p (a b)"), psum[:, 4 + q % 2, :]).then_inc(s_turnc, 1)

                        def exps(H):
                            at = H.parity * HALF
                            act.wait_ge(s_e, H.times(1, 3))
                            act.wait_ge(s_sum, H.times(HALF, HALF))
                            act.activation(msg[:, at:at + HALF, F:ROW], score[:, H.parity, :, :], ACT.Exp).then_inc(s_exp, 1)

                        copy_turned(Half(None, 0))

                        def body(H):
                            exps(H)
                            copy_turned(H + 1)

                        halves(act, 0, NH - 1, body)
                        exps(Half(None, NH - 1))

                    @block.tensor
                    def _(pe):
                        pe.sem_inc(s_turnc, 2)
                        pe.sem_inc(s_ad, QUADS)
                        pe.sem_inc(s_sum, BODY)
                        regs = [pe.alloc_register(f"pe{u}") for u in range(HALF)]

                        def turn(H):
                            for q in range(QUADS):
                                pe.wait_ge(s_one, H.times(QUADS, q + 1))
                                pe.wait_ge(s_turnc, H.times(QUADS, q + 1))
                                for j in range(4):
                                    last = pe.transpose(psum[:, 4 + q % 2, j * P:(j + 1) * P], onehot[:, H.parity * HALF + 4 * q + j, :], ident[:])
                                last.then_inc(s_turn, 1)

                        def dst_rows(H):
                            nodes = tile_numbers(pe, regs, tile_of_d, H.times(HALF))
                            pe.wait_ge(s_e, H.times(1, 1))
                            for q in range(QUADS):
                                pe.wait_ge(s_turnc, H.times(QUADS, q + 3))
                                for j in range(4):
                                    u = 4 * q + j
                                    last = pe.matmul(psum[:, 6 + H.parity, u * 16:(u + 1) * 16], turned[:, q, j, :],
                                                     dst_max[:, ds(nodes[u], 1), :].rearrange("p a w -> p (a w)"), start=True, stop=True)
                                last.then_inc(s_ad, 1)

                        def sum_tiles(H):
                            for u in range(HALF):
                                if u % 4 == 0:
                                    pe.wait_ge(s_msg, H.times(QUADS, u // 4 + 1 + 2 * QUADS))
                                pe.wait_ge(s_add, H.times(HALF, u + 1))
                                at = H.parity * HALF + u
                                pe.matmul(psum[:, u % SUM_BANKS, 0:ROW], onehot[:, at, :], msg[:, at, :],
                                          start=True, stop=True).then_inc(s_sum, 1)

                        for n in range(2):
                            turn(Half(None, n))
                            dst_rows(Half(None, n))

                        def body(H):
                            sum_tiles(H + -1)
                            turn(H + 1)
                            dst_rows(H + 1)

                        halves(pe, 1, NH - 1, body)
                        sum_tiles(Half(None, NH - 2))
                        sum_tiles(Half(None, NH - 1))
                        for r in regs:
                            pe.free_register(r)

                    @block.vector
                    def _(v):
                        v.sem_inc(s_e, 2)
                        v.sem_inc(s_msg, 2 * QUADS)
                        v.sem_inc(s_add, SUM_BANKS)
                        regs = [v.alloc_register(f"a{u}") for u in range(HALF)]

                        def onehots(H):
                            v.wait_ge(rec_loaded[H.parity], H.turns(rec0))
                            v.wait_ge(s_sum, H.times(HALF, HALF))
                            for u in range(HALF):
                                last = v.tensor_scalar(onehot[:, H.parity * HALF + u, :], iota_row[:], rec[:, H.parity, u, COL_LOCAL:COL_LOCAL + 1],
                                                       None, ALU.is_equal)
                                if u % 4 == 3:
                                    last.then_inc(s_one, 1)

                        def scores(H):
                            at = H.parity * HALF
                            sc = score[:, H.parity, :, :]
                            ad = psum[:, 6 + H.parity, 0:16 * HALF].rearrange("p (a w) -> p a w", a=HALF)
                            n = [0]

                            def link(ins):
                                n[0] += 1
                                ins.then_inc(s_steps, 1)
                                v.wait_ge(s_steps, H.times(3, n[0]))

                            v.wait_ge(s_rows[H.parity], H.turns())
                            v.wait_ge(s_ad, H.times(QUADS, 2 * QUADS))
                            link(v.tensor_tensor(sc, ad[:, :, 0:HEADS], gathered[:, at:at + HALF, F:ROW], ALU.add))
                            link(v.scalar_tensor_tensor(sc, sc, SLOPE, sc, ALU.mult, ALU.max))
                            link(v.tensor_tensor(sc, sc, ad[:, :, HEADS:], ALU.subtract))
                            v.tensor_single_scalar(sc, sc, 0.0, ALU.min).then_inc(s_e, 1)

                        def messages(H):
                            v.wait_ge(s_exp, H.times(1, 1))
                            for q in range(QUADS):
                                at = H.parity * HALF + 4 * q
                                v.tensor_tensor(
                                    msg[:, at:at + 4, 0:F].rearrange("p t (h c) -> p t h c", h=HEADS),
                                    gathered[:, at:at + 4, 0:F].rearrange("p t (h c) -> p t h c", h=HEADS),
                                    msg[:, at:at + 4, F:ROW].unsqueeze(3).to_broadcast([P, 4, HEADS, HEAD_CH]), ALU.mult).then_inc(s_msg, 1)

                        def add(H):
                            nodes = tile_numbers(v, regs, tile_of_d, H.times(HALF))
                            for u in range(HALF):
                                v.wait_ge(s_sum, H.times(HALF, u + 1 + BODY))
                                v.wait_ge(s_add, H.times(HALF, u + SUM_BANKS))
                                to = sums[:, ds(nodes[u], 1), FEAT:].rearrange("p a w -> p (a w)")
                                v.tensor_tensor(to, psum[:, u % SUM_BANKS, 0:ROW], to, ALU.add).then_inc(s_add, 1)

                        onehots(Half(None, 0))
                        scores(Half(None, 0))
                        onehots(Half(None, 1))
                        messages(Half(None, 0))

                        def body(H):
                            add(H + -1)
                            scores(H)
                            onehots(H + 1)
                            messages(H)

                        halves(v, 1, NH - 1, body)
                        add(Half(None, NH - 2))
                        scores(Half(None, NH - 1))
                        messages(Half(None, NH - 1))
                        add(Half(None, NH - 1))
                        for r in regs:
                            v.free_register(r)
            turns_rec[0] += NH // 2

        def attention_finish(x_old, x_new):
            s_x, s_rows, s_chain, s_score, s_self, s_var, s_root, s_min, s_exp, s_new, s_st = (sem(f"g_{n}") for n in (
                "x_loaded", "rows_loaded", "steps", "scores", "self_exps", "variances", "roots", "minima", "exps", "normed", "stored"))
            with ExitStack() as scope:
                xo = sb("g_x", [P, GROUP, F], f32, scope)
                zz = sb("g_z", [P, GROUP, F], f32, scope)
                ee = sb("g_e", [P, GROUP, F], f32, scope)
                xn = sb("g_new", [P, GROUP, F], f32, scope)
                hr = sb("g_rows", [P, GROUP, ROW], f32, scope)
                score = sb("g_score", [P, GROUP, HEADS], f32, scope)
                den = sb("g_den", [P, GROUP, HEADS], f32, scope)
                stats = sb("g_stats", [P, GROUP, 6], f32, scope)
                mv = sb("g_mv", [P, GROUP, 4], f32, scope)
                STEPS = 18
                with nc.Block() as block:

                    @block.sync
                    def _(sp):
                        view = x_old.rearrange("(t p) f -> p t f", p=P)
                        rows_view = hrow.rearrange("(t p) f -> p t f", p=P)
                        sp.sem_inc(s_new, 1)
                        with sp.Fori(0, GROUPS) as g:
                            sp.wait_ge(s_new, g + 1)
                            sp.dma_start(xo[:], view[:, ds(g * GROUP, GROUP), :]).then_inc(s_x, 16)
                            sp.dma_start(hr[:], rows_view[:, ds(g * GROUP, GROUP), :]).then_inc(s_rows, 16)

                    @block.scalar
                    def _(act):
                        prime(act, s_st, 1)
                        with act.Fori(0, GROUPS) as g:
                            act.wait_ge(s_score, g + 1)
                            act.activation(score[:], score[:], ACT.Exp).then_inc(s_self, 1)
                            for r in range(2):
                                act.wait_ge(s_var, g * 2 + (r + 1))
                                act.activation(mv[:, :, 2:3], mv[:, :, 1:2], ACT.Sqrt, bias=eps[:]).then_inc(s_root, 1)
                                if r == 0:
                                    act.wait_ge(s_min, g + 1)
                                    act.activation(ee[:], ee[:], ACT.Exp).then_inc(s_exp, 1)
                            act.wait_ge(s_new, g + 2)
                            store_group(act, x_new, g, xn[:], s_st)
                        act.wait_ge(s_st, 16 * (GROUPS + 1))

                    @block.vector
                    def _(v):
                        wide = lambda a: a.unsqueeze(1).to_broadcast([P, GROUP, F])
                        with v.Fori(0, GROUPS) as g:
                            n = [0]

                            def link(ins):
                                n[0] += 1
                                ins.then_inc(s_chain, 1)
                                v.wait_ge(s_chain, g * STEPS + n[0])

                            here = lambda m: m[:, ds(g * GROUP, GROUP), :]
                            v.wait_ge(s_rows, g * 16 + 16)
                            link(v.tensor_tensor(score[:], hr[:, :, F:ROW], here(dst_max)[:, :, 0:HEADS], ALU.add))
                            link(v.scalar_tensor_tensor(score[:], score[:], SLOPE, score[:], ALU.mult, ALU.max))
                            v.tensor_tensor(score[:], score[:], here(dst_max)[:, :, HEADS:], ALU.subtract).then_inc(s_score, 1)
                            v.wait_ge(s_self, g + 1)
                            link(v.tensor_tensor(den[:], here(sums)[:, :, DEN:], score[:], ALU.add))
                            link(v.reciprocal(den[:], den[:]))
                            blocks = lambda m, j: m[:, j, 0:F].rearrange("p (h c) -> p h c", h=HEADS)
                            each = lambda m, j: m[:, j, :].unsqueeze(2).to_broadcast([P, HEADS, HEAD_CH])
                            for j in range(GROUP):
                                last = v.tensor_tensor(blocks(zz, j), blocks(hr, j), each(score, j), ALU.mult)
                            link(last)
                            link(v.tensor_tensor(zz[:], zz[:], here(sums)[:, :, FEAT:FEAT + F], ALU.add))
                            for j in range(GROUP):
                                last = v.tensor_tensor(blocks(zz, j), blocks(zz, j), each(den, j), ALU.mult)
                            link(last)
                            link(v.tensor_tensor(zz[:], zz[:], wide(bias_1), ALU.add))
                            link(norm_rows(v, link, zz, zz, stats, mv, s_var, s_root, 0, g * 2 + 1))
                            link(v.tensor_tensor(zz[:], zz[:], wide(gamma_1), ALU.mult))
                            link(v.tensor_tensor(zz[:], zz[:], wide(beta_1), ALU.add))
                            v.tensor_single_scalar(ee[:], zz[:], 0.0, ALU.min).then_inc(s_min, 1)
                            v.wait_ge(s_min, g + 1)
                            link(v.tensor_single_scalar(zz[:], zz[:], 0.0, ALU.max))
                            v.wait_ge(s_exp, g + 1)
                            link(v.scalar_tensor_tensor(zz[:], ee[:], -1.0, zz[:], ALU.add, ALU.add))
                            v.wait_ge(s_x, g * 16 + 16)
                            link(v.tensor_tensor(zz[:], zz[:], xo[:], ALU.add))
                            v.wait_ge(s_st, g * 16 + 16)
                            norm_rows(v, link, zz, xn, stats, mv, s_var, s_root, 0, g * 2 + 2).then_inc(s_new, 1)
                            assert n[0] == STEPS, n

        attrs = (COL_ATTR, REC)
        sum_layer(rec_d, REC, rec, tile_of_d, xs[0], attrs)
        mlp_phase(we_0, w1_0, b1_0, w2_0, b2_0, 2)
        bn_phase()
        finish_phase(bn_scale, bn_shift, xs[0], xs[1])
        project_phase(xs[1])
        max_phase()
        attention_phase()
        attention_finish(xs[1], xs[2])
        clear_sums(FEAT, DEN)
        sum_layer(rec_d, REC, rec, tile_of_d, xs[2], None)
        mlp_phase(we_2, w1_2, b1_2, w2_2, b2_2, 1)
        finish_phase(one_col, zero_col, xs[2], xs[3])
        clear_sums(0, DEN)
        sum_layer(rec_s, REC_S, recs, tile_of_s, xs[3], (2, 3))
        mlp_phase(None, None, None, w_3t, None, 0, extra_out=b_3, scale=agg_w)
        finish_phase(one_col, zero_col, xs[3], out, last_layer=True)


_INS = ["x", "src", "dst", "edge_attr_16", "edge_attr_3", "edge_attr_6",
        "L0_gnn_We0", "L0_gnn_be0", "L0_gnn_We1", "L0_gnn_be1", "L0_gnn_W1", "L0_gnn_b1", "L0_gnn_W2", "L0_gnn_b2",
        "L0_gnn_gamma", "L0_gnn_beta", "L1_gnn_W", "L1_gnn_att_src", "L1_gnn_att_dst", "L1_gnn_bias",
        "L1_gnn_ln_gamma", "L1_gnn_ln_beta", "L2_gnn_We", "L2_gnn_be", "L2_gnn_W1", "L2_gnn_b1", "L2_gnn_W2",
        "L2_gnn_b2", "L3_gnn_W", "L3_gnn_b", "L3_gnn_agg_weight"]


def kernel(**inputs):
    import numpy as _np
    import concourse.bacc as _bacc
    from concourse import mybir as _mybir
    from concourse.bass_utils import run_bass_kernel_spmd as _run

    nc = _bacc.Bacc("TRN2", target_bir_lowering=False, num_devices=1)
    arrays, t = {}, {}
    for name in _INS:
        a = _np.ascontiguousarray(inputs[name])
        arrays[f"in_{name}"] = a
        t[name] = nc.dram_tensor(f"in_{name}", a.shape, _mybir.dt.from_np(a.dtype), kind="ExternalInput").ap()
    n, f = inputs["x"].shape
    out = nc.dram_tensor("out_0", (n, f), _mybir.dt.float32, kind="ExternalOutput").ap()
    gnn_kernel(nc, t, out)
    r = _run(nc, [arrays], core_ids=[0])
    return r.results[0]["out_0"]
```

```python
from contextlib import ExitStack

import concourse.bass as bass
from concourse import mybir

P = 128
F = 128
HEADS = 8
HEAD_CH = F // HEADS
HALF = 16
BODY = 2 * HALF
GROUP = 4
GROUP_W = GROUP * P
COL_LOCAL, COL_INDEX, COL_ATTR, COL_PACK = 0, 1, 2, 28
REC = COL_PACK + 2
EXTRA = COL_PACK - COL_ATTR
REC_S = 4
SUM_W = EXTRA + F + HEADS
FEAT = EXTRA
DEN = EXTRA + F
ROW = F + HEADS
PARTS_A = 3
ROW_G = ROW + PARTS_A * HEADS // 2
ONEHOTS = 8
SUM_BANKS = 4
BIG = float(2.0 ** 100)
NORM_EPS = 1e-5
SLOPE = 0.2


def _sizes(n_nodes, n_edges):
    s = {}
    s["tiles"] = -(-n_nodes // P)
    s["groups"] = -(-s["tiles"] // GROUP)
    s["padded_tiles"] = s["groups"] * GROUP
    most = (n_edges + s["tiles"] * (P - 1)) // P
    s["slots"] = -(-most // BODY) * BODY
    s["cols"] = n_edges // P
    s["tail"] = n_edges - s["cols"] * P
    s["sort_half"] = max(k for k in range(1, 13) if s["cols"] % (2 * k) == 0)
    return s


def gnn_kernel(nc, t, out):
    f32, bf16, i32 = mybir.dt.float32, mybir.dt.bfloat16, mybir.dt.int32
    ALU, ACT, AX = mybir.AluOpType, mybir.ActivationFunctionType, mybir.AxisListType
    N, E = t["x"].shape[0], t["src"].shape[0]
    z = _sizes(N, E)
    TILES, GROUPS, PT, NT = z["tiles"], z["groups"], z["padded_tiles"], z["slots"]
    COLS, TAIL, CS = z["cols"], z["tail"], z["sort_half"]
    SORT_ITERS, ITERS = COLS // (2 * CS), NT // BODY
    MAIN = COLS * P
    ds = bass.ds

    ctx = ExitStack()
    with ctx:
        def sb(name, shape, dt=f32, where=ctx):
            return where.enter_context(nc.sbuf_tensor(name, shape, dt))

        def sem(name):
            return ctx.enter_context(nc.semaphore(name))

        def dram(name, shape, dt=f32):
            return nc.dram_tensor(name, shape, dt, kind="Internal").ap()

        rec_d = dram("rec_by_dst", (P * NT, REC))
        rec_s = dram("rec_by_src", (P * NT, REC_S))
        xs = [dram(f"x_layer{k}", (PT * P, F)) for k in range(4)]
        hrow = dram("attention_rows", (PT * P, ROW_G))
        gathered_rows = dram("gathered_rows", (P, NT, ROW_G))

        psum = ctx.enter_context(nc.psum_tensor("psum", [P, 8, 512], f32))

        iota_row = sb("iota_row", [P, P])
        iota_part = sb("iota_part", [P, 1])
        ident = sb("ident", [P, P])
        ident_b = sb("ident_b", [P, P], bf16)
        eps = sb("eps", [P, 1])
        w1_0 = sb("w1_0", [P, 2 * F])
        w2_0 = sb("w2_0", [P, 2, F])
        we_0 = sb("we_0", [EXTRA, F])
        be1_0 = sb("be1_0", [EXTRA, F])
        w_gat = sb("w_gat", [P, F + 2 * HEADS])
        att = sb("att", [P, 2, F])
        att_w = sb("att_w", [P, 2, F])
        w1_2 = sb("w1_2", [P, F])
        w2_2 = sb("w2_2", [P, 1, F])
        we_2 = sb("we_2", [EXTRA, F])
        w_3 = sb("w_3", [P, F])
        w_3t = sb("w_3t", [P, F])
        b_3 = sb("b_3", [EXTRA, F])
        b1_0 = sb("b1_0", [P, 2])
        cols = sb("cols", [P, 8])
        b2_0, gamma_0, beta_0, b1_2, b2_2, agg_w = (cols[:, k:k + 1] for k in range(6))
        rows = sb("rows", [P, 3, F])
        bias_1, gamma_1, beta_1 = (rows[:, k, :] for k in range(3))
        affine = sb("affine", [P, 4])
        bn_scale, bn_shift, one_col, zero_col = (affine[:, k:k + 1] for k in range(4))
        tile_of_d = sb("tile_of_d", [1, NT], i32)
        tile_of_s = sb("tile_of_s", [1, NT], i32)
        sums = sb("sums", [P, PT, SUM_W])
        dst_max = sb("dst_max", [P, PT, 2 * HEADS])
        rec_src = sb("rec_src", [P, COLS + 1, REC_S])
        addr_src = sb("addr_src", [P, COLS + 1], i32)

        loaded = sem("loaded")
        made = sem("made")
        dve_steps = sem("dve_steps")
        hist_done = sem("hist_done")
        bins_made = sem("bins_made")
        counted = sem("counted")
        signs_summed = sem("signs_summed")
        prefix_done = sem("prefix_done")
        owner_done = sem("owner_done")
        owner_copied = sem("owner_copied")
        filled = sem("filled")
        small_psum = sem("small_psum")

        BY_SIGNS = TILES // 3 * 2

        sort = ctx.enter_context(ExitStack())
        with sort:
            W = COLS + 1
            key = [sb(f"key{k}", [P, W], i32, sort) for k in range(2)]
            tmp = addr_src
            square_all = addr_src[:].bitcast(f32).unsqueeze(2)
            junk, sign_out = (addr_src[:].bitcast(bf16)[:, k * W:(k + 1) * W] for k in range(2))
            bin_ = [sb(f"bin{k}", [P, W], f32, sort) for k in range(2)]
            local_dst = sb("local_dst", [P, W], f32, sort)
            local = [local_dst[:].unsqueeze(2), rec_src[:, :, COL_LOCAL:COL_LOCAL + 1]]
            signs = sb("signs", [P, TILES + 1], f32, sort)
            less = sb("less", [P, TILES], f32, sort)
            hist = sb("hist", [P, 2, TILES], f32, sort)
            tiles_f = sb("tiles_f", [P, 2, TILES], f32, sort)
            tiles_i = sb("tiles_i", [P, 2, TILES], i32, sort)
            ends = sb("ends", [P, 2, TILES], f32, sort)
            zeros = sb("zeros", [P, TILES], f32, sort)
            place = sb("place", [P, 2, TILES], f32, sort)
            end_col = sb("end_col", [P, 2], f32, sort)
            before = sb("before", [P, P], f32, sort)
            ones = sb("ones", [P, P], f32, sort)
            iota_t = sb("iota_t", [P, NT], f32, sort)
            ended = sb("ended", [P, NT], f32, sort)
            blank = sb("blank", [P, HALF, REC], f32, sort)
            FILL = blank[:, :, :]
            picked = sb("picked", [P, 2, 2, TILES], f32, sort)
            pos = sb("pos", [P, 2, 2, CS], f32, sort)
            pos_i = sb("pos_i", [P, 2, 2, CS], i32, sort)
            pos_t = sb("pos_t", [P, 2, 2, CS], i32, sort)
            addr = sb("addr", [P, 2, CS], i32, sort)
            ea = [sb(f"ea{w}", [P, 2, CS, w], f32, sort) for w in (6, 3, 16)]
            out_d = sb("out_d", [P, 2, CS, REC], f32, sort)
            pack = sb("pack", [P, W, 4], bf16, sort)
            out_d_b = out_d[:].bitcast(bf16)
            spare_row = sb("spare_row", [1, F], f32, sort)

            keys_in = [t["dst"], t["src"]]
            attrs_in = [t["edge_attr_6"], t["edge_attr_3"], t["edge_attr_16"]]

            with nc.Block() as block:

                @block.sync
                def _(sp):
                    sp.wait_ge(made, 2)
                    for k in range(2):
                        sp.dma_start(key[k][:, 0:COLS], keys_in[k][0:MAIN].rearrange("(p c) -> p c", p=P)).then_inc(loaded, 16)
                        if TAIL:
                            sp.dma_start(key[k][0:TAIL, COLS:W], keys_in[k][MAIN:E].rearrange("(p c) -> p c", c=1)).then_inc(loaded, 16)
                    sp.wait_ge(loaded, 16 * (4 if TAIL else 2))
                    col = lambda a, c=1: a.rearrange("(p c) -> p c", c=c)
                    row = lambda a: a.rearrange("(a n) -> a n", a=1)
                    sp.wait_ge(made, 3)
                    small = [
                        (w1_0[:], t["L0_gnn_W1"]), (w2_0[:], t["L0_gnn_W2"].rearrange("(j p) n -> p j n", j=2)),
                        (we_0[0:6, :], t["L0_gnn_We0"]), (we_0[6:9, :], t["L0_gnn_We1"]),
                        (we_0[25:26, :], row(t["L0_gnn_be0"])), (be1_0[25:26, :], row(t["L0_gnn_be1"])),
                        (w_gat[:, 0:F], t["L1_gnn_W"]),
                        (att[:, 0, :], row(t["L1_gnn_att_src"].rearrange("h c -> (h c)")).to_broadcast([P, F])),
                        (att[:, 1, :], row(t["L1_gnn_att_dst"].rearrange("h c -> (h c)")).to_broadcast([P, F])),
                        (w1_2[:], t["L2_gnn_W1"]), (w2_2[:, 0, :], t["L2_gnn_W2"]),
                        (we_2[9:25, :], t["L2_gnn_We"]), (we_2[25:26, :], row(t["L2_gnn_be"])),
                        (w_3[:], t["L3_gnn_W"]), (b_3[25:26, :], row(t["L3_gnn_b"])),
                        (b2_0, col(t["L0_gnn_b2"])), (gamma_0, col(t["L0_gnn_gamma"])), (beta_0, col(t["L0_gnn_beta"])),
                        (b1_2, col(t["L2_gnn_b1"])), (b2_2, col(t["L2_gnn_b2"])),
                        (agg_w, row(t["L3_gnn_agg_weight"]).to_broadcast([P, 1])),
                        (bias_1, row(t["L1_gnn_bias"]).to_broadcast([P, F])),
                        (gamma_1, row(t["L1_gnn_ln_gamma"]).to_broadcast([P, F])),
                        (beta_1, row(t["L1_gnn_ln_beta"]).to_broadcast([P, F])),
                        (b1_0[:, 0:1], col(t["L0_gnn_b1"][0:P])), (b1_0[:, 1:2], col(t["L0_gnn_b1"][P:2 * P])),
                    ]
                    for to, of in small:
                        sp.dma_start(to, of).then_inc(loaded, 16)
                    sp.wait_ge(loaded, 16 * ((4 if TAIL else 2) + len(small)))

                @block.scalar
                def _(act):
                    act.wait_ge(made, 4)
                    rd = rec_d.rearrange("(p t) w -> p t w", t=NT)
                    with act.Fori(0, NT // HALF) as i:
                        act.dma_start(rd[:, ds(i * HALF, HALF), :], FILL).then_inc(filled, 16)
                    rs = rec_s.rearrange("(p t) w -> p t w", t=NT)
                    few = blank[:, :, 0:REC_S]
                    with act.Fori(0, NT // HALF) as i:
                        act.dma_start(rs[:, ds(i * HALF, HALF), :], few).then_inc(filled, 16)
                    act.dma_start(xs[0][0:N, :], t["x"]).then_inc(filled, 16)
                    total = 2 * (NT // HALF) + 1
                    spare = PT * P - N
                    for r in range(0, spare, P):
                        k = min(P, spare - r)
                        act.dma_start(xs[0][N + r:N + r + k, :], ones[0:k, :]).then_inc(filled, 16)
                        total += 1
                    act.wait_ge(bins_made, 1)
                    for b in range(BY_SIGNS, TILES):
                        act.activation(sign_out, bin_[1][:], ACT.Sign, bias=less[:, b:b + 1],
                                       accum_out=signs[:, b:b + 1]).then_inc(signs_summed, 1)
                        act.wait_ge(signs_summed, b - BY_SIGNS + 1)
                    act.wait_ge(filled, 16 * total)

                @block.gpsimd
                def _(pool):
                    for k in range(2):
                        pool.memset(key[k][:, COLS:W], -P).then_inc(made, 1)
                    for m in (we_0, be1_0, we_2, b_3):
                        pool.memset(m[:], 0.0)
                    pool.memset(dst_max[:], 0.0)
                    pool.memset(zeros[:], 0.0)
                    pool.memset(rec_src[:], 0.0)
                    pool.memset(one_col, 1.0)
                    pool.memset(zero_col, 0.0)
                    pool.memset(eps[:], NORM_EPS).then_inc(made, 1)
                    pool.memset(ones[:], 1.0)
                    pool.memset(blank[:], 0.0).then_inc(small_psum, 1)
                    pool.wait_ge(small_psum, 1)
                    blank_b = blank[:].bitcast(bf16)
                    for n, value in enumerate((-1.0, 1.0, 0.0, 1.0)):
                        pool.memset(blank_b[:, :, 2 * COL_PACK + n:2 * COL_PACK + n + 1], value)
                    pool.memset(blank[:, :, 0:1], -1.0).then_inc(made, 1)
                    pool.iota(iota_row[:], pattern=[[1, P]], base=0, channel_multiplier=0, allow_small_or_imprecise_dtypes=True)
                    pool.iota(iota_part[:], pattern=[[0, 1]], base=0, channel_multiplier=1, allow_small_or_imprecise_dtypes=True)
                    pool.iota(iota_t[:], pattern=[[1, NT]], base=0, channel_multiplier=0, allow_small_or_imprecise_dtypes=True).then_inc(made, 1)

                @block.vector
                def _(v):
                    n = [0]

                    def link(ins):
                        n[0] += 1
                        ins.then_inc(dve_steps, 1)
                        v.wait_ge(dve_steps, n[0])

                    v.memset(sums[:, :, :], 0.0)
                    v.memset(signs[:, TILES:TILES + 1], -float(W))
                    v.wait_ge(made, 5)
                    link(v.tensor_scalar(less[:], iota_row[:, 0:TILES], -1.0, 0.5, ALU.mult, ALU.add))
                    link(v.tensor_scalar(ident[:], iota_row[:], iota_part[:], None, ALU.is_equal))
                    v.tensor_copy(ident_b[:], ident[:])
                    v.tensor_scalar(before[:], iota_row[:], iota_part[:], None, ALU.is_gt)
                    v.wait_ge(loaded, 16 * (4 if TAIL else 2))
                    for k in range(2):
                        link(v.tensor_single_scalar(tmp[:], key[k][:], 7, ALU.arith_shift_right))
                        link(v.tensor_copy(bin_[k][:], tmp[:]))
                        link(v.tensor_single_scalar(tmp[:], key[k][:], P - 1, ALU.bitwise_and))
                        link(v.tensor_copy(local[k], tmp[:].unsqueeze(2)))
                    v.tensor_copy(rec_src[:, :, COL_INDEX:COL_INDEX + 1].bitcast(i32), key[0][:].unsqueeze(2))
                    v.memset(rec_src[:, :, 2:3], 1.0)
                    loc = local[0]
                    link(v.tensor_mul(square_all, loc, loc))
                    v.tensor_copy(pack[:, :, 0:1], loc)
                    v.memset(pack[:, :, 3:4], 1.0)
                    link(v.tensor_copy(pack[:, :, 1:2], square_all))
                    link(v.tensor_sub(pack[:, :, 2:3], square_all, pack[:, :, 1:2]))
                    v.sem_inc(bins_made, 1)
                    for b in range(TILES):
                        v.tensor_scalar(junk, bin_[0][:], float(b), 0.0, ALU.is_equal, ALU.add,
                                        accum_out=hist[:, 0, b:b + 1]).then_inc(counted, 1)
                        v.wait_ge(counted, b + 1)
                    for b in range(BY_SIGNS):
                        v.tensor_scalar(junk, bin_[1][:], float(b), 0.0, ALU.is_equal, ALU.add,
                                        accum_out=hist[:, 1, b:b + 1]).then_inc(counted, 1)
                        v.wait_ge(counted, TILES + b + 1)
                    v.wait_ge(signs_summed, TILES - BY_SIGNS)
                    link(v.tensor_sub(hist[:, 1, BY_SIGNS:], signs[:, BY_SIGNS:TILES], signs[:, BY_SIGNS + 1:TILES + 1]))
                    link(v.tensor_single_scalar(hist[:, 1, BY_SIGNS:], hist[:, 1, BY_SIGNS:], 0.5, ALU.mult))
                    v.sem_inc(hist_done, 1)
                    v.wait_ge(prefix_done, 1)
                    total_p = psum[:, 1, 0:2 * TILES].rearrange("p (k b) -> p k b", k=2)
                    prefix_p = psum[:, 0, 0:2 * TILES].rearrange("p (k b) -> p k b", k=2)
                    link(v.tensor_single_scalar(tiles_f[:], total_p, float(P - 1), ALU.add))
                    link(v.tensor_copy(tiles_i[:], tiles_f[:]))
                    link(v.tensor_single_scalar(tiles_i[:], tiles_i[:], 7, ALU.arith_shift_right))
                    link(v.tensor_copy(tiles_f[:], tiles_i[:]))
                    for k in range(2):
                        link(v.tensor_tensor_scan(ends[:, k, :], tiles_f[:, k, :], zeros[:], 0.0, ALU.add, ALU.add))
                    link(v.tensor_sub(place[:], ends[:], tiles_f[:]))
                    link(v.scalar_tensor_tensor(place[:], place[:], float(P), prefix_p, ALU.mult, ALU.add))
                    for k in range(2):
                        link(v.tensor_tensor(picked[0:TILES, 0, k, :], ends[0:TILES, k, :], ident[0:TILES, 0:TILES], ALU.mult))
                        link(v.tensor_reduce(end_col[0:TILES, k:k + 1], picked[0:TILES, 0, k, :], AX.X, ALU.add))
                    for k, table in enumerate((tile_of_d, tile_of_s)):
                        if k:
                            v.wait_ge(owner_done, 1)
                        link(v.tensor_scalar(ended[0:TILES, :], iota_t[0:TILES, :], end_col[0:TILES, k:k + 1], None, ALU.is_ge))
                        v.sem_inc(owner_copied, 1)
                        v.wait_ge(owner_done, k + 1)
                        for c in range(0, NT, 512):
                            w = min(512, NT - c)
                            link(v.tensor_single_scalar(table[0:1, c:c + w], psum[0:1, 4 + c // 512, 0:w], float(TILES - 1), ALU.min))
                    v.sem_inc(owner_copied, 1)
                    v.wait_ge(loaded, 16 * ((4 if TAIL else 2) + 26))
                    link(v.tensor_tensor(att_w[:], att[:], w_gat[:, 0:F].unsqueeze(1).to_broadcast([P, 2, F]), ALU.mult))
                    link(v.tensor_reduce(w_gat[:, F:F + 2 * HEADS], att_w[:].rearrange("p a (h c) -> p (a h) c", h=HEADS), AX.X, ALU.add))
                    link(v.tensor_add(we_0[:], we_0[:], be1_0[:]))
                    v.wait_ge(owner_done, 3)
                    link(v.tensor_copy(w_3t[:], psum[:, 2, 0:P]))

                @block.tensor
                def _(pe):
                    pe.wait_ge(hist_done, 1)
                    h2 = hist[:].rearrange("p k b -> p (k b)")
                    pe.matmul(psum[:, 0, 0:2 * TILES], before[:], h2, start=True, stop=True)
                    pe.matmul(psum[:, 1, 0:2 * TILES], ones[:], h2, start=True, stop=True).then_inc(prefix_done, 1)
                    for k in range(2):
                        pe.wait_ge(owner_copied, k + 1)
                        for c in range(0, NT, 512):
                            w = min(512, NT - c)
                            last = pe.matmul(psum[:, 4 + c // 512, 0:w], ones[0:TILES, :], ended[0:TILES, c:c + w], start=True, stop=True)
                        last.then_inc(owner_done, 1)
                    pe.wait_ge(loaded, 16 * ((4 if TAIL else 2) + 26))
                    pe.transpose(psum[:, 2, 0:P], w_3[:], ident[:]).then_inc(owner_done, 1)

            attrs_loaded = [sem(f"attrs_loaded{h}") for h in range(2)]
            attrs_copied = sem("attrs_copied")
            keys_copied = sem("keys_copied")
            addr_ready = sem("addr_ready")
            scattered = [sem(f"scattered{h}") for h in range(2)]
            half_free = [sem(f"half_free{h}") for h in range(2)]
            half_taken = sem("half_taken")
            rank_step = sem("rank_step")
            addr_step = sem("addr_step")
            HALF_SC = CS * 16

            def attr_src(k, start, h):
                return attrs_in[k][0:MAIN, :].rearrange("(p c) w -> p c w", c=COLS)[:, ds(start, CS), :]

            with nc.Block() as block:

                @block.sync
                def _(sp):
                    with sp.Fori(0, SORT_ITERS) as i:
                        for h in range(2):
                            sp.wait_ge(attrs_copied, i * 2 + h + 1)
                            for k in range(3):
                                sp.dma_start(ea[k][:, h, :, :], attr_src(k, i * (2 * CS) + h * CS, h)).then_inc(attrs_loaded[h], 16)
                    if TAIL:
                        sp.wait_ge(attrs_copied, 2 * SORT_ITERS + 1)
                        for k in range(3):
                            sp.dma_start(ea[k][0:TAIL, 0, 0, :], attrs_in[k][MAIN:E, :]).then_inc(attrs_loaded[0], 16)

                @block.scalar
                def _(act):
                    def copy_attrs(h, rows, c, pack_at):
                        at = COL_ATTR
                        for k in range(3):
                            w = ea[k].shape[3]
                            act.copy(out_d[0:rows, h, 0:c, at:at + w], ea[k][0:rows, h, 0:c, :])
                            at += w
                        act.copy(out_d_b[0:rows, h, 0:c, 2 * COL_PACK:2 * REC], pack[0:rows, pack_at, :])
                        return act.copy(out_d[0:rows, h, 0:c, COL_PACK - 1:COL_PACK], one_col[0:rows].unsqueeze(1).to_broadcast([rows, c, 1]))

                    act.sem_inc(attrs_copied, 2)
                    act.sem_inc(half_free[0], 1)
                    with act.Fori(0, SORT_ITERS) as i:
                        for h in range(2):
                            act.wait_ge(half_free[h], i + 1)
                            act.wait_ge(attrs_loaded[h], i * 48 + 48)
                            copy_attrs(h, P, CS, ds(i * (2 * CS) + h * CS, CS)).then_inc(attrs_copied, 1)
                    if TAIL:
                        act.wait_ge(half_free[0], SORT_ITERS + 1)
                        act.wait_ge(attrs_loaded[0], SORT_ITERS * 48 + 48)
                        copy_attrs(0, TAIL, 1, ds(COLS, 1)).then_inc(attrs_copied, 1)

                @block.vector
                def _(v):
                    def rank(col, h, j, step):
                        for k in range(2):
                            v.wait_ge(rank_step, step + k)
                            v.scalar_tensor_tensor(picked[:, h, k, :], iota_row[:, 0:TILES], bin_[k][:, col], place[:, k, :],
                                                   ALU.is_equal, ALU.mult, accum_out=pos[:, h, k, j:j + 1])
                        for k in range(2):
                            v.scalar_tensor_tensor(place[:, k, :], iota_row[:, 0:TILES], bin_[k][:, col], place[:, k, :],
                                                   ALU.is_equal, ALU.add).then_inc(rank_step, 1)

                    def address(h, c, col0, n_rank, n_addr, rows):
                        sl = lambda m: m[0:rows, h, :, 0:c]
                        v.wait_ge(rank_step, n_rank)
                        v.tensor_copy(sl(pos_i), sl(pos)).then_inc(addr_step, 1)
                        v.wait_ge(addr_step, n_addr + 1)
                        v.tensor_single_scalar(sl(pos_t), sl(pos_i), 7, ALU.arith_shift_right).then_inc(addr_step, 1)
                        v.wait_ge(addr_step, n_addr + 2)
                        v.tensor_single_scalar(sl(pos_i), sl(pos_i), P - 1, ALU.bitwise_and).then_inc(addr_step, 1)
                        v.wait_ge(addr_step, n_addr + 3)
                        v.tensor_copy(out_d[0:rows, h, 0:c, COL_LOCAL], local_dst[0:rows, col0])
                        v.tensor_copy(out_d[0:rows, h, 0:c, COL_INDEX].bitcast(i32), key[1][0:rows, col0])
                        v.scalar_tensor_tensor(addr_src[0:rows, col0], pos_i[0:rows, h, 1, 0:c], float(NT), pos_t[0:rows, h, 1, 0:c], ALU.mult, ALU.add)
                        v.scalar_tensor_tensor(addr[0:rows, h, 0:c], pos_i[0:rows, h, 0, 0:c], float(NT), pos_t[0:rows, h, 0, 0:c], ALU.mult, ALU.add).then_inc(addr_ready, 1)

                    v.sem_inc(rank_step, 2)
                    with v.Fori(0, SORT_ITERS) as i:
                        for h in range(2):
                            for j in range(CS):
                                rank(ds(i * (2 * CS) + h * CS + j, 1), h, j, i * (4 * CS) + 2 * (h * CS + j) + 1)
                            v.wait_ge(half_free[h], i + 1)
                            address(h, CS, ds(i * (2 * CS) + h * CS, CS), i * (4 * CS) + 2 * (h + 1) * CS + 2,
                                    i * 6 + h * 3, P)
                    if TAIL:
                        rank(ds(COLS, 1), 0, 0, 2 * COLS + 1)
                        v.wait_ge(half_free[0], SORT_ITERS + 1)
                        address(0, 1, ds(COLS, 1), 2 * COLS + 4, SORT_ITERS * 6, TAIL)

                @block.gpsimd
                def _(pool):
                    def scatter(h, c, rows, other_done=None):
                        for j in range(c):
                            if other_done is not None and j == min(2, c - 1):
                                pool.wait_ge(scattered[1 - h], other_done)
                                pool.sem_inc(half_free[1 - h], 1)
                            pool.indirect_dma_start(
                                rec_d, bass.IndirectOffsetOnAxis(ap=addr[0:rows, h, j:j + 1], axis=0),
                                out_d[0:rows, h, j, :], None).then_inc(scattered[h], 16)

                    pool.dma_start(spare_row[:], t["x"][0:1, :]).then_inc(scattered[1], 16)
                    with pool.Fori(0, SORT_ITERS) as i:
                        for h in range(2):
                            pool.wait_ge(attrs_copied, i * 2 + h + 3)
                            pool.wait_ge(addr_ready, i * 2 + h + 1)
                            pool.sem_inc(half_taken, 1)
                            scatter(h, CS, P, i * HALF_SC + (HALF_SC if h else 16))
                    if TAIL:
                        pool.wait_ge(attrs_copied, 2 * SORT_ITERS + 3)
                        pool.wait_ge(addr_ready, 2 * SORT_ITERS + 1)
                        scatter(0, 1, TAIL)
                    pool.wait_ge(scattered[0], SORT_ITERS * HALF_SC + (16 if TAIL else 0))
                    pool.wait_ge(scattered[1], SORT_ITERS * HALF_SC + 16)

        onehot_ready = sem("onehot_ready")
        tile_summed = sem("tile_summed")
        tile_added = sem("tile_added")
        rec_loaded = [sem(f"rec_loaded{h}") for h in range(2)]
        row_here = [sem(f"row_here{s}") for s in range(BODY)]
        cleared = sem("cleared")
        spare = sb("spare", [1, 2, F])
        half_started = sem("half_started")
        stats_made = sem("stats_made")
        work = ctx.enter_context(ExitStack())
        rec = sb("rec", [P, 2, HALF, REC])
        recs = sb("recs", [P, 2, HALF, REC_S])
        gathered = sb("gathered", [P, BODY, ROW_G])
        onehot = sb("onehot", [P, BODY, P])
        loop = [0]

        def free_rings(pe, v):
            if pe is not None and loop[0] == 0:
                pe.sem_inc(tile_summed, BODY)
            if v is not None and loop[0] == 0:
                v.sem_inc(tile_added, SUM_BANKS)

        NH = NT // HALF
        turns_rec, turns_row = [0], [0]

        class Half:

            def __init__(self, i, n):
                self.i, self.n, self.parity = i, n, n % 2

            def __add__(self, k):
                return Half(self.i, self.n + k)

            def times(self, k, c=0):
                return self.n * k + c if self.i is None else self.i * (2 * k) + (self.n * k + c)

            def turns(self, before=0):
                return self.times(8, 16 * (before + 1) - 8 * self.parity)

        def halves(eng, start, stop, body):
            pairs = (stop - start) // 2
            with eng.Fori(0, pairs) as i:
                for k in range(2):
                    body(Half(i, start + k))
            if (stop - start) % 2:
                body(Half(None, stop - 1))

        def load_records(sp, table, width, ring):
            view = table.rearrange("(p t) w -> p t w", t=NT)
            base = loop[0] * NT
            with sp.Fori(0, ITERS) as i:
                for h in range(2):
                    sp.wait_ge(tile_summed, i * BODY + (base + h * HALF + HALF))
                    sp.dma_start(ring[:, h, :, :], view[:, ds(i * BODY + h * HALF, HALF), :]).then_inc(rec_loaded[h], 16)

        def gather_rows(pool, table, width, ring):
            base = loop[0] * NT
            with pool.Fori(0, ITERS) as i:
                for h in range(2):
                    pool.wait_ge(rec_loaded[h], i * 16 + (turns_rec[0] + 1) * 16)
                    pool.wait_ge(tile_summed, i * BODY + (base + h * HALF + HALF))
                    pool.sem_inc(half_started, 1)
                    for u in range(HALF):
                        slot = h * HALF + u
                        pool.indirect_dma_start(
                            gathered[:, slot, 0:width], None, table,
                            bass.IndirectOffsetOnAxis(ap=ring[:, h, u, COL_INDEX:COL_INDEX + 1].bitcast(i32), axis=0),
                        ).then_inc(row_here[slot], 16)

        def tile_numbers(eng, regs, table, at):
            eng.load(regs, table[0:1, ds(at, HALF)])
            return [eng.snap(r, min_val=0, max_val=TILES - 1) for r in regs]

        def sum_layer(rec_table, rec_w, ring, tile_of, x_table, extra):
            base = loop[0] * NT
            at = EXTRA - (extra[1] - extra[0]) if extra else FEAT
            end = FEAT + F
            width = end - at

            with nc.Block() as block:

                @block.sync
                def _(sp):
                    load_records(sp, rec_table, rec_w, ring)

                @block.gpsimd
                def _(pool):
                    gather_rows(pool, x_table, F, ring)

                @block.vector
                def _(v):
                    free_rings(None, v)
                    regs = [v.alloc_register(f"v{loop[0]}_{u}") for u in range(HALF)]
                    with v.Fori(0, ITERS) as i:
                        for h in range(2):
                            nodes = tile_numbers(v, regs, tile_of, i * BODY + h * HALF)
                            v.wait_ge(rec_loaded[h], i * 16 + (turns_rec[0] + 1) * 16)

                            def make_onehot(u):
                                s = h * HALF + u
                                v.wait_ge(tile_summed, i * BODY + (base + s + 1 + BODY - ONEHOTS))
                                v.tensor_scalar(onehot[:, s % ONEHOTS, :], iota_row[:], ring[:, h, u, COL_LOCAL:COL_LOCAL + 1],
                                                None, ALU.is_equal).then_inc(onehot_ready, 1)

                            def add(u):
                                s = h * HALF + u
                                v.wait_ge(tile_summed, i * BODY + (base + s + 1 + BODY))
                                v.wait_ge(tile_added, i * BODY + (base + s + SUM_BANKS))
                                to = sums[:, ds(nodes[u], 1), at:end].rearrange("p a w -> p (a w)")
                                v.tensor_tensor(to, psum[:, s % SUM_BANKS, 0:width], to, ALU.add).then_inc(tile_added, 1)

                            for u in range(3):
                                make_onehot(u)
                            for u in range(HALF):
                                if u + 3 < HALF:
                                    make_onehot(u + 3)
                                add(u)
                    for r in regs:
                        v.free_register(r)

                @block.tensor
                def _(pe):
                    free_rings(pe, None)
                    with pe.Fori(0, ITERS) as i:
                        for s in range(BODY):
                            h, u, bank = s // HALF, s % HALF, s % SUM_BANKS
                            pe.wait_ge(onehot_ready, i * BODY + (base + s + 1))
                            pe.wait_ge(tile_added, i * BODY + (base + s + 1))
                            if extra:
                                pe.matmul(psum[:, bank, 0:width - F], onehot[:, s % ONEHOTS, :], ring[:, h, u, extra[0]:extra[1]],
                                          start=True, stop=True)
                            pe.wait_ge(row_here[s], i * 16 + (turns_row[0] + 1) * 16)
                            pe.matmul(psum[:, bank, width - F:width], onehot[:, s % ONEHOTS, :], gathered[:, s, 0:F],
                                      start=True, stop=True).then_inc(tile_summed, 1)
            loop[0] += 1
            turns_rec[0] += ITERS
            turns_row[0] += ITERS

        def clear_sums(lo, hi):
            with nc.Block() as block:
                @block.vector
                def _(v):
                    v.memset(sums[:, :, lo:hi], 0.0).then_inc(cleared, 1)

        phase = [0]

        def feats(g):
            return sums[:, ds(g * GROUP, GROUP), FEAT:FEAT + F]

        def mlp_phase(we, w1, b1, w2, b2, hidden, extra_out=None, scale=None):
            k = phase[0]
            phase[0] += 1
            s_stage, s_ext, s_extc, s_agg, s_aggc, s_h, s_hc, s_o, s_oc = (sem(f"m{k}_{n}") for n in (
                "staged", "extras_turned", "extras_copied", "sums_turned", "sums_copied", "hidden", "hidden_copied", "outs", "outs_copied"))
            with ExitStack() as scope:
                stage = sb(f"m{k}_stage", [P, GROUP, SUM_W], f32, scope)
                ext = sb(f"m{k}_ext", [EXTRA, GROUP_W], f32, scope)
                agg = sb(f"m{k}_agg", [P, GROUP_W], f32, scope)
                hid = sb(f"m{k}_hid", [P, max(hidden, 1), GROUP_W], f32, scope)
                with nc.Block() as block:

                    @block.vector
                    def _(v):
                        v.sem_inc(s_agg, 1)
                        with v.Fori(0, GROUPS) as g:
                            v.wait_ge(s_agg, g + 1)
                            v.tensor_copy(stage[:], sums[:, ds(g * GROUP, GROUP), :]).then_inc(s_stage, 1)
                            v.wait_ge(s_ext, g + 1)
                            v.tensor_copy(ext[:], psum[0:EXTRA, 0, :]).then_inc(s_extc, 1)
                            v.wait_ge(s_agg, g + 2)
                            v.tensor_copy(agg[:], psum[:, 1, :]).then_inc(s_aggc, 1)

                    @block.scalar
                    def _(act):
                        wide_psum = psum[:, 4, :].rearrange("p (j f) -> p j f", j=GROUP)
                        with act.Fori(0, GROUPS) as g:
                            for j in range(hidden):
                                act.wait_ge(s_h, g * hidden + (j + 1))
                                act.activation(hid[:, j, :], psum[:, 2 + j, :], ACT.Relu, bias=b1[:, j:j + 1]).then_inc(s_hc, 1)
                            act.wait_ge(s_o, g + 1)
                            if hidden:
                                act.activation(feats(g), wide_psum, ACT.Identity, bias=b2).then_inc(s_oc, 1)
                            else:
                                act.activation(feats(g), wide_psum, ACT.Copy, scale=scale).then_inc(s_oc, 1)

                    @block.tensor
                    def _(pe):
                        pe.sem_inc(s_oc, 1)
                        with pe.Fori(0, GROUPS) as g:
                            pe.wait_ge(s_stage, g + 1)
                            for j in range(GROUP):
                                last = pe.transpose(psum[0:EXTRA, 0, j * P:(j + 1) * P], stage[:, j, 0:EXTRA], ident[:])
                            last.then_inc(s_ext, 1)
                            pe.wait_ge(s_extc, g + 1)
                            for j in range(GROUP):
                                last = pe.matmul(psum[:, 1, j * P:(j + 1) * P], stage[:, j, FEAT:FEAT + F], ident[:],
                                                 start=j == 0, stop=not hidden and j == GROUP - 1)
                            if hidden:
                                last = pe.matmul(psum[:, 1, :], we[:], ext[:], start=False, stop=True)
                            last.then_inc(s_agg, 1)
                            pe.wait_ge(s_aggc, g + 1)
                            for j in range(hidden):
                                pe.matmul(psum[:, 2 + j, :], w1[:, j * F:(j + 1) * F], agg[:], start=True, stop=True).then_inc(s_h, 1)
                            pe.wait_ge(s_oc, g + 1)
                            if hidden:
                                for j in range(hidden):
                                    pe.wait_ge(s_hc, g * hidden + (j + 1))
                                    last = pe.matmul(psum[:, 4, :], w2[:, j, :], hid[:, j, :], start=j == 0, stop=j == hidden - 1)
                            else:
                                pe.matmul(psum[:, 4, :], w2[:], agg[:], start=True, stop=False)
                                last = pe.matmul(psum[:, 4, :], extra_out[:], ext[:], start=False, stop=True)
                            last.then_inc(s_o, 1)

        def bn_phase():
            whole, rest_n = N // P, N % P
            chunks = [(c, min(GROUP, whole - c), P) for c in range(0, whole, GROUP)] + [(whole, 1, rest_n)] * (rest_n > 0)
            steps, rooted = sem("bn_steps"), sem("bn_rooted")
            with ExitStack() as scope:
                stats = sb("bn_stats", [P, len(chunks), 6], f32, scope)
                mv = sb("bn_mv", [P, 4], f32, scope)
                with nc.Block() as block:

                    @block.vector
                    def _(v):
                        for n, (c, k, w) in enumerate(chunks):
                            v.bn_stats(stats[:, n, :], sums[:, c:c + k, FEAT:FEAT + w]).then_inc(steps, 1)
                        n = [len(chunks)]
                        v.wait_ge(steps, n[0])

                        def link(ins):
                            n[0] += 1
                            ins.then_inc(steps, 1)
                            v.wait_ge(steps, n[0])

                        link(v.bn_aggr(mv[:, 0:2], stats[:].rearrange("p a b -> p (a b)")))
                        v.wait_ge(rooted, 1)
                        link(v.reciprocal(mv[:, 3:4], mv[:, 2:3]))
                        link(v.tensor_mul(bn_scale, mv[:, 3:4], gamma_0))
                        link(v.tensor_mul(mv[:, 0:1], mv[:, 0:1], bn_scale))
                        link(v.tensor_sub(bn_shift, beta_0, mv[:, 0:1]))

                    @block.scalar
                    def _(act):
                        act.wait_ge(steps, len(chunks) + 1)
                        act.activation(mv[:, 2:3], mv[:, 1:2], ACT.Sqrt, bias=eps[:]).then_inc(rooted, 1)

        def norm_rows(v, link, src, dst, stats, mv, root_in, root_out, n_out, stored=None, n_stored=None):
            for j in range(GROUP):
                last = v.bn_stats(stats[:, j, :], src[:, j, :])
            link(last)
            v.sem_inc(stats_made, 1)
            for j in range(GROUP):
                last = v.bn_aggr(mv[:, j, 0:2], stats[:, j, :])
            last.then_inc(root_in, 1)
            v.wait_ge(root_out, n_out)
            link(v.reciprocal(mv[:, :, 3:4], mv[:, :, 2:3]))
            if stored is not None:
                v.wait_ge(stored, n_stored)
            for j in range(GROUP):
                last = v.tensor_scalar(dst[:, j, :], src[:, j, :], mv[:, j, 0:1], mv[:, j, 3:4], ALU.subtract, ALU.mult)
            return last

        def store_group(sp, table, g, tile, done):
            whole = table[0:table.shape[0] // GROUP_W * GROUP_W, :]
            sp.dma_start(whole.rearrange("(t p) f -> p t f", p=P)[:, ds(g * GROUP, GROUP), :], tile).then_inc(done, 16)

        def prime(eng, done, n=1):
            for j in range(n):
                eng.dma_start(spare[0:1, j, :], t["x"][0:1, :]).then_inc(done, 16)

        finish_sems = [sem(f"finish_{n}") for n in (
            "affine", "turned", "x_loaded", "steps", "variances", "roots", "normed", "stored")]

        def finish_phase(turn, scale, shift, x_old, x_new, last_layer=False):
            k = phase[0]
            phase[0] += 1
            before = turn * GROUPS
            s_y, s_turned, s_x, s_chain, s_var, s_root, s_new, s_st = finish_sems
            with ExitStack() as scope:
                yt = sb(f"f{k}_yt", [P, GROUP, P], f32, scope)
                xo = sb(f"f{k}_x", [P, GROUP, F], f32, scope)
                zz = sb(f"f{k}_z", [P, GROUP, F], f32, scope)
                xn = sb(f"f{k}_new", [P, GROUP, F], f32, scope)
                stats = sb(f"f{k}_stats", [P, GROUP, 6], f32, scope)
                mv = sb(f"f{k}_mv", [P, GROUP, 4], f32, scope)
                with nc.Block() as block:

                    @block.sync
                    def _(sp):
                        view = x_old.rearrange("(t p) f -> p t f", p=P)
                        with sp.Fori(0, GROUPS) as g:
                            sp.wait_ge(s_chain, g * 3 + (before * 3 + 1))
                            sp.dma_start(xo[:], view[:, ds(g * GROUP, GROUP), :]).then_inc(s_x, 16)

                    @block.scalar
                    def _(act):
                        def affine(g):
                            act.wait_ge(s_turned, g + (before + 1))
                            act.activation(yt[:], feats(g), ACT.Identity, bias=shift, scale=scale).then_inc(s_y, 1)

                        def roots(g):
                            act.wait_ge(s_var, g + (before + 1))
                            act.activation(mv[:, :, 2:3], mv[:, :, 1:2], ACT.Sqrt, bias=eps[:]).then_inc(s_root, 1)
                            act.wait_ge(s_new, g + (before + 2))

                        if turn == 0:
                            act.sem_inc(s_turned, 1)
                            act.sem_inc(s_new, 1)
                            prime(act, s_st, 1)
                        affine(0)
                        with act.Fori(0, GROUPS - 1) as g:
                            affine(g + 1)
                            roots(g)
                            store_group(act, x_new, g, xn[:], s_st)
                        roots(GROUPS - 1)
                        if last_layer:
                            n = 0
                            for j in range(GROUP):
                                r0 = (GROUPS - 1) * GROUP_W + j * P
                                rows_here = min(P, N - r0)
                                if rows_here > 0:
                                    act.dma_start(x_new[r0:r0 + rows_here, :], xn[0:rows_here, j, :]).then_inc(s_st, 16)
                                    n += 1
                        else:
                            store_group(act, x_new, GROUPS - 1, xn[:], s_st)
                            n = 1
                        act.wait_ge(s_st, 16 * (before + GROUPS + n))

                    @block.tensor
                    def _(pe):
                        if turn == 0:
                            pe.sem_inc(s_chain, 3)
                        with pe.Fori(0, GROUPS) as g:
                            pe.wait_ge(s_y, g + (before + 1))
                            pe.wait_ge(s_chain, g * 3 + (before * 3 + 1))
                            for j in range(GROUP):
                                last = pe.transpose(psum[:, 0, j * P:(j + 1) * P], yt[:, j, :], ident[:])
                            last.then_inc(s_turned, 1)

                    @block.vector
                    def _(v):
                        with v.Fori(0, GROUPS) as g:
                            n = [0]

                            def link(ins):
                                n[0] += 1
                                ins.then_inc(s_chain, 1)
                                v.wait_ge(s_chain, g * 3 + (before * 3 + n[0] + 3))

                            v.wait_ge(s_new, g + (before + 1))
                            v.wait_ge(s_turned, g + (before + 2))
                            v.wait_ge(s_x, g * 16 + (before * 16 + 16))
                            link(v.tensor_tensor(zz[:], psum[:, 0, :].rearrange("p (j f) -> p j f", j=GROUP), xo[:], ALU.add))
                            norm_rows(v, link, zz, xn, stats, mv, s_var, s_root, g + (before + 1),
                                      s_st, g * 16 + (before * 16 + 16)).then_inc(s_new, 1)
                            assert n[0] == 3

        def project_phase(x_table):
            k = phase[0]
            phase[0] += 1
            s_x, s_t, s_tc, s_h, s_hc, s_st, s_ad, s_parts = (sem(f"p{k}_{n}") for n in (
                "x_loaded", "turned", "turned_copied", "rows", "rows_copied", "stored", "dst_copied", "parts"))
            with ExitStack() as scope:
                xo = sb(f"p{k}_x", [P, GROUP, F], f32, scope)
                xt = sb(f"p{k}_xt", [P, GROUP, P], f32, scope)
                hr = sb(f"p{k}_rows", [P, GROUP, ROW_G], f32, scope)
                rest = sb(f"p{k}_rest", [P, GROUP, HEADS], f32, scope)
                WP = 256
                with nc.Block() as block:

                    @block.sync
                    def _(sp):
                        sp.sem_inc(s_t, 1)
                        view = x_table.rearrange("(t p) f -> p t f", p=P)
                        with sp.Fori(0, GROUPS) as g:
                            sp.wait_ge(s_t, g + 1)
                            sp.dma_start(xo[:], view[:, ds(g * GROUP, GROUP), :]).then_inc(s_x, 16)

                    @block.tensor
                    def _(pe):
                        pe.sem_inc(s_hc, 1)
                        pe.sem_inc(s_ad, 1)
                        with pe.Fori(0, GROUPS) as g:
                            pe.wait_ge(s_x, g * 16 + 16)
                            for j in range(GROUP):
                                last = pe.transpose(psum[:, 0, j * P:(j + 1) * P], xo[:, j, :], ident[:])
                            last.then_inc(s_t, 1)
                            pe.wait_ge(s_tc, g + 1)
                            pe.wait_ge(s_hc, g + 1)
                            pe.wait_ge(s_ad, g + 1)
                            for j in range(GROUP):
                                last = pe.matmul(psum[:, 2 + j // 2, (j % 2) * WP:(j % 2) * WP + ROW + HEADS], xt[:, j, :], w_gat[:], start=True, stop=True)
                            last.then_inc(s_h, 1)

                    @block.scalar
                    def _(act):
                        prime(act, s_st, 1)
                        hv = psum[:, 2:4, :].rearrange("p a (b w) -> p (a b) w", b=2)
                        hd = hrow.rearrange("(t p) f -> p t f", p=P)
                        with act.Fori(0, GROUPS) as g:
                            act.wait_ge(s_t, g + 2)
                            act.copy(xt[:].rearrange("p j f -> p (j f)"), psum[:, 0, :]).then_inc(s_tc, 1)
                            act.wait_ge(s_h, g + 1)
                            act.wait_ge(s_st, g * 16 + 16)
                            act.copy(hr[:, :, 0:ROW], hv[:, :, 0:ROW]).then_inc(s_hc, 1)
                            act.wait_ge(s_parts, g * 5 + 5)
                            act.dma_start(hd[:, ds(g * GROUP, GROUP), :], hr[:]).then_inc(s_st, 16)
                        act.wait_ge(s_st, GROUPS * 16 + 16)

                    @block.vector
                    def _(v):
                        hv = psum[:, 2:4, :].rearrange("p a (b w) -> p (a b) w", b=2)
                        v.memset(sums[:, :, FEAT:], 0.0).then_inc(cleared, 1)
                        with v.Fori(0, GROUPS) as g:
                            v.wait_ge(s_hc, g + 2)
                            v.tensor_copy(dst_max[:, ds(g * GROUP, GROUP), 0:HEADS], hv[:, :, ROW:ROW + HEADS])
                            v.tensor_copy(dst_max[:, ds(g * GROUP, GROUP), HEADS:], hv[:, :, F:ROW]).then_inc(s_ad, 1)
                            n = [0]

                            def link(ins):
                                n[0] += 1
                                ins.then_inc(s_parts, 1)
                                v.wait_ge(s_parts, g * 5 + n[0])

                            of = hr[:, :, F:ROW]
                            part = lambda m: hr[:].bitcast(bf16)[:, :, 2 * ROW + m * HEADS:2 * ROW + (m + 1) * HEADS]
                            link(v.tensor_copy(part(0), of))
                            link(v.tensor_sub(rest[:], of, part(0)))
                            link(v.tensor_copy(part(1), rest[:]))
                            link(v.tensor_sub(rest[:], rest[:], part(1)))
                            link(v.tensor_copy(part(2), rest[:]))

        def max_phase():
            QUADS = HALF // 4
            ROUNDS = [(0, 3), (3, 6), (6, 8)]
            UNITS = len(ROUNDS)
            PARTS = P
            PREP = 16
            LOC = 3 * HEADS
            s_split, s_turn, s_turnc, s_prod, s_red, s_max, s_steps = (sem(f"x_{n}") for n in (
                "rows_split", "turned", "turned_copied", "products", "reduced", "maxima", "steps"))
            s_apart = sem("x_apart_turned")
            s_spill = [sem(f"x_rows_kept{k}") for k in range(2)]
            rec0, row0 = turns_rec[0], turns_row[0]
            with ExitStack() as scope:
                parts = sb("x_parts", [P, 2, HALF, PARTS], bf16, scope)
                turned = sb("x_turned", [PARTS, 2 * QUADS, GROUP_W], bf16, scope)
                select = sb("x_select", [PARTS, HEADS, P], bf16, scope)
                apart_n = sb("x_apart_n", [P, PARTS], bf16, scope)
                apart = sb("x_apart", [PARTS, P], bf16, scope)
                node_sq = sb("x_node_sq", [P, 4], f32, scope)
                sel_i = sb("x_sel_i", [P, 2], i32, scope)
                sel_f = sb("x_sel_f", [P, 1], f32, scope)
                sel_c = sb("x_sel_c", [P, HEADS], f32, scope)
                real = sb("x_real", [P, 1], f32, scope)
                big = sb("x_big", [P, 2, QUADS, HEADS, 4], f32, scope)
                psum_b = psum[:].bitcast(bf16)
                gathered_b = gathered[:].bitcast(bf16)
                rec_b = rec[:].bitcast(bf16)
                with nc.Block() as block:
                    @block.vector
                    def _(v):
                        n = [0]

                        def link(ins):
                            n[0] += 1
                            ins.then_inc(s_steps, 1)
                            v.wait_ge(s_steps, n[0])

                        link(v.memset(parts[:], 0.0))
                        link(v.memset(parts[:, :, :, LOC + 3:LOC + 5], 1.0))
                        link(v.tensor_copy(sel_i[:, 0:1], iota_part[:]))
                        link(v.tensor_single_scalar(sel_i[:, 1:2], sel_i[:, 0:1], HEADS - 1, ALU.bitwise_and))
                        link(v.tensor_copy(sel_f[:], sel_i[:, 1:2]))
                        link(v.tensor_single_scalar(real[:], iota_part[:], float(LOC), ALU.is_lt))
                        link(v.tensor_scalar(sel_c[:], iota_row[:, 0:HEADS], sel_f[:], real[:], ALU.is_equal, ALU.mult))
                        link(v.tensor_copy(select[:], sel_c[0:PARTS, :].unsqueeze(2).to_broadcast([PARTS, HEADS, P])))
                        link(v.memset(apart_n[:], 0.0))
                        link(v.tensor_mul(node_sq[:, 0:1], iota_part[:], iota_part[:]))
                        link(v.tensor_single_scalar(node_sq[:, 0:1], node_sq[:, 0:1], -BIG, ALU.mult))
                        link(v.tensor_single_scalar(apart_n[:, LOC:LOC + 1], iota_part[:], 2.0 * BIG, ALU.mult))
                        link(v.memset(apart_n[:, LOC + 1:LOC + 3], -BIG))
                        link(v.tensor_copy(apart_n[:, LOC + 3:LOC + 4], node_sq[:, 0:1]))
                        link(v.tensor_sub(apart_n[:, LOC + 4:LOC + 5], node_sq[:, 0:1], apart_n[:, LOC + 3:LOC + 4]))
                        v.sem_inc(s_split, 2)
                        v.wait_ge(s_apart, 1)
                        link(v.tensor_copy(apart[:], psum_b[0:PARTS, 6, 0:P]))
                        assert n[0] == PREP
                        v.sem_inc(s_red, 2)

                    @block.tensor
                    def _(pe):
                        pe.wait_ge(s_split, 2)
                        pe.wait_ge(s_steps, PREP - 1)
                        pe.transpose(psum_b[0:PARTS, 6, 0:P], apart_n[:], ident_b[:]).then_inc(s_apart, 1)
                        pe.sem_inc(s_turn, 2 * QUADS)
                        pe.sem_inc(s_prod, 2 * QUADS * UNITS)

                    @block.scalar
                    def _(act):
                        act.sem_inc(s_turnc, 2)

                with nc.Block() as block:

                    @block.sync
                    def _(sp):
                        records = rec_d.rearrange("(p t) w -> p t w", t=NT)

                        def load(H):
                            sp.wait_ge(s_split, H.times(1, 1))
                            sp.dma_start(rec[:, H.parity, :, :], records[:, ds(H.times(HALF), HALF), :]).then_inc(rec_loaded[H.parity], 16)

                        def keep(H):
                            at = H.parity * HALF
                            for u in range(HALF):
                                sp.wait_ge(row_here[at + u], H.turns(row0))
                            sp.dma_start(gathered_rows[:, ds(H.times(HALF), HALF), :], gathered[:, at:at + HALF, :]).then_inc(s_spill[H.parity], 16)

                        load(Half(None, 0))
                        load(Half(None, 1))

                        def both(H):
                            keep(H)
                            load(H + 2)

                        halves(sp, 0, NH - 2, both)
                        keep(Half(None, NH - 2))
                        keep(Half(None, NH - 1))
                        for k in range(2):
                            sp.wait_ge(s_spill[k], NH // 2 * 16)

                    @block.gpsimd
                    def _(pool):
                        def gather(H, first=False):
                            pool.wait_ge(rec_loaded[H.parity], H.turns(rec0))
                            pool.wait_ge(s_split, H.times(1, 1))
                            if not first:
                                pool.wait_ge(s_spill[H.parity], H.turns(-1))
                            pool.sem_inc(half_started, 1)
                            for u in range(HALF):
                                pool.indirect_dma_start(
                                    gathered[:, H.parity * HALF + u, :], None, hrow,
                                    bass.IndirectOffsetOnAxis(ap=rec[:, H.parity, u, COL_INDEX:COL_INDEX + 1].bitcast(i32), axis=0),
                                ).then_inc(row_here[H.parity * HALF + u], 16)

                        gather(Half(None, 0), True)
                        gather(Half(None, 1), True)
                        halves(pool, 2, NH, gather)

                    @block.scalar
                    def _(act):
                        def prepare(H):
                            act.wait_ge(rec_loaded[H.parity], H.turns(rec0))
                            for u in range(HALF):
                                act.wait_ge(row_here[H.parity * HALF + u], H.turns(row0))
                            act.wait_ge(s_turn, H.times(QUADS, QUADS))
                            at = H.parity * HALF
                            act.copy(parts[:, H.parity, :, 0:LOC], gathered_b[:, at:at + HALF, 2 * ROW:2 * ROW_G])
                            act.copy(parts[:, H.parity, :, LOC:LOC + 4], rec_b[:, H.parity, :, 2 * COL_PACK:2 * REC]).then_inc(s_split, 1)

                        def copy_turned(H):
                            for q in range(QUADS):
                                act.wait_ge(s_turn, H.times(QUADS, q + 1 + 2 * QUADS))
                                act.wait_ge(s_prod, H.times(QUADS * UNITS, (q + 1) * UNITS))
                                act.copy(turned[:, H.parity * QUADS + q, :], psum_b[0:PARTS, 6 + q % 2, 0:GROUP_W]).then_inc(s_turnc, 1)

                        def body(H):
                            prepare(H + 1)
                            copy_turned(H + 1)

                        prepare(Half(None, 0))
                        copy_turned(Half(None, 0))
                        halves(act, 0, NH - 1, body)

                    @block.tensor
                    def _(pe):
                        def turn(H):
                            pe.wait_ge(s_split, H.times(1, 3))
                            for q in range(QUADS):
                                pe.wait_ge(s_turnc, H.times(QUADS, q + 1))
                                for j in range(4):
                                    last = pe.transpose(psum_b[0:PARTS, 6 + q % 2, j * P:(j + 1) * P], parts[:, H.parity, 4 * q + j, :], ident_b[:])
                                last.then_inc(s_turn, 1)

                        def products(H, q):
                            pe.wait_ge(s_turnc, H.times(QUADS, q + 3))
                            rows_q = turned[:, H.parity * QUADS + q, :]
                            for u, (lo, hi) in enumerate(ROUNDS):
                                pe.wait_ge(s_red, H.times(QUADS * UNITS, q * UNITS + u + 1))
                                b = 3 * ((q + u) % 2)
                                for c in range(hi - lo):
                                    pe.matmul(psum[:, b + c, :], apart[:], rows_q, start=True, stop=False)
                                    last = pe.matmul(psum[:, b + c, :], select[:, lo + c, :], rows_q, start=False, stop=True)
                                last.then_inc(s_prod, 1)

                        turn(Half(None, 0))

                        def body(H):
                            products(H, 0)
                            products(H, 1)
                            turn(H + 1)
                            products(H, 2)
                            products(H, 3)

                        halves(pe, 0, NH - 1, body)
                        for q in range(QUADS):
                            products(Half(None, NH - 1), q)

                    @block.vector
                    def _(v):
                        regs = [[v.alloc_register(f"x{k}_{u}") for u in range(HALF)] for k in range(2)]

                        def load_nodes(H):
                            v.load(regs[H.parity], tile_of_d[0:1, ds(H.times(HALF), HALF)])

                        def take(H, q, t):
                            v.wait_ge(s_max, H.times(HALF, 4 * q + t + 1))
                            node = v.snap(regs[H.parity][4 * q + t], min_val=0, max_val=TILES - 1)
                            to = dst_max[:, ds(node, 1), HEADS:].rearrange("p a w -> p (a w)")
                            v.tensor_tensor(to, big[:, H.parity, q, :, t], to, ALU.max).then_inc(s_max, 1)

                        def reduce(H, quad_before, more=True):
                            for q in range(QUADS):
                                for u, (lo, hi) in enumerate(ROUNDS):
                                    v.wait_ge(s_prod, H.times(QUADS * UNITS, q * UNITS + u + 1 + 2 * QUADS * UNITS))
                                    b = 3 * ((q + u) % 2)
                                    v.tensor_reduce(big[:, H.parity, q, lo:hi, :], psum[:, b:b + hi - lo, :].rearrange("p a (t e) -> p a t e", t=4),
                                                    AX.X, ALU.max).then_inc(s_red, 1)
                                    if u and (q or quad_before):
                                        v.wait_ge(s_red, H.times(QUADS * UNITS, q * UNITS + 2))
                                        for t in (2 * u - 2, 2 * u - 1):
                                            if q:
                                                take(H, q - 1, t)
                                            else:
                                                take(H + -1, QUADS - 1, t)
                                if q == 2 and more:
                                    load_nodes(H + 1)

                        v.sem_inc(s_max, 1)
                        load_nodes(Half(None, 0))
                        reduce(Half(None, 0), False)
                        halves(v, 1, NH - 1, lambda H: reduce(H, True))
                        reduce(Half(None, NH - 1), True, False)
                        v.wait_ge(s_red, NH * QUADS * UNITS + 2)
                        for tt in range(4):
                            take(Half(None, NH - 1), QUADS - 1, tt)
                        for r in regs[0] + regs[1]:
                            v.free_register(r)
                        v.wait_ge(s_max, NT + 1)
                        c = [PREP]

                        def link(ins):
                            c[0] += 1
                            ins.then_inc(s_steps, 1)
                            v.wait_ge(s_steps, c[0])

                        m = dst_max[:, :, HEADS:]
                        link(v.tensor_add(m, m, dst_max[:, :, 0:HEADS]))
                        link(v.scalar_tensor_tensor(m, m, SLOPE, m, ALU.mult, ALU.max))
            turns_rec[0] += NH // 2
            turns_row[0] += NH // 2

        def attention_phase():
            QUADS = HALF // 4
            s_one, s_turn, s_turnc, s_dst, s_ad, s_e, s_exp, s_msg, s_sum, s_add, s_steps = (sem(f"a_{n}") for n in (
                "onehots", "turned", "turned_copied", "dst_copied", "dst_rows", "scores", "exps", "messages", "summed", "added", "steps"))
            s_rows = [sem(f"a_rows_loaded{k}") for k in range(2)]
            s_scat = [sem(f"a_scattered{k}") for k in range(2)]
            s_taken = sem("a_taken")
            rec0 = turns_rec[0]
            with ExitStack() as scope:
                turned = sb("a_turned", [P, QUADS, 4, P], f32, scope)
                score = sb("a_score", [P, 2, HALF, HEADS], f32, scope)
                dst_here = sb("a_dst_here", [P, 2, HALF, 2 * HEADS], f32, scope)
                msg = sb("a_msg", [P, BODY, ROW], f32, scope)
                to_rec = sb("a_to_rec", [P, 2, CS, REC_S], f32, scope)
                to_addr = sb("a_to_addr", [P, 2, CS], i32, scope)
                spare_a = sb("a_spare", [1, 2, F], f32, scope)
                with nc.Block() as block:

                    @block.sync
                    def _(sp):
                        records = rec_d.rearrange("(p t) w -> p t w", t=NT)

                        def load(H):
                            at = H.parity * HALF
                            sp.wait_ge(s_msg, H.times(QUADS, QUADS))
                            sp.dma_start(rec[:, H.parity, :, :], records[:, ds(H.times(HALF), HALF), :]).then_inc(rec_loaded[H.parity], 16)
                            sp.dma_start(gathered[:, at:at + HALF, :], gathered_rows[:, ds(H.times(HALF), HALF), :]).then_inc(s_rows[H.parity], 16)

                        halves(sp, 0, NH, load)

                    @block.gpsimd
                    def _(pool):
                        for h in range(2):
                            pool.dma_start(spare_a[0:1, h, :], t["x"][0:1, :]).then_inc(s_scat[h], 16)

                        def scatter(h, rows, c, col, before, n_taken):
                            pool.wait_ge(s_scat[h], before)
                            pool.tensor_copy(to_addr[0:rows, h, 0:c], addr_src[0:rows, ds(col, c)]).then_inc(s_taken, 1)
                            pool.tensor_copy(to_rec[0:rows, h, 0:c, :], rec_src[0:rows, ds(col, c), :]).then_inc(s_taken, 1)
                            pool.wait_ge(s_taken, n_taken)
                            pool.sem_inc(half_started, 1)
                            for j in range(c):
                                pool.indirect_dma_start(
                                    rec_s, bass.IndirectOffsetOnAxis(ap=to_addr[0:rows, h, j:j + 1], axis=0),
                                    to_rec[0:rows, h, j, :], None).then_inc(s_scat[h], 16)

                        with pool.Fori(0, SORT_ITERS) as i:
                            for h in range(2):
                                scatter(h, P, CS, i * (2 * CS) + h * CS, i * (CS * 16) + 16, i * 4 + (2 * h + 2))
                        if TAIL:
                            scatter(0, TAIL, 1, COLS, SORT_ITERS * CS * 16 + 16, SORT_ITERS * 4 + 2)
                        pool.wait_ge(s_scat[0], SORT_ITERS * CS * 16 + 16 + (16 if TAIL else 0))
                        pool.wait_ge(s_scat[1], SORT_ITERS * CS * 16 + 16)

                    @block.scalar
                    def _(act):
                        def copy_turned(H):
                            for q in range(QUADS):
                                act.wait_ge(s_turn, H.times(QUADS, q + 1))
                                act.wait_ge(s_ad, H.times(QUADS, q + 1 + QUADS))
                                act.copy(turned[:, q, :, :].rearrange("p a b -> p (a b)"), psum[:, 4 + q % 2, :]).then_inc(s_turnc, 1)

                        regs = [act.alloc_register(f"act{u}") for u in range(HALF)]

                        def copy_dst(H):
                            nodes = tile_numbers(act, regs, tile_of_d, H.times(HALF))
                            act.wait_ge(s_ad, H.times(QUADS, 1))
                            for u in range(HALF):
                                last = act.copy(dst_here[:, H.parity, u, :], dst_max[:, ds(nodes[u], 1), :].rearrange("p a w -> p (a w)"))
                            last.then_inc(s_dst, 1)

                        def exps(H):
                            at = H.parity * HALF
                            act.wait_ge(s_e, H.times(1, 3))
                            act.wait_ge(s_sum, H.times(HALF, HALF))
                            act.activation(msg[:, at:at + HALF, F:ROW], score[:, H.parity, :, :], ACT.Exp).then_inc(s_exp, 1)

                        copy_dst(Half(None, 0))
                        copy_turned(Half(None, 0))

                        def body(H):
                            copy_dst(H + 1)
                            exps(H)
                            copy_turned(H + 1)

                        halves(act, 0, NH - 1, body)
                        exps(Half(None, NH - 1))
                        for r in regs:
                            act.free_register(r)

                    @block.tensor
                    def _(pe):
                        pe.sem_inc(s_turnc, 2)
                        pe.sem_inc(s_ad, 2 * QUADS)
                        pe.sem_inc(s_sum, BODY)
                        def turn(H):
                            for q in range(QUADS):
                                pe.wait_ge(s_one, H.times(QUADS, q + 1))
                                pe.wait_ge(s_turnc, H.times(QUADS, q + 1))
                                for j in range(4):
                                    last = pe.transpose(psum[:, 4 + q % 2, j * P:(j + 1) * P], onehot[:, H.parity * HALF + 4 * q + j, :], ident[:])
                                last.then_inc(s_turn, 1)

                        def dst_rows(H):
                            pe.wait_ge(s_e, H.times(1, 1))
                            pe.wait_ge(s_dst, H.times(1, 1))
                            for q in range(QUADS):
                                pe.wait_ge(s_turnc, H.times(QUADS, q + 3))
                                for j in range(4):
                                    u = 4 * q + j
                                    last = pe.matmul(psum[:, 6 + H.parity, u * 16:(u + 1) * 16], turned[:, q, j, :],
                                                     dst_here[:, H.parity, u, :], start=True, stop=True)
                                last.then_inc(s_ad, 1)

                        def sum_tiles(H):
                            for u in range(HALF):
                                if u % 4 == 0:
                                    pe.wait_ge(s_msg, H.times(QUADS, u // 4 + 1 + 2 * QUADS))
                                pe.wait_ge(s_add, H.times(HALF, u + 1))
                                at = H.parity * HALF + u
                                pe.matmul(psum[:, u % SUM_BANKS, 0:ROW], onehot[:, at, :], msg[:, at, :],
                                          start=True, stop=True).then_inc(s_sum, 1)

                        for n in range(2):
                            turn(Half(None, n))
                            dst_rows(Half(None, n))

                        def body(H):
                            sum_tiles(H + -1)
                            turn(H + 1)
                            dst_rows(H + 1)

                        halves(pe, 1, NH - 1, body)
                        sum_tiles(Half(None, NH - 2))
                        sum_tiles(Half(None, NH - 1))

                    @block.vector
                    def _(v):
                        v.sem_inc(s_e, 2)
                        v.sem_inc(s_msg, 2 * QUADS)
                        v.sem_inc(s_add, SUM_BANKS)
                        regs = [v.alloc_register(f"a{u}") for u in range(HALF)]

                        def onehots(H):
                            v.wait_ge(rec_loaded[H.parity], H.turns(rec0))
                            v.wait_ge(s_sum, H.times(HALF, HALF))
                            for u in range(HALF):
                                last = v.tensor_scalar(onehot[:, H.parity * HALF + u, :], iota_row[:], rec[:, H.parity, u, COL_LOCAL:COL_LOCAL + 1],
                                                       None, ALU.is_equal)
                                if u % 4 == 3:
                                    last.then_inc(s_one, 1)

                        def scores(H):
                            at = H.parity * HALF
                            sc = score[:, H.parity, :, :]
                            ad = psum[:, 6 + H.parity, 0:16 * HALF].rearrange("p (a w) -> p a w", a=HALF)
                            n = [0]

                            def link(ins):
                                n[0] += 1
                                ins.then_inc(s_steps, 1)
                                v.wait_ge(s_steps, H.times(3, n[0]))

                            v.wait_ge(s_rows[H.parity], H.turns())
                            v.wait_ge(s_ad, H.times(QUADS, 3 * QUADS))
                            link(v.tensor_tensor(sc, ad[:, :, 0:HEADS], gathered[:, at:at + HALF, F:ROW], ALU.add))
                            link(v.scalar_tensor_tensor(sc, sc, SLOPE, sc, ALU.mult, ALU.max))
                            link(v.tensor_tensor(sc, sc, ad[:, :, HEADS:], ALU.subtract))
                            v.tensor_single_scalar(sc, sc, 0.0, ALU.min).then_inc(s_e, 1)

                        def messages(H):
                            v.wait_ge(s_exp, H.times(1, 1))
                            for q in range(QUADS):
                                at = H.parity * HALF + 4 * q
                                v.tensor_tensor(
                                    msg[:, at:at + 4, 0:F].rearrange("p t (h c) -> p t h c", h=HEADS),
                                    gathered[:, at:at + 4, 0:F].rearrange("p t (h c) -> p t h c", h=HEADS),
                                    msg[:, at:at + 4, F:ROW].unsqueeze(3).to_broadcast([P, 4, HEADS, HEAD_CH]), ALU.mult).then_inc(s_msg, 1)

                        def add(H):
                            nodes = tile_numbers(v, regs, tile_of_d, H.times(HALF))
                            for u in range(HALF):
                                v.wait_ge(s_sum, H.times(HALF, u + 1 + BODY))
                                v.wait_ge(s_add, H.times(HALF, u + SUM_BANKS))
                                to = sums[:, ds(nodes[u], 1), FEAT:].rearrange("p a w -> p (a w)")
                                v.tensor_tensor(to, psum[:, u % SUM_BANKS, 0:ROW], to, ALU.add).then_inc(s_add, 1)

                        onehots(Half(None, 0))
                        scores(Half(None, 0))
                        onehots(Half(None, 1))
                        messages(Half(None, 0))

                        def body(H):
                            add(H + -1)
                            scores(H)
                            onehots(H + 1)
                            messages(H)

                        halves(v, 1, NH - 1, body)
                        add(Half(None, NH - 2))
                        scores(Half(None, NH - 1))
                        messages(Half(None, NH - 1))
                        add(Half(None, NH - 1))
                        for r in regs:
                            v.free_register(r)
            turns_rec[0] += NH // 2

        def attention_finish(x_old, x_new):
            s_x, s_rows, s_chain, s_score, s_self, s_var, s_root, s_min, s_exp, s_new, s_st = (sem(f"g_{n}") for n in (
                "x_loaded", "rows_loaded", "steps", "scores", "self_exps", "variances", "roots", "minima", "exps", "normed", "stored"))
            with ExitStack() as scope:
                xo = sb("g_x", [P, GROUP, F], f32, scope)
                zz = sb("g_z", [P, GROUP, F], f32, scope)
                ee = sb("g_e", [P, GROUP, F], f32, scope)
                xn = sb("g_new", [P, GROUP, F], f32, scope)
                hr = sb("g_rows", [P, GROUP, ROW_G], f32, scope)
                score = sb("g_score", [P, GROUP, HEADS], f32, scope)
                den = sb("g_den", [P, GROUP, HEADS], f32, scope)
                stats = sb("g_stats", [P, GROUP, 6], f32, scope)
                mv = sb("g_mv", [P, GROUP, 4], f32, scope)
                STEPS = 18
                with nc.Block() as block:

                    @block.sync
                    def _(sp):
                        view = x_old.rearrange("(t p) f -> p t f", p=P)
                        rows_view = hrow.rearrange("(t p) f -> p t f", p=P)
                        sp.sem_inc(s_chain, 3)
                        sp.sem_inc(s_new, 1)
                        with sp.Fori(0, GROUPS) as g:
                            sp.wait_ge(s_chain, g * STEPS + 1)
                            sp.dma_start(xo[:], view[:, ds(g * GROUP, GROUP), :]).then_inc(s_x, 16)
                            sp.dma_start(hr[:], rows_view[:, ds(g * GROUP, GROUP), :]).then_inc(s_rows, 16)

                    @block.scalar
                    def _(act):
                        prime(act, s_st, 1)
                        with act.Fori(0, GROUPS) as g:
                            act.wait_ge(s_score, g + 1)
                            act.activation(score[:], score[:], ACT.Exp).then_inc(s_self, 1)
                            for r in range(2):
                                act.wait_ge(s_var, g * 2 + (r + 1))
                                act.activation(mv[:, :, 2:3], mv[:, :, 1:2], ACT.Sqrt, bias=eps[:]).then_inc(s_root, 1)
                                if r == 0:
                                    act.wait_ge(s_min, g + 1)
                                    act.activation(ee[:], ee[:], ACT.Exp).then_inc(s_exp, 1)
                            act.wait_ge(s_new, g + 2)
                            store_group(act, x_new, g, xn[:], s_st)
                        act.wait_ge(s_st, 16 * (GROUPS + 1))

                    @block.vector
                    def _(v):
                        wide = lambda a: a.unsqueeze(1).to_broadcast([P, GROUP, F])
                        with v.Fori(0, GROUPS) as g:
                            n = [0]

                            def link(ins):
                                n[0] += 1
                                ins.then_inc(s_chain, 1)
                                v.wait_ge(s_chain, g * STEPS + (n[0] + 3))

                            here = lambda m: m[:, ds(g * GROUP, GROUP), :]
                            v.wait_ge(s_rows, g * 16 + 16)
                            v.wait_ge(s_new, g + 1)
                            link(v.tensor_tensor(score[:], hr[:, :, F:ROW], here(dst_max)[:, :, 0:HEADS], ALU.add))
                            link(v.scalar_tensor_tensor(score[:], score[:], SLOPE, score[:], ALU.mult, ALU.max))
                            v.tensor_tensor(score[:], score[:], here(dst_max)[:, :, HEADS:], ALU.subtract).then_inc(s_score, 1)
                            v.wait_ge(s_self, g + 1)
                            link(v.tensor_tensor(den[:], here(sums)[:, :, DEN:], score[:], ALU.add))
                            link(v.reciprocal(den[:], den[:]))
                            blocks = lambda m, j: m[:, j, 0:F].rearrange("p (h c) -> p h c", h=HEADS)
                            each = lambda m, j: m[:, j, :].unsqueeze(2).to_broadcast([P, HEADS, HEAD_CH])
                            for j in range(GROUP):
                                last = v.tensor_tensor(blocks(zz, j), blocks(hr, j), each(score, j), ALU.mult)
                            link(last)
                            link(v.tensor_tensor(zz[:], zz[:], here(sums)[:, :, FEAT:FEAT + F], ALU.add))
                            for j in range(GROUP):
                                last = v.tensor_tensor(blocks(zz, j), blocks(zz, j), each(den, j), ALU.mult)
                            link(last)
                            link(v.tensor_tensor(zz[:], zz[:], wide(bias_1), ALU.add))
                            link(norm_rows(v, link, zz, zz, stats, mv, s_var, s_root, g * 2 + 1))
                            link(v.tensor_tensor(zz[:], zz[:], wide(gamma_1), ALU.mult))
                            link(v.tensor_tensor(zz[:], zz[:], wide(beta_1), ALU.add))
                            v.tensor_single_scalar(ee[:], zz[:], 0.0, ALU.min).then_inc(s_min, 1)
                            v.wait_ge(s_min, g + 1)
                            link(v.tensor_single_scalar(zz[:], zz[:], 0.0, ALU.max))
                            v.wait_ge(s_exp, g + 1)
                            link(v.scalar_tensor_tensor(zz[:], ee[:], -1.0, zz[:], ALU.add, ALU.add))
                            v.wait_ge(s_x, g * 16 + 16)
                            link(v.tensor_tensor(zz[:], zz[:], xo[:], ALU.add))
                            norm_rows(v, link, zz, xn, stats, mv, s_var, s_root, g * 2 + 2, s_st, g * 16 + 16).then_inc(s_new, 1)
                            assert n[0] == STEPS, n

        attrs = (COL_ATTR, COL_PACK)
        sum_layer(rec_d, REC, rec, tile_of_d, xs[0], attrs)
        mlp_phase(we_0, w1_0, b1_0, w2_0, b2_0, 2)
        bn_phase()
        finish_phase(0, bn_scale, bn_shift, xs[0], xs[1])
        project_phase(xs[1])
        max_phase()
        attention_phase()
        attention_finish(xs[1], xs[2])
        clear_sums(FEAT, DEN)
        sum_layer(rec_d, REC, rec, tile_of_d, xs[2], None)
        mlp_phase(we_2, w1_2, b1_2, w2_2, b2_2, 1)
        finish_phase(1, one_col, zero_col, xs[2], xs[3])
        clear_sums(0, DEN)
        sum_layer(rec_s, REC_S, recs, tile_of_s, xs[3], (2, 3))
        mlp_phase(None, None, None, w_3t, None, 0, extra_out=b_3, scale=agg_w)
        finish_phase(2, one_col, zero_col, xs[3], out, last_layer=True)


_INS = ["x", "src", "dst", "edge_attr_16", "edge_attr_3", "edge_attr_6",
        "L0_gnn_We0", "L0_gnn_be0", "L0_gnn_We1", "L0_gnn_be1", "L0_gnn_W1", "L0_gnn_b1", "L0_gnn_W2", "L0_gnn_b2",
        "L0_gnn_gamma", "L0_gnn_beta", "L1_gnn_W", "L1_gnn_att_src", "L1_gnn_att_dst", "L1_gnn_bias",
        "L1_gnn_ln_gamma", "L1_gnn_ln_beta", "L2_gnn_We", "L2_gnn_be", "L2_gnn_W1", "L2_gnn_b1", "L2_gnn_W2",
        "L2_gnn_b2", "L3_gnn_W", "L3_gnn_b", "L3_gnn_agg_weight"]


def kernel(**inputs):
    import numpy as _np
    import concourse.bacc as _bacc
    from concourse import mybir as _mybir
    from concourse.bass_utils import run_bass_kernel_spmd as _run

    nc = _bacc.Bacc("TRN2", target_bir_lowering=False, num_devices=1)
    arrays, t = {}, {}
    for name in _INS:
        a = _np.ascontiguousarray(inputs[name])
        arrays[f"in_{name}"] = a
        t[name] = nc.dram_tensor(f"in_{name}", a.shape, _mybir.dt.from_np(a.dtype), kind="ExternalInput").ap()
    n, f = inputs["x"].shape
    out = nc.dram_tensor("out_0", (n, f), _mybir.dt.float32, kind="ExternalOutput").ap()
    gnn_kernel(nc, t, out)
    r = _run(nc, [arrays], core_ids=[0])
    return r.results[0]["out_0"]
```
